# Optimizing a Trainium2 kernel written in Bass

```python
import numpy as np
import jax
import jax.numpy as jnp

def _softmax(x, axis=-1):
    return jax.nn.softmax(x, axis=axis)

def _gelu(x):
    return jax.nn.gelu(x, approximate=True)

def _silu(x):
    return jax.nn.silu(x)

def _sigmoid(x):
    return jax.nn.sigmoid(x)

def _layernorm(x, axis=-1, eps=1e-05):
    m = jnp.mean(x, axis=axis, keepdims=True)
    v = jnp.var(x, axis=axis, keepdims=True)
    return (x - m) / jnp.sqrt(v + eps)

def _scatter_add(tgt, idx, src, axis=0):
    return tgt.at[idx].add(src)

def _segment_sum(src, seg, n):
    return jax.ops.segment_sum(src, seg, n)
kernel_name = 'mk_seq_postln_d2_jaxref_r4_a22ba0'

def setup_inputs(seed: int=0):
    np.random.seed(seed)
    _w = jnp.asarray

    def _L0_attn_setup():
        import jax, jax.numpy as jnp
        import numpy as np
        B, T, D, C = (16, 1024, 256, 128)
        key = jax.random.key(seed)
        ks = jax.random.split(key, 15)

        def w(k, out_dim, in_dim):
            return jax.random.normal(k, (out_dim, in_dim), jnp.float32) / np.sqrt(in_dim).astype(np.float32)
        return {'x': jax.random.normal(ks[0], (B, T, D), jnp.float32), 'Wq': w(ks[1], C, D), 'bq': jnp.zeros((C,), jnp.float32), 'Wk': w(ks[2], C, D), 'bk': jnp.zeros((C,), jnp.float32), 'Wv': w(ks[3], C, D), 'bv': jnp.zeros((C,), jnp.float32), 'Wa': w(ks[4], 1, D), 'ba': jnp.zeros((1,), jnp.float32), 'Wb': w(ks[5], 1, D), 'bb': jnp.zeros((1,), jnp.float32), 'Wg': w(ks[6], C, D), 'bg': jnp.zeros((C,), jnp.float32), 'Wo': w(ks[7], D, C), 'bo': jnp.zeros((D,), jnp.float32)}
    _L0_attn_in = _L0_attn_setup()

    def _L0_ffn_setup():
        import jax, jax.numpy as jnp
        import numpy as np
        DIM = 256
        DEPTH = 2
        HEADS = 8
        DIM_HEAD = 64
        WINDOW = 128
        INNER = HEADS * DIM_HEAD
        HID = int(DIM * 4 * 2 / 3)
        B, N = (2, 2048)
        QK_SCALE = 8.0

        def shift_token(t):
            t1, t2 = jnp.split(t, 2, axis=-1)
            t2 = jnp.pad(t2, ((0, 0), (1, 0), (0, 0)))[:, :-1]
            return jnp.concatenate([t1, t2], axis=-1)

        def l2norm(t):
            return t / jnp.clip(jnp.linalg.norm(t, axis=-1, keepdims=True), 1e-12)

        def rotate_half(x):
            x1, x2 = jnp.split(x, 2, axis=-1)
            return jnp.concatenate([-x2, x1], axis=-1)

        def rotary_xpos(q, k):
            n = q.shape[-2]
            half_idx = jnp.arange(0, DIM_HEAD, 2, dtype=jnp.float32)
            inv_freq = 1.0 / 10000.0 ** (half_idx / DIM_HEAD)
            t = jnp.arange(n, dtype=jnp.float32)
            freqs = t[:, None] * inv_freq[None, :]
            freqs = jnp.concatenate([freqs, freqs], axis=-1)
            base = (half_idx + 0.4 * DIM_HEAD) / (1.4 * DIM_HEAD)
            power = (t - n // 2) / float(WINDOW // 2)
            scale = base[None, :] ** power[:, None]
            scale = jnp.concatenate([scale, scale], axis=-1)
            cos, sin = (jnp.cos(freqs), jnp.sin(freqs))
            q = q * cos * scale + rotate_half(q) * sin * scale
            k = k * cos / scale + rotate_half(k) * sin / scale
            return (q, k)

        def local_attention(q, k, v):
            b, h, n, d = q.shape
            w = n // WINDOW
            bq = q.reshape(b, h, w, WINDOW, d) * QK_SCALE
            bk = k.reshape(b, h, w, WINDOW, d)
            bv = v.reshape(b, h, w, WINDOW, d)

            def look_around(t):
                p = jnp.pad(t, ((0, 0), (0, 0), (1, 0), (0, 0), (0, 0)))
                return jnp.concatenate([p[:, :, :w], p[:, :, 1:]], axis=3)
            bk, bv = (look_around(bk), look_around(bv))
            bt = jnp.arange(n).reshape(w, WINDOW)
            btp = jnp.pad(bt, ((1, 0), (0, 0)), constant_values=-1)
            btk = jnp.concatenate([btp[:w], btp[1:]], axis=1)
            sim = jnp.einsum('bhwid,bhwjd->bhwij', bq, bk)
            i = bt[:, :, None]
            j = btk[:, None, :]
            mask = (i < j) | (i > j + WINDOW) | (j == -1)
            sim = jnp.where(mask, -jnp.finfo(sim.dtype).max, sim)
            attn = jax.nn.softmax(sim, axis=-1)
            out = jnp.einsum('bhwij,bhwjd->bhwid', attn, bv)
            return out.reshape(b, h, n, d)

        def _layer(x, wqkv, qs, ksc, wo, lg, lb, w1, b1, w2, b2):
            b, n, _ = x.shape
            h = shift_token(x)
            qkv = h @ wqkv
            q, k, v = jnp.split(qkv, 3, axis=-1)
            to_heads = lambda t: t.reshape(b, n, HEADS, DIM_HEAD).transpose(0, 2, 1, 3)
            q, k, v = (to_heads(q), to_heads(k), to_heads(v))
            q = l2norm(q) * qs
            k = l2norm(k) * ksc
            q, k = rotary_xpos(q, k)
            o = local_attention(q, k, v)
            o = o.transpose(0, 2, 1, 3).reshape(b, n, INNER)
            x = x + o @ wo
            h = shift_token(x)
            mu = h.mean(-1, keepdims=True)
            var = h.var(-1, keepdims=True)
            h = (h - mu) / jnp.sqrt(var + 1e-05) * lg + lb
            h = h @ w1 + b1
            a, g = jnp.split(h, 2, axis=-1)
            h = a * jax.nn.gelu(g, approximate=False)
            x = x + h @ w2 + b2
            return x
        key = jax.random.key(seed)
        ks = jax.random.split(key, 6)
        return {'x': jax.random.normal(ks[0], (B, N, DIM), jnp.float32), 'wqkv': jax.random.normal(ks[1], (DEPTH, DIM, 3 * INNER), jnp.float32) * 0.02, 'q_scale': jnp.ones((DEPTH, DIM_HEAD), jnp.float32), 'k_scale': jnp.ones((DEPTH, DIM_HEAD), jnp.float32), 'wo': jax.random.normal(ks[2], (DEPTH, INNER, DIM), jnp.float32) * 0.02, 'ln_g': jnp.ones((DEPTH, DIM), jnp.float32), 'ln_b': jnp.zeros((DEPTH, DIM), jnp.float32), 'w1': jax.random.normal(ks[3], (DEPTH, DIM, 2 * HID), jnp.float32) * 0.02, 'b1': jnp.zeros((DEPTH, 2 * HID), jnp.float32), 'w2': jax.random.normal(ks[4], (DEPTH, HID, DIM), jnp.float32) * 0.02, 'b2': jnp.zeros((DEPTH, DIM), jnp.float32)}
    _L0_ffn_in = _L0_ffn_setup()

    def _L1_attn_setup():
        import jax, jax.numpy as jnp
        import numpy as np

        def _sin_rpe(Lq, d_model, dtype):
            inv_freq = 1.0 / 10000.0 ** (jnp.arange(0, d_model, 2, dtype=jnp.float32) / d_model)
            pos = jnp.arange(-(Lq - 1), Lq, dtype=jnp.float32)
            ang = pos[:, None] * inv_freq[None, :]
            emb = jnp.zeros((2 * Lq - 1, d_model), dtype=jnp.float32)
            emb = emb.at[:, 0::2].set(jnp.sin(ang)).at[:, 1::2].set(jnp.cos(ang))
            return emb.astype(dtype)

        def _rel_shift(x):
            B, H, Lq, Lr = x.shape
            xp = jnp.concatenate([jnp.zeros((B, H, Lq, 1), x.dtype), x], axis=-1)
            xp = xp.reshape(B, H, Lr + 1, Lq)
            return xp[:, :, 1:].reshape(B, H, Lq, Lr)[..., Lr - Lq:]
        key = jax.random.key(seed)
        ks = jax.random.split(key, 7)
        B, Lq, D, H = (1, 512, 256, 16)
        d_head = D // H
        s = 0.02
        return {'w': jax.random.normal(ks[0], (B, Lq, D), jnp.float32), 'Wq': jax.random.normal(ks[1], (D, D), jnp.float32) * s, 'Wk': jax.random.normal(ks[2], (D, D), jnp.float32) * s, 'Wv': jax.random.normal(ks[3], (D, D), jnp.float32) * s, 'Wr': jax.random.normal(ks[4], (D, D), jnp.float32) * s, 'u_bias': jax.random.normal(ks[5], (H, d_head), jnp.float32) * 0.02, 'v_bias': jax.random.normal(ks[6], (H, d_head), jnp.float32) * 0.02}
    _L1_attn_in = _L1_attn_setup()

    def _L1_ffn_setup():
        import jax, jax.numpy as jnp
        import numpy as np
        SL, BS, HS, FF, E, TOPK = (512, 2, 256, 1024, 8, 2)
        key = jax.random.key(seed)
        ks = jax.random.split(key, 6)
        T = SL * BS
        x = jax.random.normal(ks[0], (SL, BS, HS), jnp.float32)
        scores = jax.random.uniform(ks[1], (T, E), jnp.float32)
        expert_weights = jax.random.uniform(ks[2], (T, TOPK), jnp.float32)
        expert_indices = jax.random.randint(ks[3], (T, TOPK), 0, E, jnp.int32)
        w1 = jax.random.normal(ks[4], (E, HS, FF), jnp.float32) * (1.0 / np.sqrt(HS))
        w2 = jax.random.normal(ks[5], (E, FF, HS), jnp.float32) * (1.0 / np.sqrt(FF))
        bias = jnp.zeros((HS,), jnp.float32)
        return dict(x=x, scores=scores, expert_weights=expert_weights, expert_indices=expert_indices, w1=w1, w2=w2, bias=bias)
    _L1_ffn_in = _L1_ffn_setup()
    _d = {'L0_attn_x': _L0_attn_in['x'], 'L0_attn_Wq': _L0_attn_in['Wq'], 'L0_attn_bq': _L0_attn_in['bq'], 'L0_attn_Wk': _L0_attn_in['Wk'], 'L0_attn_bk': _L0_attn_in['bk'], 'L0_attn_Wv': _L0_attn_in['Wv'], 'L0_attn_bv': _L0_attn_in['bv'], 'L0_attn_Wa': _L0_attn_in['Wa'], 'L0_attn_ba': _L0_attn_in['ba'], 'L0_attn_Wb': _L0_attn_in['Wb'], 'L0_attn_bb': _L0_attn_in['bb'], 'L0_attn_Wg': _L0_attn_in['Wg'], 'L0_attn_bg': _L0_attn_in['bg'], 'L0_attn_Wo': _L0_attn_in['Wo'], 'L0_attn_bo': _L0_attn_in['bo'], 'L0_ffn_wqkv': _L0_ffn_in['wqkv'], 'L0_ffn_q_scale': _L0_ffn_in['q_scale'], 'L0_ffn_k_scale': _L0_ffn_in['k_scale'], 'L0_ffn_wo': _L0_ffn_in['wo'], 'L0_ffn_ln_g': _L0_ffn_in['ln_g'], 'L0_ffn_ln_b': _L0_ffn_in['ln_b'], 'L0_ffn_w1': _L0_ffn_in['w1'], 'L0_ffn_b1': _L0_ffn_in['b1'], 'L0_ffn_w2': _L0_ffn_in['w2'], 'L0_ffn_b2': _L0_ffn_in['b2'], 'L1_attn_Wq': _L1_attn_in['Wq'], 'L1_attn_Wk': _L1_attn_in['Wk'], 'L1_attn_Wv': _L1_attn_in['Wv'], 'L1_attn_Wr': _L1_attn_in['Wr'], 'L1_attn_u_bias': _L1_attn_in['u_bias'], 'L1_attn_v_bias': _L1_attn_in['v_bias'], 'L1_ffn_scores': _L1_ffn_in['scores'], 'L1_ffn_expert_weights': _L1_ffn_in['expert_weights'], 'L1_ffn_expert_indices': _L1_ffn_in['expert_indices'], 'L1_ffn_w1': _L1_ffn_in['w1'], 'L1_ffn_w2': _L1_ffn_in['w2'], 'L1_ffn_bias': _L1_ffn_in['bias']}
    _x0 = _d['L0_attn_x']
    _d['L0_attn_x'] = jax.random.normal(jax.random.fold_in(jax.random.key(seed), 1), (2, 2048, 256), dtype=_x0.dtype)
    del _x0
    return _d

def reference(L0_attn_x, L0_attn_Wq, L0_attn_bq, L0_attn_Wk, L0_attn_bk, L0_attn_Wv, L0_attn_bv, L0_attn_Wa, L0_attn_ba, L0_attn_Wb, L0_attn_bb, L0_attn_Wg, L0_attn_bg, L0_attn_Wo, L0_attn_bo, L0_ffn_wqkv, L0_ffn_q_scale, L0_ffn_k_scale, L0_ffn_wo, L0_ffn_ln_g, L0_ffn_ln_b, L0_ffn_w1, L0_ffn_b1, L0_ffn_w2, L0_ffn_b2, L1_attn_Wq, L1_attn_Wk, L1_attn_Wv, L1_attn_Wr, L1_attn_u_bias, L1_attn_v_bias, L1_ffn_scores, L1_ffn_expert_weights, L1_ffn_expert_indices, L1_ffn_w1, L1_ffn_w2, L1_ffn_bias):

    def _L0_attn_ref(x, Wq, bq, Wk, bk, Wv, bv, Wa, ba, Wb, bb, Wg, bg, Wo, bo):
        import jax, jax.numpy as jnp
        import numpy as np
        B, T, D, C = (16, 1024, 256, 128)
        q = x @ Wq.T + bq
        k = x @ Wk.T + bk
        k = k / jnp.maximum(jnp.linalg.norm(k, axis=-1, keepdims=True), 1e-12)
        v = x @ Wv.T + bv
        alpha = jax.nn.sigmoid(x @ Wa.T + ba)
        beta = jax.nn.sigmoid(x @ Wb.T + bb)
        gate = jax.nn.sigmoid(x @ Wg.T + bg)
        Bb, Tt, Dd = x.shape
        Cc = q.shape[-1]

        def step(S, inp):
            q_t, k_t, v_t, a_t, b_t = inp
            a = a_t[:, :, None]
            b = b_t[:, :, None]
            Sk = jnp.einsum('bij,bj->bi', S, k_t)
            S = a * (S - b * (Sk[:, :, None] * k_t[:, None, :])) + b * (v_t[:, :, None] * k_t[:, None, :])
            o = jnp.einsum('bi,bij->bj', q_t, S)
            return (S, o)
        xs = (q.swapaxes(0, 1), k.swapaxes(0, 1), v.swapaxes(0, 1), alpha.swapaxes(0, 1), beta.swapaxes(0, 1))
        S0 = jnp.zeros((Bb, Cc, Cc), x.dtype)
        _, o = jax.lax.scan(step, S0, xs)
        o = o.swapaxes(0, 1) * gate
        return o @ Wo.T + bo

    def _L0_ffn_ref(x, wqkv, q_scale, k_scale, wo, ln_g, ln_b, w1, b1, w2, b2):
        import jax, jax.numpy as jnp
        import numpy as np
        DIM = 256
        DEPTH = 2
        HEADS = 8
        DIM_HEAD = 64
        WINDOW = 128
        INNER = HEADS * DIM_HEAD
        HID = int(DIM * 4 * 2 / 3)
        B, N = (2, 2048)
        QK_SCALE = 8.0

        def shift_token(t):
            t1, t2 = jnp.split(t, 2, axis=-1)
            t2 = jnp.pad(t2, ((0, 0), (1, 0), (0, 0)))[:, :-1]
            return jnp.concatenate([t1, t2], axis=-1)

        def l2norm(t):
            return t / jnp.clip(jnp.linalg.norm(t, axis=-1, keepdims=True), 1e-12)

        def rotate_half(x):
            x1, x2 = jnp.split(x, 2, axis=-1)
            return jnp.concatenate([-x2, x1], axis=-1)

        def rotary_xpos(q, k):
            n = q.shape[-2]
            half_idx = jnp.arange(0, DIM_HEAD, 2, dtype=jnp.float32)
            inv_freq = 1.0 / 10000.0 ** (half_idx / DIM_HEAD)
            t = jnp.arange(n, dtype=jnp.float32)
            freqs = t[:, None] * inv_freq[None, :]
            freqs = jnp.concatenate([freqs, freqs], axis=-1)
            base = (half_idx + 0.4 * DIM_HEAD) / (1.4 * DIM_HEAD)
            power = (t - n // 2) / float(WINDOW // 2)
            scale = base[None, :] ** power[:, None]
            scale = jnp.concatenate([scale, scale], axis=-1)
            cos, sin = (jnp.cos(freqs), jnp.sin(freqs))
            q = q * cos * scale + rotate_half(q) * sin * scale
            k = k * cos / scale + rotate_half(k) * sin / scale
            return (q, k)

        def local_attention(q, k, v):
            b, h, n, d = q.shape
            w = n // WINDOW
            bq = q.reshape(b, h, w, WINDOW, d) * QK_SCALE
            bk = k.reshape(b, h, w, WINDOW, d)
            bv = v.reshape(b, h, w, WINDOW, d)

            def look_around(t):
                p = jnp.pad(t, ((0, 0), (0, 0), (1, 0), (0, 0), (0, 0)))
                return jnp.concatenate([p[:, :, :w], p[:, :, 1:]], axis=3)
            bk, bv = (look_around(bk), look_around(bv))
            bt = jnp.arange(n).reshape(w, WINDOW)
            btp = jnp.pad(bt, ((1, 0), (0, 0)), constant_values=-1)
            btk = jnp.concatenate([btp[:w], btp[1:]], axis=1)
            sim = jnp.einsum('bhwid,bhwjd->bhwij', bq, bk)
            i = bt[:, :, None]
            j = btk[:, None, :]
            mask = (i < j) | (i > j + WINDOW) | (j == -1)
            sim = jnp.where(mask, -jnp.finfo(sim.dtype).max, sim)
            attn = jax.nn.softmax(sim, axis=-1)
            out = jnp.einsum('bhwij,bhwjd->bhwid', attn, bv)
            return out.reshape(b, h, n, d)

        def _layer(x, wqkv, qs, ksc, wo, lg, lb, w1, b1, w2, b2):
            b, n, _ = x.shape
            h = shift_token(x)
            qkv = h @ wqkv
            q, k, v = jnp.split(qkv, 3, axis=-1)
            to_heads = lambda t: t.reshape(b, n, HEADS, DIM_HEAD).transpose(0, 2, 1, 3)
            q, k, v = (to_heads(q), to_heads(k), to_heads(v))
            q = l2norm(q) * qs
            k = l2norm(k) * ksc
            q, k = rotary_xpos(q, k)
            o = local_attention(q, k, v)
            o = o.transpose(0, 2, 1, 3).reshape(b, n, INNER)
            x = x + o @ wo
            h = shift_token(x)
            mu = h.mean(-1, keepdims=True)
            var = h.var(-1, keepdims=True)
            h = (h - mu) / jnp.sqrt(var + 1e-05) * lg + lb
            h = h @ w1 + b1
            a, g = jnp.split(h, 2, axis=-1)
            h = a * jax.nn.gelu(g, approximate=False)
            x = x + h @ w2 + b2
            return x
        for l in range(DEPTH):
            x = _layer(x, wqkv[l], q_scale[l], k_scale[l], wo[l], ln_g[l], ln_b[l], w1[l], b1[l], w2[l], b2[l])
        return x

    def _L1_attn_ref(w, Wq, Wk, Wv, Wr, u_bias, v_bias):
        import jax, jax.numpy as jnp
        import numpy as np

        def _sin_rpe(Lq, d_model, dtype):
            inv_freq = 1.0 / 10000.0 ** (jnp.arange(0, d_model, 2, dtype=jnp.float32) / d_model)
            pos = jnp.arange(-(Lq - 1), Lq, dtype=jnp.float32)
            ang = pos[:, None] * inv_freq[None, :]
            emb = jnp.zeros((2 * Lq - 1, d_model), dtype=jnp.float32)
            emb = emb.at[:, 0::2].set(jnp.sin(ang)).at[:, 1::2].set(jnp.cos(ang))
            return emb.astype(dtype)

        def _rel_shift(x):
            B, H, Lq, Lr = x.shape
            xp = jnp.concatenate([jnp.zeros((B, H, Lq, 1), x.dtype), x], axis=-1)
            xp = xp.reshape(B, H, Lr + 1, Lq)
            return xp[:, :, 1:].reshape(B, H, Lq, Lr)[..., Lr - Lq:]
        B, Lq, D = w.shape
        H, d_head = u_bias.shape
        scale = 1.0 / np.sqrt(d_head).astype(np.float32)
        r = _sin_rpe(Lq, D, w.dtype)
        q = (w @ Wq.T).reshape(B, Lq, H, d_head).transpose(0, 2, 1, 3)
        k = (w @ Wk.T).reshape(B, Lq, H, d_head).transpose(0, 2, 1, 3)
        v = (w @ Wv.T).reshape(B, Lq, H, d_head).transpose(0, 2, 1, 3)
        rp = (r @ Wr.T).reshape(2 * Lq - 1, H, d_head).transpose(1, 0, 2)
        AC = jnp.einsum('bhid,bhjd->bhij', q + u_bias[None, :, None, :], k)
        BD = jnp.einsum('bhid,hjd->bhij', q + v_bias[None, :, None, :], rp)
        BD = _rel_shift(BD)
        attn = jax.nn.softmax((AC + BD) * scale, axis=-1)
        out = jnp.einsum('bhij,bhjd->bhid', attn, v)
        return out.transpose(0, 2, 1, 3).reshape(B, Lq, D)

    def _L1_ffn_ref(x, scores, expert_weights, expert_indices, w1, w2, bias):
        import jax, jax.numpy as jnp
        import numpy as np
        SL, BS, HS, FF, E, TOPK = (512, 2, 256, 1024, 8, 2)
        sl, bs, hs = x.shape
        n_exp = w1.shape[0]
        top_k = expert_indices.shape[-1]
        xf = x.reshape(-1, hs)
        flat_idx = expert_indices.reshape(-1)
        flat_w = expert_weights.reshape(-1)
        order = jnp.argsort(flat_idx)
        tok = order // top_k
        tokens_per_expert = jnp.bincount(flat_idx, length=n_exp).astype(jnp.int32)
        xs = xf[tok]
        h = jax.nn.gelu(jax.lax.ragged_dot(xs, w1, tokens_per_expert), approximate=False)
        ys = jax.lax.ragged_dot(h, w2, tokens_per_expert)
        ys = ys * flat_w[order][:, None]
        out = jnp.zeros_like(xf).at[tok].add(ys)
        return out.reshape(sl, bs, hs) + bias
    x = L0_attn_x
    x = _layernorm(x + _L0_attn_ref(x, L0_attn_Wq, L0_attn_bq, L0_attn_Wk, L0_attn_bk, L0_attn_Wv, L0_attn_bv, L0_attn_Wa, L0_attn_ba, L0_attn_Wb, L0_attn_bb, L0_attn_Wg, L0_attn_bg, L0_attn_Wo, L0_attn_bo), axis=-1)
    x = _layernorm(x + _L0_ffn_ref(x, L0_ffn_wqkv, L0_ffn_q_scale, L0_ffn_k_scale, L0_ffn_wo, L0_ffn_ln_g, L0_ffn_ln_b, L0_ffn_w1, L0_ffn_b1, L0_ffn_w2, L0_ffn_b2), axis=-1)
    x = _layernorm(x + _L1_attn_ref(x, L1_attn_Wq, L1_attn_Wk, L1_attn_Wv, L1_attn_Wr, L1_attn_u_bias, L1_attn_v_bias), axis=-1)
    x = _layernorm(x + _L1_ffn_ref(x, L1_ffn_scores, L1_ffn_expert_weights, L1_ffn_expert_indices, L1_ffn_w1, L1_ffn_w2, L1_ffn_bias), axis=-1)
    return x

_drawn_inputs = setup_inputs


def setup_inputs(seed=0):
    import zlib

    import numpy as np

    out = dict(_drawn_inputs(seed))
    spreads = {'L0_attn_bq': (0.0, 0.1),
     'L0_attn_bk': (0.0, 0.1),
     'L0_attn_bv': (0.0, 0.1),
     'L0_attn_bg': (0.0, 0.698),
     'L0_attn_bo': (0.0, 0.1),
     'L0_ffn_q_scale': (1.0, 0.6),
     'L0_ffn_k_scale': (1.0, 0.6),
     'L0_ffn_ln_g': (1.0, 0.6),
     'L0_ffn_ln_b': (0.0, 0.8),
     'L0_ffn_b1': (0.0, 0.8),
     'L0_ffn_b2': (0.0, 0.1),
     'L1_ffn_bias': (0.0, 0.1)}
    factors = {'L0_ffn_wqkv': 3.229,
     'L0_ffn_wo': 3.02,
     'L1_attn_Wq': 8.0,
     'L1_attn_Wk': 8.0,
     'L1_attn_Wr': 8.0,
     'L1_attn_u_bias': 8.0,
     'L1_attn_v_bias': 8.0}
    for name, (base, spread) in spreads.items():
        noise = np.random.default_rng([zlib.crc32(name.encode()), seed]).standard_normal(out[name].shape)
        drawn = base * np.exp(spread * noise) if base else spread * noise
        out[name] = jnp.asarray(drawn.astype(out[name].dtype))
    for name, factor in factors.items():
        out[name] = (out[name] * factor).astype(out[name].dtype)
    return out
```

```python
from contextlib import ExitStack

import numpy as np

import concourse.bass as bass
from concourse import mybir

F32 = mybir.dt.float32
BF16 = mybir.dt.bfloat16
I32 = mybir.dt.int32
ACT = mybir.ActivationFunctionType
ALU = mybir.AluOpType
AX_X = mybir.AxisListType.X

P = 128
NB = 2
T = 2048
D = 256
KB = D // P
NT = T // P
PAD = 4
LN_EPS = 1e-5
LEVELS = 7


class Steps:

    def __init__(self, eng, sem, per_turn=0, turn=0):
        self.eng, self.sem, self.per, self.turn, self.k = eng, sem, per_turn, turn, 0

    def done(self, ins):
        self.k += 1
        ins.then_inc(self.sem, 1)
        self.eng.wait_ge(self.sem, self.turn * self.per + self.k)

    def close(self):
        assert self.k == self.per, self.k


def across(ap, n):
    return ap.unsqueeze(1).to_broadcast([ap.shape[0], n, ap.shape[1]])


def ds(at, n):
    return bass.ds(at, n)


class Scope:

    def __init__(self, nc, ctx, prefix):
        self.nc, self.ctx, self.prefix = nc, ctx, prefix

    def sb(self, name, shape, dt=F32):
        return self.ctx.enter_context(self.nc.sbuf_tensor(self.prefix + name, shape, dt))

    def pb(self, name, shape, dt=F32):
        return self.ctx.enter_context(self.nc.psum_tensor(self.prefix + name, shape, dt))

    def sem(self, name):
        return self.ctx.enter_context(self.nc.semaphore(self.prefix + name))


def delta_rule_masks():
    s, t = np.arange(P)[:, None], np.arange(P)[None, :]
    out = [s <= t, s > t]
    size = 1
    while size < P:
        out.append((t // size % 2 == 1) & (s // size == t // size - 1))
        size *= 2
    return np.stack(out, 1).astype(np.float32)


def delta_rule_stage(nc, io, g):
    xT, ident, ones, mhalf = g["xT"], g["ident"], g["ones"], g["mhalf"]
    PER_DVE, PER_ACT = 6, 1
    C = P
    NKV = 2 * C + 2
    with ExitStack() as ctx:
        m = Scope(nc, ctx, "dr_")
        masks = m.sb("masks", [P, 2 + LEVELS, P])
        upto, after = masks[:, 0, :], masks[:, 1, :]
        wkv = m.sb("wkv", [P, KB, NKV])
        wqg = m.sb("wqg", [P, KB, 2, C])
        wo = m.sb("wo", [P, D])
        bkv = m.sb("bkv", [1, NKV])
        bo = m.sb("bo", [1, D])
        bqg = m.sb("bqg", [P, 2])
        xs = m.sb("xs", [P, KB, NB, P])
        junk = m.sb("junk", [P, NB, C])
        ss = m.sb("ss", [P, NB])
        rn = m.sb("rn", [P, NB])
        z = m.sb("z", [P, NB, 2])
        e = m.sb("e", [P, NB, 2])
        den = m.sb("den", [P, NB, 2])
        zneg = m.sb("zneg", [P, NB])
        beta = m.sb("beta", [P, NB, 2])
        ln1 = m.sb("ln1", [P, NB])
        la = m.sb("la", [P, NB])
        laB = m.sb("laB", [P, NB, P])
        gcol = m.sb("gcol", [P, NB])
        eg = m.sb("eg", [P, 3, NB])
        gb = m.sb("gb", [P, NB])
        kn = m.sb("kn", [P, NB, C])
        kb = m.sb("kb", [P, NB, C])
        gbk = m.sb("gbk", [P, NB, C])
        kend = m.sb("kend", [P, NB, C])
        bv = m.sb("bv", [P, NB, C])
        qT = m.sb("qT", [P, NB, P])
        qgT = m.sb("qgT", [P, NB, P])
        gz = m.sb("gz", [P, NB, P])
        gd = m.sb("gd", [P, NB, P])
        gateT = m.sb("gateT", [P, NB, P])
        dneg = m.sb("dneg", [P, NB, P])
        dec = m.sb("dec", [P, NB, P])
        decM = m.sb("decM", [P, NB, P])
        egrow = m.sb("egrow", [P, NB, P])
        kT = m.sb("kT", [P, 2, NB, P])
        AT = m.sb("AT", [P, NB, P])
        XT = m.sb("XT", [P, LEVELS, NB, P])
        TR = m.sb("TR", [P, 2, NB, P])
        Y = m.sb("Y", [P, NB, P])
        W0 = m.sb("W0", [P, 2, NB, P])
        W1T = m.sb("W1T", [P, NB, P])
        U = m.sb("U", [P, 2, NB, P])
        S = m.sb("S", [P, NB, 2, P])
        PT = m.sb("PT", [P, NB, P])
        ogT = m.sb("ogT", [P, NB, P])
        st6 = m.sb("st6", [P, NB, 6])
        mv = m.sb("mv", [P, NB, 2])
        vpe = m.sb("vpe", [P, NB])
        rstd = m.sb("rstd", [P, NB])
        yn = m.sb("yn", [P, NB, D])

        pKV = [m.pb(f"pKV{b}", [P, 512]) for b in range(NB)]
        pQG = m.pb("pQG", [P, 2, NB, P])
        pG = m.pb("pG", [P, 512])
        pT = m.pb("pT", [P, 2, NB, P])
        pY = m.pb("pY", [P, 512])
        pZ = m.pb("pZ", [P, 2, NB, P])
        pO = m.pb("pO", [P, 2, NB, P])
        grow_p = pG[:, 0:NB * P].rearrange("p (b t) -> p b t", b=NB)
        gcol_p = pG[:, 256:256 + 3 * NB].rearrange("p (k b) -> p k b", k=3)
        Y_p = pY[:, 0:NB * P].rearrange("p (b t) -> p b t", b=NB)
        S_p = pT[:, :, :, :]
        O_p, PT_p = pO[:, 0, :, :], pO[:, 1, :, :]
        out_p = pY[:, :].rearrange("p (b d) -> p b d", b=NB)

        loaded, staged, kv_p, qg_p, ss_ready, ssm_ready, rn_ready = map(m.sem, (
            "loaded", "staged", "kv_p", "qg_p", "ss_ready", "ssm_ready", "rn_ready"))
        q_ready, gz_ready, z_ready, ln_ready, la_ready, g_p, eg_ready = map(m.sem, (
            "q_ready", "gz_ready", "z_ready", "ln_ready", "la_ready", "g_p", "eg_ready"))
        d_ready, dec_ready, decM_ready, qgT_ready, scaled, kT_p, kT_ready = map(m.sem, (
            "d_ready", "dec_ready", "decM_ready", "qgT_ready", "scaled", "kT_p", "kT_ready"))
        kk_p, at_ready, xt_ready, tr_ready, level_y, y_ready, level_z = map(m.sem, (
            "kk_p", "at_ready", "xt_ready", "tr_ready", "level_y", "y_ready", "level_z"))
        w_p, w0_ready, w1_ready, u_p, u_ready, pt_p, pt_ready, s_p, s_ready, o_p, og_ready = map(m.sem, (
            "w_p", "w0_ready", "w1_ready", "u_p", "u_ready", "pt_p", "pt_ready", "s_p", "s_ready", "o_p", "og_ready"))
        y_p, var_ready, rstd_ready, yn_ready, ynT_p, x_stored, inited, dve_step = map(m.sem, (
            "y_p", "var_ready", "rstd_ready", "yn_ready", "ynT_p", "x_stored", "inited", "dve_step"))
        act_step = m.sem("act_step")

        with nc.Block() as block:
            @block.sync
            def _(sp):
                for dst, src in ((masks[:, :, :], io["masks"]), (wkv[:, :, :], io["dr_wkv"]),
                                 (wqg[:, :, :, :], io["dr_wqg"]), (wo[:, :], io["dr_wo"]),
                                 (bkv[:, :], io["dr_bkv"]), (bo[:, :], io["dr_bo"]), (bqg[:, :], io["dr_bqg"]),
                                 (ident[:, :], io["ident"])):
                    sp.dma_start(dst, src).then_inc(loaded, 16)
                for k in range(KB):
                    sp.dma_start(xT[:, k, :, PAD:], io["xT"][:, k, :, :]).then_inc(loaded, 16)
                sp.wait_ge(loaded, 16 * (8 + KB))

            @block.gpsimd
            def _(pool):
                pool.memset(xT[:, :, :, 0:PAD], 0.0)
                pool.memset(ones[:, :], 1.0)
                pool.memset(mhalf[:, :], -0.5)
                pool.memset(S[:, :, :, :], 0.0).then_inc(s_ready, 1)
                pool.memset(ss[:, :], 1.0).then_inc(y_p, 1)
                pool.memset(z[:, :, :], 0.0).then_inc(x_stored, 1)

        with nc.Block() as block:
            @block.gpsimd
            def _(pool):
                with pool.Fori(0, NT) as n:
                    pool.wait_ge(y_p, n + 1)
                    for b in range(NB):
                        nc.gpsimd.tensor_copy(xs[:, :, b, :], xT[:, :, b, ds(n * P + PAD, P)]).then_inc(staged, 1)
                    pool.wait_ge(ssm_ready, n + 1)
                    nc.gpsimd.tensor_tensor(rn[:, :], ss[:, :], mhalf[:, 0:NB], ALU.pow).then_inc(rn_ready, 1)
                    pool.wait_ge(q_ready, n + 1)
                    pool.wait_ge(eg_ready, n + 1)
                    nc.gpsimd.tensor_tensor(qgT[:, :, :], qT[:, :, :], egrow[:, :, :], ALU.mult).then_inc(qgT_ready, 1)
                    pool.wait_ge(dec_ready, n + 1)
                    nc.gpsimd.tensor_tensor(decM[:, :, :], dec[:, :, :], across(upto, NB), ALU.mult).then_inc(decM_ready, 1)
                    pool.wait_ge(at_ready, n + 1)
                    for lv in range(LEVELS):
                        nc.gpsimd.tensor_tensor(XT[:, lv, :, :], AT[:, :, :], across(masks[:, 2 + lv, :], NB),
                                                ALU.mult).then_inc(xt_ready, 1)
                    pool.wait_ge(var_ready, n + 1)
                    nc.gpsimd.tensor_tensor(rstd[:, :], vpe[:, :], mhalf[:, 0:NB], ALU.pow).then_inc(rstd_ready, 1)

            @block.scalar
            def _(act):
                with act.Fori(0, NT) as n:
                    own = Steps(act, act_step, PER_ACT, n)
                    act.wait_ge(kv_p, n + 1)
                    for b in range(NB):
                        nc.scalar.activation(z[:, b, 0:1], pKV[b][:, 2 * C:2 * C + 1], ACT.Abs)
                        nc.scalar.activation(z[:, b, 1:2], pKV[b][:, 2 * C + 1:2 * C + 2], ACT.Copy)
                        ins = nc.scalar.activation(junk[:, b, :], pKV[b][:, 0:C], ACT.Square, accum_out=ss[:, b:b + 1])
                    ins.then_inc(ss_ready, 1)
                    act.wait_ge(qg_p, n + 1)
                    nc.scalar.activation(qT[:, :, :], pQG[:, 0, :, :], ACT.Identity, bias=bqg[:, 0:1]).then_inc(q_ready, 1)
                    nc.scalar.activation(gz[:, :, :], pQG[:, 1, :, :], ACT.Exp, bias=bqg[:, 1:2],
                                         scale=-1.0).then_inc(gz_ready, 1)
                    act.wait_ge(ss_ready, n + 1)
                    own.done(nc.scalar.activation(e[:, :, :], z[:, :, :], ACT.Exp, scale=-1.0))
                    nc.scalar.activation(ln1[:, :], e[:, :, 0], ACT.Ln, bias=1.0).then_inc(ln_ready, 1)
                    act.wait_ge(d_ready, n + 1)
                    nc.scalar.activation(eg[:, :, :], gcol_p, ACT.Exp)
                    nc.scalar.activation(egrow[:, :, :], grow_p, ACT.Exp).then_inc(eg_ready, 1)
                    nc.scalar.activation(dec[:, :, :], dneg[:, :, :], ACT.Exp).then_inc(dec_ready, 1)
                    act.wait_ge(kT_p, n + 1)
                    nc.scalar.activation(kT[:, :, :, :], pT[:, :, :, :], ACT.Copy).then_inc(kT_ready, 1)
                    act.wait_ge(w_p, n + 1)
                    nc.scalar.activation(W1T[:, :, :], pT[:, 0, :, :], ACT.Copy).then_inc(w1_ready, 1)
                    act.wait_ge(ynT_p, n + 1)
                    for b in range(NB):
                        ins = nc.scalar.activation(xT[:, :, b, ds(n * P + PAD, P)], pQG[:, :, b, :], ACT.Copy)
                    ins.then_inc(x_stored, 1)
                    own.close()

            @block.vector
            def _(dve):
                nc.vector.tensor_scalar(bqg[:, 1:2], bqg[:, 1:2], -1.0, None, ALU.mult).then_inc(inited, 1)
                with dve.Fori(0, NT) as n:
                    own = Steps(dve, dve_step, PER_DVE, n)
                    dve.wait_ge(ss_ready, n + 1)
                    for b in range(NB):
                        za = pKV[b][:, 2 * C:2 * C + 1]
                        ins = nc.vector.tensor_scalar(zneg[:, b:b + 1], za, 0.0, None, ALU.min)
                    nc.vector.tensor_scalar(ss[:, :], ss[:, :], 1e-24, None, ALU.max).then_inc(ssm_ready, 1)
                    dve.wait_ge(ssm_ready, n + 1)
                    dve.wait_ge(ln_ready, n + 1)
                    nc.vector.tensor_tensor(la[:, :], zneg[:, :], ln1[:, :], ALU.subtract)
                    own.done(nc.vector.tensor_scalar(den[:, :, :], e[:, :, :], 1.0, None, ALU.add))
                    nc.vector.reciprocal(beta[:, :, :], den[:, :, :])
                    for b in range(NB):
                        ins = nc.vector.tensor_scalar(laB[:, b, :], ones[:, :], la[:, b:b + 1], None, ALU.mult)
                    ins.then_inc(la_ready, 1)
                    dve.wait_ge(gz_ready, n + 1)
                    own.done(nc.vector.tensor_scalar(gd[:, :, :], gz[:, :, :], 1.0, None, ALU.add))
                    nc.vector.reciprocal(gateT[:, :, :], gd[:, :, :])
                    dve.wait_ge(g_p, n + 1)
                    own.done(nc.vector.tensor_copy(gcol[:, :], gcol_p[:, 0, :]))
                    for b in range(NB):
                        ins = nc.vector.tensor_scalar(dneg[:, b, :], grow_p[:, b, :], gcol[:, b:b + 1], 0.0,
                                                      ALU.subtract, ALU.min)
                    ins.then_inc(d_ready, 1)
                    dve.wait_ge(rn_ready, n + 1)
                    dve.wait_ge(eg_ready, n + 1)
                    nc.vector.tensor_tensor(gb[:, :], beta[:, :, 1], eg[:, 0, :], ALU.mult)
                    for b in range(NB):
                        nc.vector.tensor_scalar(bv[:, b, :], pKV[b][:, C:2 * C], beta[:, b, 1:2], None, ALU.mult)
                        ins = nc.vector.tensor_scalar(kn[:, b, :], pKV[b][:, 0:C], rn[:, b:b + 1], None, ALU.mult)
                    own.done(ins)
                    for b in range(NB):
                        nc.vector.tensor_scalar(kb[:, b, :], kn[:, b, :], beta[:, b, 1:2], None, ALU.mult)
                        nc.vector.tensor_scalar(gbk[:, b, :], kn[:, b, :], gb[:, b:b + 1], None, ALU.mult)
                        ins = nc.vector.tensor_scalar(kend[:, b, :], kn[:, b, :], eg[:, 1, b:b + 1], None, ALU.mult)
                    ins.then_inc(scaled, 1)
                    nc.vector.tensor_copy(TR[:, :, :, :].rearrange("p a b t -> p (a b) t"),
                                          across(ident[:, :], 2 * NB)).then_inc(tr_ready, 1)
                    dve.wait_ge(kk_p, n + 1)
                    dve.wait_ge(dec_ready, n + 1)
                    nc.vector.tensor_tensor(AT[:, :, :], Y_p, dec[:, :, :], ALU.mult).then_inc(at_ready, 1)
                    for lv in range(LEVELS):
                        dve.wait_ge(level_y, n * LEVELS + lv + 1)
                        nc.vector.tensor_copy(Y[:, :, :], Y_p).then_inc(y_ready, 1)
                        dve.wait_ge(tr_ready, n * (LEVELS + 1) + lv + 1)
                        dve.wait_ge(level_z, n * LEVELS + lv + 1)
                        nc.vector.tensor_tensor(TR[:, :, :, :], TR[:, :, :, :], pZ[:, :, :, :],
                                                ALU.subtract).then_inc(tr_ready, 1)
                    dve.wait_ge(w_p, n + 1)
                    nc.vector.tensor_copy(W0[:, :, :, :], pZ[:, :, :, :]).then_inc(w0_ready, 1)
                    dve.wait_ge(w0_ready, n + 1)
                    dve.wait_ge(u_p, n + 1)
                    nc.vector.tensor_tensor(U[:, :, :, :], W0[:, :, :, :], pZ[:, :, :, :], ALU.subtract).then_inc(u_ready, 1)
                    dve.wait_ge(pt_p, n + 1)
                    dve.wait_ge(decM_ready, n + 1)
                    nc.vector.tensor_tensor(PT[:, :, :], PT_p, decM[:, :, :], ALU.mult).then_inc(pt_ready, 1)
                    dve.wait_ge(o_p, n + 1)
                    nc.vector.tensor_tensor(ogT[:, :, :], O_p, gateT[:, :, :], ALU.mult).then_inc(og_ready, 1)
                    dve.wait_ge(s_p, n + 1)
                    for b in range(NB):
                        ins = nc.vector.scalar_tensor_tensor(S[:, b, :, :], S[:, b, :, :], eg[:, 2, b:b + 1], S_p[:, b, :, :],
                                                             ALU.mult, ALU.add)
                    ins.then_inc(s_ready, 1)
                    dve.wait_ge(y_p, n + 2)
                    for b in range(NB):
                        ins = nc.vector.bn_stats(st6[:, b, :], out_p[:, b, :])
                    own.done(ins)
                    dve.nop(nofuse=True)
                    for b in range(NB):
                        ins = nc.vector.bn_aggr(mv[:, b, :], st6[:, b, :])
                    own.done(ins)
                    nc.vector.tensor_scalar(vpe[:, :], mv[:, :, 1], LN_EPS, None, ALU.add).then_inc(var_ready, 1)
                    dve.wait_ge(rstd_ready, n + 1)
                    for b in range(NB):
                        ins = nc.vector.tensor_scalar(yn[:, b, :], out_p[:, b, :], mv[:, b, 0:1], rstd[:, b:b + 1],
                                                      ALU.subtract, ALU.mult)
                    ins.then_inc(yn_ready, 1)
                    own.close()

            @block.tensor
            def _(pe):
                mm = nc.tensor.matmul
                with pe.Fori(0, NT) as n:
                    pe.wait_ge(staged, NB * (n + 1))
                    for b in range(NB):
                        for k in range(KB):
                            mm(pKV[b][:, 0:NKV], xs[:, k, b, :], wkv[:, k, :], start=(k == 0), stop=False)
                        ins = mm(pKV[b][:, 0:NKV], ones[0:1, :], bkv[0:1, :], start=False, stop=True)
                    ins.then_inc(kv_p, 1)
                    pe.wait_ge(inited, 1)
                    pe.wait_ge(x_stored, n + 1)
                    for i in range(2):
                        for k in range(KB):
                            ins = mm(pQG[:, i, :, :], wqg[:, k, i, :], xs[:, k, :, :], start=(k == 0), stop=(k == KB - 1))
                    ins.then_inc(qg_p, 1)
                    pe.wait_ge(la_ready, n + 1)
                    for i, w in enumerate((upto, after, ones[:, :])):
                        mm(gcol_p[:, i, :], w, la[:, :], start=True, stop=True)
                    for b in range(NB):
                        ins = mm(grow_p[:, b, :], laB[:, b, :], upto, start=True, stop=True)
                    ins.then_inc(g_p, 1)
                    pe.wait_ge(scaled, n + 1)
                    for b in range(NB):
                        nc.tensor.transpose(pT[:, 0, b, :], kn[:, b, :], ident[:, :])
                        ins = nc.tensor.transpose(pT[:, 1, b, :], kb[:, b, :], ident[:, :])
                    ins.then_inc(kT_p, 1)
                    pe.wait_ge(kT_ready, n + 1)
                    for b in range(NB):
                        ins = mm(Y_p[:, b, :], kT[:, 0, b, :], kT[:, 1, b, :], start=True, stop=True)
                    ins.then_inc(kk_p, 1)
                    for lv in range(LEVELS):
                        pe.wait_ge(xt_ready, n * LEVELS + lv + 1)
                        pe.wait_ge(tr_ready, n * (LEVELS + 1) + lv + 1)
                        for b in range(NB):
                            ins = mm(Y_p[:, b, :], XT[:, lv, b, :], TR[:, 0, b, :], start=True, stop=True)
                        ins.then_inc(level_y, 1)
                        pe.wait_ge(y_ready, n * LEVELS + lv + 1)
                        for b in range(NB):
                            mm(pZ[:, 0, b, :], TR[:, 1, b, :], Y[:, b, :], start=True, stop=True)
                            ins = mm(pZ[:, 1, b, :], Y[:, b, :], TR[:, 1, b, :], start=True, stop=True)
                        ins.then_inc(level_z, 1)
                    pe.wait_ge(tr_ready, (n + 1) * (LEVELS + 1))
                    for b in range(NB):
                        mm(pT[:, 0, b, :], gbk[:, b, :], TR[:, 1, b, :], start=True, stop=True)
                        mm(pZ[:, 0, b, :], TR[:, 1, b, :], bv[:, b, :], start=True, stop=True)
                        ins = mm(pZ[:, 1, b, :], bv[:, b, :], TR[:, 1, b, :], start=True, stop=True)
                    ins.then_inc(w_p, 1)
                    pe.wait_ge(w0_ready, n + 1)
                    pe.wait_ge(w1_ready, n + 1)
                    pe.wait_ge(s_ready, n + 1)
                    for b in range(NB):
                        mm(pZ[:, 0, b, :], W1T[:, b, :], S[:, b, 1, :], start=True, stop=True)
                        ins = mm(pZ[:, 1, b, :], S[:, b, 1, :], W1T[:, b, :], start=True, stop=True)
                    ins.then_inc(u_p, 1)
                    pe.wait_ge(u_ready, n + 1)
                    pe.wait_ge(q_ready, n + 1)
                    for b in range(NB):
                        ins = mm(PT_p[:, b, :], U[:, 1, b, :], qT[:, b, :], start=True, stop=True)
                    ins.then_inc(pt_p, 1)
                    for b in range(NB):
                        mm(S_p[:, b, 0, :], U[:, 0, b, :], kend[:, b, :], start=True, stop=True)
                        ins = mm(S_p[:, b, 1, :], kend[:, b, :], U[:, 0, b, :], start=True, stop=True)
                    ins.then_inc(s_p, 1)
                    pe.wait_ge(pt_ready, n + 1)
                    pe.wait_ge(qgT_ready, n + 1)
                    for b in range(NB):
                        mm(O_p[:, b, :], S[:, b, 0, :], qgT[:, b, :], start=True, stop=False)
                        ins = mm(O_p[:, b, :], kn[:, b, :], PT[:, b, :], start=False, stop=True)
                    ins.then_inc(o_p, 1)
                    pe.wait_ge(og_ready, n + 1)
                    for b in range(NB):
                        mm(out_p[:, b, :], ogT[:, b, :], wo[:, :], start=True, stop=False)
                        for k in range(KB):
                            mm(out_p[:, b, k * P:(k + 1) * P], xs[:, k, b, :], ident[:, :], start=False,
                               stop=False, skip_group_check=True)
                        ins = mm(out_p[:, b, :], ones[0:1, :], bo[0:1, :], start=False, stop=True)
                    ins.then_inc(y_p, 1)
                    pe.wait_ge(yn_ready, n + 1)
                    for b in range(NB):
                        for k in range(KB):
                            ins = nc.tensor.transpose(pQG[:, k, b, :], yn[:, b, k * P:(k + 1) * P], ident[:, :])
                    ins.then_inc(ynT_p, 1)


DEPTH = 2
HEADS = 8
DH = 64
INNER = HEADS * DH
HP = INNER // P
WINDOW = 128
HID = 682
HC = -(-HID // P)
QKV_AT = 0
WO_AT = QKV_AT + KB * 3 * INNER
W1_AT = WO_AT + HP * D
W2_AT = W1_AT + KB * 2 * HID
B1_AT = W2_AT + HC * D
B2_AT = B1_AT + 2 * HC
LG_AT = B2_AT + KB
LB_AT = LG_AT + KB
QS_AT = LB_AT + KB
TAB_AT = QS_AT + 4 * DH
LAYER_COLS = TAB_AT + NT * 4 * DH
MASKED = -3.0e38


def rotary_tables():
    half = np.arange(0, DH, 2, dtype=np.float32)
    inv = (1.0 / 10000.0 ** (half / DH)).astype(np.float32)
    t = np.arange(T, dtype=np.float32)
    freqs = (t[:, None] * inv[None, :]).astype(np.float32)
    base = ((half + 0.4 * DH) / (1.4 * DH)).astype(np.float32)
    power = (t - T // 2) / float(WINDOW // 2)
    scale = base[None, :].astype(np.float64) ** power[:, None]
    cos, sin = np.cos(freqs.astype(np.float64)), np.sin(freqs.astype(np.float64))

    def both(a, sign=1.0):
        return np.concatenate([sign * a, a], -1)

    kinds = [both(cos * scale) * 8.0, both(cos / scale), both(sin * scale, -1.0) * 8.0, both(sin / scale, -1.0)]
    tab = np.stack(kinds, 1).astype(np.float32)
    return tab.reshape(NT, P, 4 * DH).transpose(1, 0, 2).reshape(P, -1)


def window_masks():
    i, j = np.arange(P)[:, None], np.arange(P)[None, :]
    no = np.full((P, P), MASKED)
    this = np.where(j <= i, 0.0, MASKED)
    last = np.where(j >= i, 0.0, MASKED)
    first, later = np.concatenate([no, this], 1), np.concatenate([last, this], 1)
    return np.stack([np.concatenate([a, a], 1) for a in (first, later)], 1).astype(np.float32)


def local_stage(nc, io, g):
    xT, x1T, ident, ones, mhalf = g["xT"], g["x1T"], g["ident"], g["ones"], g["mhalf"]
    with ExitStack() as ctx:
        m = Scope(nc, ctx, "lo_")
        wts = m.sb("wts", [P, LAYER_COLS])

        def part(at, *shape):
            n = int(np.prod(shape))
            names = "abc"[:len(shape)]
            return wts[:, at:at + n].rearrange(f"p ({' '.join(names)}) -> p {' '.join(names)}",
                                               **dict(zip(names, shape)))

        wqkv = part(QKV_AT, KB, 3 * INNER)
        wo = part(WO_AT, HP, D)
        w1 = part(W1_AT, KB, 2, HID)
        w2 = part(W2_AT, HC, D)
        b1 = part(B1_AT, 2, HC)
        b2, lg, lb = wts[:, B2_AT:B2_AT + KB], wts[:, LG_AT:LG_AT + KB], wts[:, LB_AT:LB_AT + KB]
        qs = wts[:, QS_AT:QS_AT + 4 * DH]
        tab = part(TAB_AT, NT, 4 * DH)

        maskf = m.sb("maskf", [P, 2, 4 * P])
        maskt = m.sb("maskt", [P, 2, 4 * P], BF16)
        identb = m.sb("identb", [P, P], BF16)
        HS = 4
        hs = m.sb("hs", [P, KB, NB, HS + P])
        sq = m.sb("sq", [P, 2 * HEADS, DH])
        ss = m.sb("ss", [P, 2 * HEADS])
        ssm = m.sb("ssm", [P, 2 * HEADS])
        rn = m.sb("rn", [P, 2 * HEADS])
        qn = m.sb("qn", [P, 2, HEADS, DH])
        r1 = m.sb("r1", [P, 2, HEADS, DH])
        r2 = m.sb("r2", [P, 2, HEADS, DH])
        qT = m.sb("qT", [P, HP, P])
        kT = m.sb("kT", [P, HP, NB, 2 * P])
        V = m.sb("V", [P, NB, 2, INNER])
        Pm = m.sb("Pm", [P, 2, 2, 2 * P])
        sums = m.sb("sums", [P, HEADS])
        rsum = m.sb("rsum", [P, HEADS])
        nmx = m.sb("nmx", [P, HEADS])
        PT = m.sb("PT", [P, 2, 4, P])
        OT = m.sb("OT", [P, HP, NB, P])
        xm = m.sb("xm", [P, KB, NB, HS + P])
        st6 = m.sb("st6", [P, NB, 6])
        mv = m.sb("mv", [P, NB, 2])
        vpe = m.sb("vpe", [P, NB])
        rstd = m.sb("rstd", [P, NB])
        hn = m.sb("hn", [P, NB, D])
        hnT = m.sb("hnT", [P, KB, NB, P])
        KLAST = HID - (HC - 1) * P
        hu = m.sb("hu", [P, 2, HC, NB * P])
        hid = m.sb("hid", [P, HC, NB * P])

        pQKV = [m.pb(f"pQKV{n}", [P, 512]) for n in range(3)]
        pAB = [m.pb(f"p{n}", [P, 4, P]) for n in "AB"]
        pS = [m.pb(f"pS{n}", [P, 2, 2 * P]) for n in range(2)]
        pO = m.pb("pO", [P, 4, P])
        y_b = pQKV[0][:, :].rearrange("p (f b t) -> p f b t", f=KB, b=NB)
        x_p = pO[:, :, :].rearrange("p (f b) t -> p f b t", f=KB)
        hn_p = pAB[0][:, :, :].rearrange("p (b k) t -> p b (k t)", b=NB)
        hT_b = pAB[1][:, :, :].rearrange("p (k b) t -> p k b t", k=KB)

        (weights, tables, staged, qkv_p, sq_ready, v_ready, ssm_ready, rn_ready, qn_ready, r2_ready, qr_ready,
         qkT_p, qkT_ready) = map(m.sem, (
             "weights", "tables", "staged", "qkv_p", "sq_ready", "v_ready", "ssm_ready", "rn_ready", "qn_ready",
             "r2_ready", "qr_ready", "qkT_p", "qkT_ready"))
        pool_step, shifted, u_ready, att_step, mlp_step = map(m.sem, (
            "pool_step", "shifted", "u_ready", "att_step", "mlp_step"))
        (s_p, mx_ready, e_ready, pn_ready, pT_p, pT_ready, o_p, ot_ready, xm_p, xm_ready, h_p, var_ready, rstd_ready,
         hn_ready, hT_p, hnT_ready, u_p, gl_ready, hid_ready, y_p, x_stored        ) = map(m.sem, (
             "s_p", "mx_ready", "e_ready", "pn_ready", "pT_p", "pT_ready", "o_p", "ot_ready", "xm_p", "xm_ready",
             "h_p", "var_ready", "rstd_ready", "hn_ready", "hT_p", "hnT_ready", "u_p", "gl_ready", "hid_ready",
             "y_p", "x_stored"))

        with nc.Block() as block:
            @block.sync
            def _(sp):
                sp.dma_start(maskf[:, :, :], io["lo_mask"]).then_inc(weights, 16)
                sp.wait_ge(weights, 16)

            @block.gpsimd
            def _(pool):
                pool.memset(hs[:, :, :, :], 0.0)
                pool.memset(xm[:, :, :, :], 0.0)
                pool.memset(kT[:, :, :, :], 0.0)
                pool.memset(V[:, :, :, :], 0.0).then_inc(x_stored, 1)

            @block.vector
            def _(dve):
                dve.wait_ge(weights, 16)
                nc.vector.tensor_copy(maskt[:, :, :], maskf[:, :, :])
                nc.vector.tensor_copy(identb[:, :], ident[:, :])

            @block.scalar
            def _(act):
                for k in range(KB):
                    nc.scalar.activation(x1T[:, k, :, :], xT[:, k, :, :], ACT.Copy)

        def layers(eng, turn):
            with eng.Fori(0, DEPTH) as layer:
                turn(layer, layer * NT, 0, True, False)
                with eng.Fori(1, NT) as w:
                    turn(layer, layer * NT + w, w, True, True)
                turn(layer, layer * NT + NT, NT, False, True)

        with nc.Block() as block:
            @block.sync
            def _(sp):
                with sp.Fori(0, DEPTH) as layer:
                    sp.wait_ge(x_stored, layer * NT + 1)
                    sp.dma_start(wts[:, :], io["lo_wts"][ds(layer, 1), :, :].rearrange("l p n -> (l p) n")).then_inc(weights, 16)

            @block.gpsimd
            def _(pool):
                def rotate(t, w, b):
                    pool.wait_ge(ssm_ready, t * NB + b + 1)
                    nc.gpsimd.tensor_tensor(rn[:, :], ssm[:, :], mhalf[:, :], ALU.pow).then_inc(rn_ready, 1)
                    pool.wait_ge(qn_ready, t * NB + b + 1)
                    pool.nop(nofuse=True)
                    for to, frm in ((0, DH // 2), (DH // 2, 0)):
                        for qk in range(2):
                            sines = tab[:, ds(w, 1), (2 + qk) * DH + to:(2 + qk) * DH + to + DH // 2]
                            nc.gpsimd.tensor_tensor(r2[:, qk, :, to:to + DH // 2], qn[:, qk, :, frm:frm + DH // 2],
                                                    sines.to_broadcast([P, HEADS, DH // 2]),
                                                    ALU.mult).then_inc(r2_ready, 1)

                def turn(layer, t, w, att, mlp):
                    if not mlp:
                        pool.wait_ge(tables, layer + 1)
                        pool.nop(nofuse=True)
                        nc.gpsimd.memset(hs[:, :, :, HS - 1:HS], 0.0).then_inc(pool_step, 1)
                        nc.gpsimd.memset(V[:, :, 0, :], 0.0).then_inc(shifted, 1)
                    elif att:
                        pool.wait_ge(qkv_p, t * NB)
                        pool.nop(nofuse=True)
                        nc.gpsimd.tensor_copy(hs[:, :, :, HS - 1:HS], hs[:, :, :, HS + P - 1:HS + P]).then_inc(pool_step, 1)
                        pool.wait_ge(pool_step, t + 1)
                        pool.nop(nofuse=True)
                    if att:
                        for k in range(KB):
                            nc.gpsimd.tensor_copy(hs[:, k, :, HS:], x1T[:, k, :, ds(w * P + PAD, P)]).then_inc(staged, 1)
                    if att and mlp:
                        pool.wait_ge(o_p, t * NB)
                        pool.nop(nofuse=True)
                        nc.gpsimd.tensor_copy(V[:, :, 0, :], V[:, :, 1, :])
                        nc.gpsimd.tensor_copy(kT[:, :, :, 0:P], kT[:, :, :, P:]).then_inc(shifted, 1)
                    if att:
                        rotate(t, w, 0)
                    if mlp:
                        pool.wait_ge(var_ready, t)
                        nc.gpsimd.tensor_tensor(rstd[:, :], vpe[:, :], mhalf[:, 0:NB], ALU.pow).then_inc(rstd_ready, 1)
                    if att:
                        rotate(t, w, 1)

                layers(pool, turn)

            @block.scalar
            def _(act):
                def squares_and_v(t, b):
                    act.wait_ge(qkv_p, t * NB + b + 1)
                    for i in range(2):
                        ins = nc.scalar.activation(sq[:, i * HEADS:(i + 1) * HEADS, :].rearrange("p h d -> p (h d)"),
                                                   pQKV[i][:, :], ACT.Square)
                    ins.then_inc(sq_ready, 1)
                    act.wait_ge(shifted, t + 1)
                    nc.scalar.activation(V[:, b, 1, :], pQKV[2][:, :], ACT.Copy).then_inc(v_ready, 1)

                def turned(t, b):
                    act.wait_ge(qkT_p, t * NB + b + 1)
                    nc.scalar.activation(qT[:, :, :], pAB[0][:, :, :], ACT.Copy)
                    nc.scalar.activation(kT[:, :, b, P:], pAB[1][:, :, :], ACT.Copy).then_inc(qkT_ready, 1)

                def probabilities(t, b):
                    at = (t * NB + b) * HP

                    def exps(u):
                        act.wait_ge(mx_ready, at + u + 1)
                        for j in range(2):
                            h = 2 * u + j
                            ins = nc.scalar.activation(Pm[:, u % 2, j, :], pS[u % 2][:, j, :], ACT.Exp,
                                                       bias=nmx[:, h:h + 1], accum_out=sums[:, h:h + 1])
                        ins.then_inc(e_ready, 1)

                    def evac(u):
                        act.wait_ge(pT_p, at + u + 1)
                        nc.scalar.activation(PT[:, u % 2, :, :], pAB[u % 2][:, :, :], ACT.Copy).then_inc(pT_ready, 1)

                    exps(0)
                    exps(1)
                    for u in range(HP):
                        evac(u)
                        if u + 2 < HP:
                            exps(u + 2)
                    act.wait_ge(o_p, t * NB + b + 1)
                    nc.scalar.activation(OT[:, :, b, :], pO[:, :, :], ACT.Copy).then_inc(ot_ready, 1)

                def turn(layer, t, w, att, mlp):
                    if att:
                        squares_and_v(t, 0)
                        squares_and_v(t, 1)
                    if mlp:
                        act.wait_ge(hT_p, t)
                        for k in range(KB):
                            ins = nc.scalar.activation(hnT[:, k, :, :], hT_b[:, k, :, :], ACT.Identity,
                                                       bias=lb[:, k:k + 1], scale=lg[:, k:k + 1])
                        ins.then_inc(hnT_ready, 1)
                    if att:
                        turned(t, 0)
                        probabilities(t, 0)
                        turned(t, 1)
                    if mlp:
                        act.wait_ge(u_ready, t * HC)
                        nc.scalar.activation(hu[:, 1, 0:HC - 1, :], hu[:, 1, 0:HC - 1, :], ACT.Gelu)
                        nc.scalar.activation(hu[0:KLAST, 1, HC - 1, :], hu[0:KLAST, 1, HC - 1, :], ACT.Gelu).then_inc(gl_ready, 1)
                    if att:
                        probabilities(t, 1)

                layers(act, turn)

            @block.vector
            def _(dve):
                def turn(layer, t, w, att, mlp):
                    own = Steps(dve, att_step, 12, t)
                    mine = Steps(dve, mlp_step, 3, t - 1)

                    def lengths(b):
                        dve.wait_ge(sq_ready, t * NB + b + 1)
                        own.done(nc.vector.tensor_reduce(ss[:, :], sq[:, :, :], AX_X, ALU.add))
                        nc.vector.tensor_scalar(ssm[:, :], ss[:, :], 1e-24, None, ALU.max).then_inc(ssm_ready, 1)

                    def unit(b):
                        dve.wait_ge(rn_ready, t * NB + b + 1)
                        rnb = rn[:, :].rearrange("p (a h) -> p a h", a=2)
                        for i in range(2):
                            ins = nc.vector.tensor_tensor(qn[:, i, :, :], pQKV[i][:, :].rearrange("p (h d) -> p h d", d=DH),
                                                          rnb[:, i, :].unsqueeze(2).to_broadcast([P, HEADS, DH]), ALU.mult)
                        ins.then_inc(qn_ready, 1)

                    def rotate(b):
                        dve.wait_ge(qn_ready, t * NB + b + 1)
                        if b:
                            dve.wait_ge(qkT_p, t * NB + b)
                        for qk in range(2):
                            cosines = tab[:, ds(w, 1), qk * DH:(qk + 1) * DH]
                            ins = nc.vector.tensor_tensor(r1[:, qk, :, :], qn[:, qk, :, :],
                                                          cosines.to_broadcast([P, HEADS, DH]), ALU.mult)
                        own.done(ins)
                        dve.wait_ge(r2_ready, (t * NB + b + 1) * 4)
                        nc.vector.tensor_tensor(r1[:, :, :, :], r1[:, :, :, :], r2[:, :, :, :], ALU.add).then_inc(qr_ready, 1)

                    def peak(b, u):
                        dve.wait_ge(s_p, (t * NB + b) * HP + u + 1)
                        nc.vector.tensor_reduce(nmx[:, 2 * u:2 * u + 2], pS[u % 2][:, :, :], AX_X, ALU.max,
                                                negate=True).then_inc(mx_ready, 1)

                    def norm(b, u):
                        dve.wait_ge(e_ready, (t * NB + b) * HP + u + 1)
                        own.done(nc.vector.reciprocal(rsum[:, 2 * u:2 * u + 2], sums[:, 2 * u:2 * u + 2]))
                        for j in range(2):
                            h = 2 * u + j
                            ins = nc.vector.tensor_scalar(Pm[:, u % 2, j, :], Pm[:, u % 2, j, :], rsum[:, h:h + 1],
                                                          None, ALU.mult)
                        ins.then_inc(pn_ready, 1)

                    def hidden(c):
                        K = min(P, HID - c * P)
                        dve.wait_ge(u_p, (t - 1) * HC + c + 1)
                        for ag in range(2):
                            ins = nc.vector.tensor_scalar(hu[0:K, ag, c, :], pQKV[c % 3][0:K, ag * NB * P:(ag + 1) * NB * P],
                                                          b1[0:K, ag, c:c + 1], None, ALU.add)
                        ins.then_inc(u_ready, 1)

                    def gated():
                        dve.wait_ge(gl_ready, t)
                        dve.wait_ge(u_ready, t * HC)
                        nc.vector.tensor_tensor(hid[:, 0:HC - 1, :], hu[:, 0, 0:HC - 1, :], hu[:, 1, 0:HC - 1, :], ALU.mult)
                        nc.vector.tensor_tensor(hid[0:KLAST, HC - 1, :], hu[0:KLAST, 0, HC - 1, :], hu[0:KLAST, 1, HC - 1, :],
                                                ALU.mult).then_inc(hid_ready, 1)

                    if not mlp:
                        dve.wait_ge(weights, layer * 16 + 32)
                        nc.vector.memset(xm[:, :, :, HS + P - 1:HS + P], 0.0)
                        nc.vector.tensor_tensor(tab[:, :, :], tab[:, :, :], across(qs, NT), ALU.mult).then_inc(tables, 1)
                        dve.wait_ge(tables, layer + 1)
                    if att:
                        lengths(0)
                    if mlp:
                        mine.done(nc.vector.tensor_copy(xm[:, :, :, HS - 1:HS], xm[:, :, :, HS + P - 1:HS + P]))
                        dve.wait_ge(xm_p, t)
                        for k in range(KB):
                            ins = nc.vector.tensor_tensor(xm[:, k, :, HS:], x_p[:, k, :, :],
                                                          x1T[:, k, :, ds(w * P - P + PAD, P)], ALU.add)
                        ins.then_inc(xm_ready, 1)
                    if att:
                        unit(0)
                    if mlp:
                        dve.wait_ge(h_p, t)
                        for b in range(NB):
                            ins = nc.vector.bn_stats(st6[:, b, :], hn_p[:, b, :])
                        mine.done(ins)
                        dve.nop(nofuse=True)
                        for b in range(NB):
                            ins = nc.vector.bn_aggr(mv[:, b, :], st6[:, b, :])
                        mine.done(ins)
                        nc.vector.tensor_scalar(vpe[:, :], mv[:, :, 1], LN_EPS, None, ALU.add).then_inc(var_ready, 1)
                    if att:
                        rotate(0)
                    if mlp:
                        dve.wait_ge(rstd_ready, t)
                        for b in range(NB):
                            ins = nc.vector.tensor_scalar(hn[:, b, :], hn_p[:, b, :], mv[:, b, 0:1], rstd[:, b:b + 1],
                                                          ALU.subtract, ALU.mult)
                        ins.then_inc(hn_ready, 1)
                        mine.close()
                    if att:
                        lengths(1)
                        unit(1)
                        peak(0, 0)
                        peak(0, 1)
                        rotate(1)
                    for u in range(HP):
                        if mlp and u == 0:
                            hidden(0)
                            hidden(1)
                        if att:
                            norm(0, u)
                            if u + 2 < HP:
                                peak(0, u + 2)
                        if mlp:
                            hidden(u + 2)
                    if att:
                        peak(1, 0)
                        peak(1, 1)
                    if mlp:
                        gated()
                    if att:
                        for u in range(HP):
                            norm(1, u)
                            if u + 2 < HP:
                                peak(1, u + 2)
                        own.close()
                    if mlp:
                        dve.wait_ge(xm_ready, t)
                        dve.wait_ge(y_p, t)
                        for k in range(KB):
                            ins = nc.vector.scalar_tensor_tensor(x1T[:, k, :, ds(w * P - P + PAD, P)], y_b[:, k, :, :],
                                                                 b2[:, k:k + 1], xm[:, k, :, HS:], ALU.add, ALU.add)
                        ins.then_inc(x_stored, 1)

                layers(dve, turn)

            @block.tensor
            def _(pe):
                mm = nc.tensor.matmul

                def turn(layer, t, w, att, mlp):
                    def project(b):
                        for i in range(3):
                            for k in range(KB):
                                ins = mm(pQKV[i][:, :], hs[:, k, b, HS - k:HS - k + P], wqkv[:, k, i * INNER:(i + 1) * INNER],
                                         start=(k == 0), stop=(k == KB - 1))
                        ins.then_inc(qkv_p, 1)

                    def turn_qk(b):
                        pe.wait_ge(qr_ready, t * NB + b + 1)
                        for qk in range(2):
                            for hp in range(HP):
                                ins = nc.tensor.transpose(pAB[qk][:, hp, :],
                                                          r1[:, qk, 2 * hp:2 * hp + 2, :].rearrange("p h d -> p (h d)"),
                                                          ident[:, :])
                        ins.then_inc(qkT_p, 1)

                    def scores(b, u):
                        if u >= 2:
                            pe.wait_ge(e_ready, (t * NB + b) * HP + u - 1)
                        hh = u % 2
                        for j in range(2):
                            hp = u // 2 * 2 + j
                            mm(pS[u % 2][:, j, :], qT[hh * DH:(hh + 1) * DH, hp, :],
                               kT[hh * DH:(hh + 1) * DH, hp, b, :], start=(j == 0), stop=True, skip_group_check=True)
                        mm(pS[u % 2][:, :, :].rearrange("p a n -> p (a n)"), identb[:, :], maskt[:, 1 if mlp else 0, :],
                           start=False, stop=True, skip_group_check=True).then_inc(s_p, 1)

                    def turn_p(b, u):
                        pe.wait_ge(pn_ready, (t * NB + b) * HP + u + 1)
                        for j in range(2):
                            for half in range(2):
                                ins = nc.tensor.transpose(pAB[u % 2][:, 2 * j + half, :],
                                                          Pm[:, u % 2, j, half * P:(half + 1) * P], ident[:, :])
                        ins.then_inc(pT_p, 1)

                    def mix(b, u):
                        pe.wait_ge(pT_ready, (t * NB + b) * HP + u + 1)
                        if b and u == 0:
                            pe.wait_ge(ot_ready, t * NB + 1)
                        hh = u % 2
                        for j in range(2):
                            hp = u // 2 * 2 + j
                            h = 2 * hp + hh
                            for half in range(2):
                                ins = mm(pO[hh * DH:(hh + 1) * DH, hp, :], V[:, b, half, h * DH:(h + 1) * DH],
                                         PT[:, u % 2, 2 * j + half, :], start=(half == 0), stop=(half == 1))
                        if u == HP - 1:
                            ins.then_inc(o_p, 1)

                    def up(c):
                        K = min(P, HID - c * P)
                        if c == 0 and att:
                            pe.wait_ge(qn_ready, (t + 1) * NB)
                            pe.wait_ge(v_ready, (t + 1) * NB)
                        if c >= 3:
                            pe.wait_ge(u_ready, (t - 1) * HC + c - 2)
                        for ag in range(2):
                            for k in range(KB):
                                ins = mm(pQKV[c % 3][0:K, ag * NB * P:(ag + 1) * NB * P], w1[:, k, ag, c * P:c * P + K],
                                         hnT[:, k, :, :], start=(k == 0), stop=(k == KB - 1))
                        ins.then_inc(u_p, 1)

                    def down(f):
                        if f == 0:
                            pe.wait_ge(hid_ready, t)
                        for c in range(HC):
                            K = min(P, HID - c * P)
                            ins = mm(y_b[:, f, :, :], w2[0:K, c, f * P:(f + 1) * P], hid[0:K, c, :],
                                     start=(c == 0), stop=(c == HC - 1))
                        if f == KB - 1:
                            ins.then_inc(y_p, 1)

                    if not mlp:
                        pe.wait_ge(weights, layer * 16 + 32)
                    if att:
                        pe.wait_ge(staged, (t + 1) * KB)
                        if mlp:
                            pe.wait_ge(x_stored, t)
                        project(0)
                    if mlp:
                        pe.wait_ge(ot_ready, t * NB)
                        for f in range(KB):
                            for hp in range(HP):
                                ins = mm(x_p[:, f, :, :], wo[:, hp, f * P:(f + 1) * P], OT[:, hp, :, :],
                                         start=(hp == 0), stop=(hp == HP - 1))
                        ins.then_inc(xm_p, 1)
                    if att:
                        pe.wait_ge(qn_ready, t * NB + 1)
                        pe.wait_ge(v_ready, t * NB + 1)
                        project(1)
                    if mlp:
                        pe.wait_ge(xm_ready, t)
                        for b in range(NB):
                            for k in range(KB):
                                ins = nc.tensor.transpose(hn_p[:, b, k * P:(k + 1) * P], xm[:, k, b, HS - k:HS - k + P], ident[:, :])
                        ins.then_inc(h_p, 1)
                        pe.wait_ge(hn_ready, t)
                        for b in range(NB):
                            for k in range(KB):
                                ins = nc.tensor.transpose(hT_b[:, k, b, :], hn[:, b, k * P:(k + 1) * P], ident[:, :])
                        ins.then_inc(hT_p, 1)
                        pe.wait_ge(hnT_ready, t)
                    if att:
                        turn_qk(0)
                        pe.wait_ge(qkT_ready, t * NB + 1)
                        scores(0, 0)
                        scores(0, 1)
                    for u in range(HP):
                        if mlp and u == 0:
                            up(0)
                            up(1)
                        if att:
                            turn_p(0, u)
                            if u + 2 < HP:
                                scores(0, u + 2)
                            mix(0, u)
                        if mlp:
                            up(u + 2)
                    if att:
                        turn_qk(1)
                        pe.wait_ge(qkT_ready, (t + 1) * NB)
                        scores(1, 0)
                        scores(1, 1)
                    for u in range(HP):
                        if mlp and u % 2 == 0:
                            down(u // 2)
                        if att:
                            turn_p(1, u)
                            if u + 2 < HP:
                                scores(1, u + 2)
                            mix(1, u)

                layers(pe, turn)


def add_norm_stage(nc, io, g):
    xT, x1T, ident, mhalf = g["xT"], g["x1T"], g["ident"], g["mhalf"]
    with ExitStack() as ctx:
        m = Scope(nc, ctx, "an_")
        s = m.sb("s", [P, KB, NB, P])
        st6 = m.sb("st6", [P, NB, 6])
        mv = m.sb("mv", [P, NB, 2])
        vpe = m.sb("vpe", [P, NB])
        rstd = m.sb("rstd", [P, NB])
        yn = m.sb("yn", [P, NB, D])
        pT = m.pb("pT", [P, NB, D])
        pB = m.pb("pB", [P, KB, NB, P])
        sum_ready, t_p, var_ready, rstd_ready, yn_ready, b_p, x_stored, dve_step = map(m.sem, (
            "sum_ready", "t_p", "var_ready", "rstd_ready", "yn_ready", "b_p", "x_stored", "dve_step"))
        with nc.Block() as block:
            @block.gpsimd
            def _(pool):
                nc.gpsimd.memset(vpe[:, :], 1.0).then_inc(x_stored, 1)
                with pool.Fori(0, NT) as n:
                    pool.wait_ge(var_ready, n + 1)
                    nc.gpsimd.tensor_tensor(rstd[:, :], vpe[:, :], mhalf[:, 0:NB], ALU.pow).then_inc(rstd_ready, 1)

            @block.scalar
            def _(act):
                with act.Fori(0, NT) as n:
                    act.wait_ge(b_p, n + 1)
                    for b in range(NB):
                        ins = nc.scalar.activation(xT[:, :, b, ds(n * P + PAD, P)], pB[:, :, b, :], ACT.Copy)
                    ins.then_inc(x_stored, 1)

            @block.vector
            def _(dve):
                with dve.Fori(0, NT) as n:
                    own = Steps(dve, dve_step, 2, n)
                    dve.wait_ge(x_stored, n + 1)
                    for b in range(NB):
                        ins = nc.vector.tensor_tensor(s[:, :, b, :], xT[:, :, b, ds(n * P + PAD, P)],
                                                      x1T[:, :, b, ds(n * P + PAD, P)], ALU.add)
                    ins.then_inc(sum_ready, 1)
                    dve.wait_ge(t_p, n + 1)
                    for b in range(NB):
                        ins = nc.vector.bn_stats(st6[:, b, :], pT[:, b, :])
                    own.done(ins)
                    dve.nop(nofuse=True)
                    for b in range(NB):
                        ins = nc.vector.bn_aggr(mv[:, b, :], st6[:, b, :])
                    own.done(ins)
                    nc.vector.tensor_scalar(vpe[:, :], mv[:, :, 1], LN_EPS, None, ALU.add).then_inc(var_ready, 1)
                    dve.wait_ge(rstd_ready, n + 1)
                    for b in range(NB):
                        ins = nc.vector.tensor_scalar(yn[:, b, :], pT[:, b, :], mv[:, b, 0:1], rstd[:, b:b + 1],
                                                      ALU.subtract, ALU.mult)
                    ins.then_inc(yn_ready, 1)
                    own.close()

            @block.tensor
            def _(pe):
                with pe.Fori(0, NT) as n:
                    pe.wait_ge(sum_ready, n + 1)
                    for b in range(NB):
                        for k in range(KB):
                            ins = nc.tensor.transpose(pT[:, b, k * P:(k + 1) * P], s[:, k, b, :], ident[:, :])
                    ins.then_inc(t_p, 1)
                    pe.wait_ge(yn_ready, n + 1)
                    for b in range(NB):
                        for k in range(KB):
                            ins = nc.tensor.transpose(pB[:, k, b, :], yn[:, b, k * P:(k + 1) * P], ident[:, :])
                    ins.then_inc(b_p, 1)


RH = 16
RD = D // RH
SCALE = 1.0 / np.sqrt(np.float32(RD))
DIAG = P + 2
TERMS_L = (0, 0, 0, 1, 1, 1, 2, 2)
TERMS_R = (0, 1, 2, 0, 1, 2, 0, 1)
E0 = T - P


def angle_tables():
    f = (1.0 / 10000.0 ** (np.arange(0, D, 2, dtype=np.float32) / D)).astype(np.float32).astype(np.float64)
    off = np.arange(-E0, T)
    e = np.stack([np.sin(off[None, :] * f[:, None]), np.cos(off[None, :] * f[:, None])], 1)
    i = np.arange(P)
    lo, up = (T - 1 - i)[None, :] * f[:, None], (-(T + 1) - i)[None, :] * f[:, None]
    rot = np.stack([np.stack([np.stack([np.cos(x)] * 2, 1), np.stack([np.sin(x)] * 2, 1)], 1) for x in (lo, up)], 1)
    return e.astype(np.float32), rot.astype(np.float32)


def diagonal_masks():
    i, d = np.arange(P)[:, None], np.arange(DIAG)[None, :]
    return np.stack([d <= i, d >= i + 2], 1).astype(np.float32)


def keep_x(nc, io, g, scratch, back):
    with nc.semaphore("x_kept_back" if back else "x_kept") as kept, nc.Block() as block:
        @block.sync
        def _(sp):
            for k in range(KB):
                here, there = g["xT"][:, k, :, PAD:], scratch["x"][:, k, :, :]
                sp.dma_start(*((here, there) if back else (there, here))).then_inc(kept, 16)
            sp.wait_ge(kept, 16 * KB)


def project_stage(nc, io, g, scratch, Vall):
    xT, ident = g["xT"], g["ident"]
    CH = 512
    NCH = T // CH
    with ExitStack() as ctx:
        m = Scope(nc, ctx, "pr_")
        wq, wk, wv = (m.sb(n, [P, KB, D]) for n in ("wq", "wk", "wv"))
        uv = m.sb("uv", [P, 2, KB])
        wr = m.sb("wr", [P, KB, D])
        full = m.sb("full", [P, 3, CH])
        parts = m.sb("parts", [P, 3, 3, CH], BF16)
        rest = m.sb("rest", [P, 3, CH])
        wrp = m.sb("wrp", [P, 3, KB, D], BF16)
        wrr = m.sb("wrr", [P, KB, D])
        xs = m.sb("xs", [P, KB, P])
        pq, pk = m.pb("pq", [P, CH]), m.pb("pk", [P, CH])
        pv = m.pb("pv", [P, D])
        loaded, wr_step, wr_out, qk_p, full_ready, dve_step, parts_ready, stored, staged, v_p, v_ready = map(m.sem, (
            "loaded", "wr_step", "wr_out", "qk_p", "full_ready", "dve_step", "parts_ready", "stored", "staged",
            "v_p", "v_ready"))
        LOADS = 16 * 5

        with nc.Block() as block:
            @block.sync
            def _(sp):
                for dst, src in ((wq, "rl_wq"), (wk, "rl_wk"), (wv, "rl_wv"), (wr, "rl_wr"), (uv, "rl_uv")):
                    sp.dma_start(dst[:, :, :], io[src]).then_inc(loaded, 16)
                sp.wait_ge(wr_step, 5)
                for p in range(3):
                    for k in range(KB):
                        for b in range(NB):
                            last = (p, k, b) == (2, KB - 1, NB - 1)
                            at = b * D + k * P
                            sp.dma_start(scratch["wr"][p, at:at + P, :],
                                         wrp[:, p, k, :]).then_inc(stored if last else wr_out, 16)
                sp.wait_ge(wr_out, 16 * (3 * KB * NB - 1))
                for mb in range(KB):
                    for b in range(NB):
                        with sp.Fori(0, NCH) as c:
                            turn = (mb * NB + b) * NCH + c
                            sp.wait_ge(parts_ready, turn + 2)
                            for a in range(3):
                                at = b * D + mb * P
                                to = scratch["quk"][a, :, at:at + P, ds(c * CH, CH)]
                                sp.dma_start(to.rearrange("p f t -> f p t"), parts[:, a, :, :]).then_inc(stored, 16)
                sp.wait_ge(stored, 16 * (3 * KB * NB * NCH + 1))

            @block.gpsimd
            def _(pool):
                nc.gpsimd.memset(xs[:, :, :], 0.0).then_inc(v_ready, 1)
                nc.gpsimd.memset(full[:, 0, :], 0.0).then_inc(full_ready, 1)
                nc.gpsimd.memset(full[:, 1, :], 0.0).then_inc(parts_ready, 1)
                for b in range(NB):
                    with pool.Fori(0, NT) as n:
                        pool.wait_ge(v_ready, n + b * NT + 1)
                        pool.nop(nofuse=True)
                        nc.gpsimd.tensor_copy(xs[:, :, :], xT[:, :, b, ds(n * P + PAD, P)]).then_inc(staged, 1)

            @block.scalar
            def _(act):
                act.wait_ge(loaded, LOADS)
                for mb in range(KB):
                    for b in range(NB):
                        with act.Fori(0, NCH) as c:
                            turn = (mb * NB + b) * NCH + c
                            act.wait_ge(qk_p, turn + 1)
                            act.wait_ge(parts_ready, turn + 1)
                            for a in range(2):
                                nc.scalar.activation(full[:, a, :], pq[:, :], ACT.Identity, bias=uv[:, a, mb:mb + 1])
                            nc.scalar.activation(full[:, 2, :], pk[:, :], ACT.Copy).then_inc(full_ready, 1)
                for b in range(NB):
                    with act.Fori(0, NT) as n:
                        act.wait_ge(v_p, n + b * NT + 1)
                        nc.scalar.activation(Vall[:, ds(n, 1), b * D:(b + 1) * D], pv[:, :].unsqueeze(1), ACT.Copy).then_inc(v_ready, 1)

            @block.vector
            def _(dve):
                def split(x, r, part, step):
                    for p in range(3):
                        src = x if p == 0 else r
                        ins = nc.vector.tensor_copy(part(p), src)
                        if p < 2:
                            step(ins)
                            step(nc.vector.tensor_tensor(r, src, part(p), ALU.subtract))
                    return ins

                dve.wait_ge(loaded, LOADS)
                own = Steps(dve, wr_step)
                split(wr[:, :, :], wrr[:, :, :], lambda p: wrp[:, p, :, :], own.done).then_inc(wr_step, 1)
                for mb in range(KB):
                    for b in range(NB):
                        with dve.Fori(0, NCH) as c:
                            turn = (mb * NB + b) * NCH + c
                            own = Steps(dve, dve_step, 4, turn)
                            dve.wait_ge(full_ready, turn + 2)
                            dve.wait_ge(stored, turn * 48 + 16)
                            split(full[:, :, :], rest[:, :, :], lambda p: parts[:, :, p, :], own.done).then_inc(parts_ready, 1)
                            own.close()

            @block.tensor
            def _(pe):
                mm = nc.tensor.matmul
                pe.wait_ge(loaded, LOADS)
                for mb in range(KB):
                    for b in range(NB):
                        with pe.Fori(0, NCH) as c:
                            turn = (mb * NB + b) * NCH + c
                            pe.wait_ge(full_ready, turn + 1)
                            for w, p in ((wq, pq), (wk, pk)):
                                for k in range(KB):
                                    ins = mm(p[:, :], w[:, k, mb * P:(mb + 1) * P], xT[:, k, b, ds(c * CH + PAD, CH)],
                                             start=(k == 0), stop=(k == KB - 1))
                            ins.then_inc(qk_p, 1)
                for b in range(NB):
                    with pe.Fori(0, NT) as n:
                        pe.wait_ge(staged, n + b * NT + 1)
                        for k in range(KB):
                            ins = mm(pv[:, :], xs[:, k, :], wv[:, k, :], start=(k == 0), stop=(k == KB - 1))
                        ins.then_inc(v_p, 1)


def relative_stage(nc, io, g, scratch, Vall, At):
    ident = g["ident"]
    NI = NT
    HEADS_ALL = NB * RH
    CH = 512
    NCH = T // CH
    RING = 4
    ROWS = 4
    ANGLES_AT = (6, 10, 14, 18)
    with ExitStack() as ctx:
        m = Scope(nc, ctx, "rl_")
        E = m.sb("E", [P, KB, E0 + T])
        rot = m.sb("rot", [P, 2, 2, KB, P])
        dmask = m.sb("dmask", [P, 2, DIAG])
        sel = m.sb("sel", [P, RD])
        qu, kk = (m.sb(n, [P, 2 * T], BF16) for n in ("qu", "kk"))
        qv = m.sb("qv", [P, T], BF16)
        wrp = m.sb("wrp", [P, KB, P], BF16)
        ab = m.sb("ab", [P, KB, T + 4])
        m1, m2 = (m.sb(n, [P, 2, KB, P]) for n in ("m1", "m2"))
        co = m.sb("co", [P, RING, 4, P])
        row = g["xT"][:, :, :, :].rearrange("p k b t -> p (k b t)")[:, 0:ROWS * T].rearrange("p (r t) -> p r t", t=T)
        t12 = m.sb("t12", [P, 2, DIAG])
        td = m.sb("td", [P, DIAG])
        nmx = m.sb("nmx", [P, NI])
        nms = m.sb("nms", [P, NI])
        sums = m.sb("sums", [P, NI])
        rsum = m.sb("rsum", [P, NI])
        PT = m.sb("PT", [P, 2, 4, P])
        vst = m.sb("vst", [P, NT, 32])
        O4 = m.sb("O4", [P, P])

        pS = [m.pb(f"pS{n}", [P, CH]) for n in range(2)]
        pD = m.pb("pD", [P, 2, 256])
        pT = [m.pb(f"pT{n}", [P, 4, P]) for n in range(2)]
        pO = m.pb("pO", [P, 512])
        pM = [m.pb(f"pM{n}", [P, CH]) for n in range(2)]

        (loaded, vst_ready, ab_p, ab_ready, co_ready, co_step, dg_p, diag_done, s_p, row_ready,
         mx_ready, e_ready, pT_p, pt_ready, o_p, o4_ready, r_p, an_ready, dve_step) = map(m.sem, (
             "loaded", "vst_ready", "ab_p", "ab_ready", "co_ready", "co_step", "dg_p",
             "diag_done", "s_p", "row_ready", "mx_ready", "e_ready", "pT_p", "pt_ready", "o_p", "o4_ready", "r_p",
             "an_ready", "dve_step"))
        packed = [m.sem(f"packed{a}") for a in range(3)]
        rsum_ready = m.sem("rsum_ready")

        with nc.Block() as block:
            @block.sync
            def _(sp):
                for dst, src in ((E[:, :, :], "rl_E"), (dmask[:, :, :], "rl_dmask"), (sel[:, :], "rl_sel"),
                                 (rot[:, :, :, :, :].rearrange("p u c k i -> p (u c k i)"), "rl_rot")):
                    sp.dma_start(dst, io[src]).then_inc(loaded, 16)
                sp.wait_ge(loaded, 16 * 4)

            @block.gpsimd
            def _(pool):
                for s, k in ((o_p, 1), (s_p, RING * NCH), (row_ready, 2), (pt_ready, 2), (pT_p, ROWS * NCH),
                             (diag_done, 1), (o4_ready, 1), (an_ready, 1), (co_ready, 1)):
                    pool.sem_inc(s, k)
                nc.gpsimd.memset(ab[:, :, T:], 0.0)
                nc.gpsimd.memset(vst[:, :, :], 0.0)

        LAST = HEADS_ALL - 1

        def row_of(s):
            return row[:, s % ROWS, :]

        def heads(eng, step):
            for s in range(3):
                step(0, s, True, False)
            with eng.Fori(0, LAST) as n:
                for s in range(3, NI + 3):
                    step(n, s, False, False)
            for s in range(3, NI + 3):
                step(LAST, s, False, True)

        with nc.Block() as block:
            @block.sync
            def _(sp):
                def gather(n, arrays):
                    for a, dst, terms in arrays:
                        for i, part in enumerate(terms):
                            at = dst if a == 1 else dst[:, ds(n % 2 * T, T)]
                            sp.dma_start(at[i * RD:(i + 1) * RD, :],
                                         scratch["quk"][a, part, ds(n * RD, RD), :]).then_inc(packed[a], 16)

                def gather_q(n):
                    gather(n, ((1, qv, TERMS_R),))
                    for i, part in enumerate(TERMS_L):
                        sp.dma_start(wrp[i * RD:(i + 1) * RD, :, :].rearrange("p k f -> p (k f)"),
                                     scratch["wr"][part, ds(n * RD, RD), :]).then_inc(packed[1], 16)

                def gather_k(n):
                    gather(n, ((0, qu, TERMS_L), (2, kk, TERMS_R)))

                gather_q(0)
                gather_k(0)
                with sp.Fori(0, LAST) as n:
                    sp.wait_ge(ab_p, (n + 1) * NCH)
                    gather_q(n + 1)
                    sp.wait_ge(s_p, n * NI * NCH + RING * NCH + 1)
                    gather_k(n + 1)

            @block.gpsimd
            def _(pool):
                def blocks(n, first, last):
                    for I in range(first, last):
                        pool.wait_ge(ab_ready, n * NCH + min(NCH - 1, (I + 1) * P // CH) + 1)
                        pool.wait_ge(s_p, (n * NI + I + 1) * NCH)
                        pool.wait_ge(co_ready, n * NI + I + 1)
                        pool.nop(nofuse=True)
                        for u in range(2):
                            x = ab[:, :, I * P + u:I * P + u + P]
                            nc.gpsimd.tensor_tensor(m1[:, u, :, :], x, rot[:, u, 0, :, :], ALU.mult)
                            ins = nc.gpsimd.tensor_tensor(m2[:, u, :, :], x, rot[:, u, 1, :, :], ALU.mult)
                        ins.then_inc(co_step, 1)
                        pool.wait_ge(co_step, n * NI + I + 1)
                        to = co[:, I % RING, :, :].rearrange("p (u k) i -> p u k i", u=2)
                        nc.gpsimd.tensor_tensor(to[:, :, 0, :], m1[:, :, 0, :], m2[:, :, 1, :], ALU.subtract)
                        nc.gpsimd.tensor_tensor(to[:, :, 1, :], m1[:, :, 1, :], m2[:, :, 0, :], ALU.add).then_inc(co_ready, 1)

                with pool.Fori(0, HEADS_ALL) as n:
                    blocks(n, 0, 3)
                    pool.wait_ge(o_p, n * NI + 1)
                    pool.nop(nofuse=True)
                    nc.gpsimd.tensor_copy(vst[:, :, 0:RD], Vall[:, :, ds(n * RD, RD)]).then_inc(vst_ready, 1)
                    blocks(n, 3, NI)

            @block.scalar
            def _(act):
                def angles(n, c):
                    act.wait_ge(ab_p, n * NCH + c + 1)
                    for k in range(KB):
                        ins = nc.scalar.activation(ab[:, k, c * CH:(c + 1) * CH], pM[k][:, :], ACT.Copy)
                    ins.then_inc(ab_ready, 1)

                def attention_out(n, J):
                    act.wait_ge(o_p, n * NI + J + 2)
                    nc.scalar.activation(O4[:, :], pO[:, 0:P], ACT.Copy).then_inc(o4_ready, 1)

                def evac(n, J, c):
                    act.wait_ge(pT_p, (n * NI + J) * NCH + c + 1 + NCH * ROWS)
                    nc.scalar.activation(PT[:, c % 2, :, :], pT[c % 2][:, :, :], ACT.Copy).then_inc(pt_ready, 1)

                def softmax(n, I):
                    act.wait_ge(mx_ready, n * NI + I + 1)
                    r = row_of(I)
                    nc.scalar.activation(r, r, ACT.Exp, bias=nms[:, I % NI:I % NI + 1], scale=float(SCALE),
                                         accum_out=sums[:, I % NI:I % NI + 1]).then_inc(e_ready, 1)

                for c in range(NCH):
                    angles(0, c)

                def step(n, s, first, last):
                    if s >= 3:
                        attention_out(n, s - 3)
                        if not last and s in ANGLES_AT:
                            c = ANGLES_AT.index(s)
                            act.wait_ge(co_ready, n * NI + min(NI, (c + 1) * CH // P) + 1)
                            angles(n + 1, c)
                    for c in range(NCH):
                        if 0 <= s - 2 and (s - 2 < NI or not last):
                            evac(n, s - 2, c)
                        if c == 1 and 0 <= s - 1 and (s - 1 < NI or not last):
                            softmax(n, s - 1)

                heads(act, step)

            @block.vector
            def _(dve):
                def scores(n, s):
                    I = s % NI
                    g = n * NI + s
                    own = Steps(dve, dve_step, 3, g)
                    dve.wait_ge(dg_p, g + 1)
                    for u in range(2):
                        ins = nc.vector.tensor_tensor(t12[:, u, :], pD[:, u, 0:DIAG], dmask[:, u, :], ALU.mult)
                    own.done(ins)
                    nc.vector.tensor_tensor(td[:, :], t12[:, 0, :], t12[:, 1, :], ALU.add).then_inc(diag_done, 1)
                    dve.wait_ge(diag_done, g + 2)
                    dve.wait_ge(pT_p, g * NCH + NCH)
                    for c in range(NCH):
                        dve.wait_ge(s_p, g * NCH + c + 1 + RING * NCH)
                        nc.vector.tensor_copy(row_of(s)[:, c * CH:(c + 1) * CH], pS[c % 2][:, :]).then_inc(row_ready, 1)
                    dve.wait_ge(row_ready, (g + 1) * NCH + 2)
                    W = min(DIAG, T - I * P)
                    at = row_of(s)[:, I * P:I * P + W]
                    own.done(nc.vector.tensor_tensor(at, at, td[:, 0:W], ALU.add))
                    own.done(nc.vector.tensor_reduce(nmx[:, I:I + 1], row_of(s), AX_X, ALU.max, negate=True))
                    nc.vector.tensor_scalar(nms[:, I:I + 1], nmx[:, I:I + 1], float(SCALE), None,
                                            ALU.mult).then_inc(mx_ready, 1)
                    own.close()

                def attention_out(n, J):
                    g = n * NI + J
                    dve.wait_ge(e_ready, g + 1)
                    nc.vector.reciprocal(rsum[:, J:J + 1], sums[:, J:J + 1]).then_inc(rsum_ready, 1)
                    dve.wait_ge(rsum_ready, g + 1)
                    dve.wait_ge(r_p, g + 1)
                    nc.vector.tensor_scalar(At[:, J, ds(n * RD, RD)], pM[0][:, 0:RD], rsum[:, J:J + 1], None,
                                            ALU.mult).then_inc(an_ready, 1)

                def step(n, s, first, last):
                    if s < NI or not last:
                        scores(n, s)
                    if s >= 3:
                        attention_out(n, s - 3)

                heads(dve, step)

            @block.tensor
            def _(pe):
                mm = nc.tensor.matmul

                def angles(n, c):
                    if c == 0:
                        pe.wait_ge(packed[1], (n + 1) * 16 * 2 * len(TERMS_L))
                    for k in range(KB):
                        ins = mm(pM[k][:, :], wrp[:, k, :], qv[:, c * CH:(c + 1) * CH], start=True, stop=True)
                    ins.then_inc(ab_p, 1)

                def diagonal(n, s):
                    g = n * NI + s
                    pe.wait_ge(co_ready, g + 2)
                    pe.wait_ge(diag_done, g + 1)
                    for u in range(2):
                        for k in range(KB):
                            ins = mm(pD[:, u, 0:DIAG], co[:, s % RING, 2 * u + k, :], E[:, k, E0:E0 + DIAG],
                                     start=(k == 0), stop=(k == KB - 1))
                    ins.then_inc(dg_p, 1)

                def scores(n, s, c):
                    p, I, head = pS[c % 2], s % NI, n + s // NI
                    pe.wait_ge(row_ready, (n * NI + s) * NCH + c + 1)
                    lo_end = min((c + 1) * CH, I * P)
                    up_at = max(c * CH, I * P + DIAG)
                    spans = []
                    if lo_end > c * CH:
                        spans.append((0, c * CH, lo_end))
                    if up_at < (c + 1) * CH:
                        spans.append((1, up_at, (c + 1) * CH))
                    ins = mm(p[:, :], qu[:, ds(head % 2 * T + I * P, P)], kk[:, ds(head % 2 * T + c * CH, CH)],
                             start=True, stop=True, skip_group_check=True)
                    for u, j0, j1 in spans:
                        for k in range(KB):
                            e0 = j0 - I * P + E0
                            ins = mm(p[:, j0 - c * CH:j1 - c * CH], co[:, I % RING, 2 * u + k, :], E[:, k, e0:e0 + j1 - j0],
                                     start=False, stop=True, skip_group_check=True)
                    ins.then_inc(s_p, 1)

                def turn(n, s, c):
                    g = n * NI + s
                    if c == 0:
                        pe.wait_ge(e_ready, g + 1)
                    pe.wait_ge(pt_ready, g * NCH + c + 1)
                    for j in range(4):
                        at = (4 * c + j) * P
                        ins = nc.tensor.transpose(pT[c % 2][:, j, :], row_of(s)[:, at:at + P], ident[:, :])
                    ins.then_inc(pT_p, 1)

                def mix(n, s, c):
                    g = n * NI + s
                    pe.wait_ge(pt_ready, g * NCH + c + 3)
                    if c == 0:
                        pe.wait_ge(o4_ready, g + 1)
                        pe.wait_ge(vst_ready, n + s // NI + 1)
                    for j in range(4):
                        ins = mm(pO[32 * j:32 * j + 32, 0:P], vst[:, 4 * c + j, :], PT[:, c % 2, j, :],
                                 start=(c == 0), stop=(c == NCH - 1))
                    if c == NCH - 1:
                        ins.then_inc(o_p, 1)

                def add_groups(n, J):
                    g = n * NI + J
                    pe.wait_ge(o4_ready, g + 2)
                    pe.wait_ge(an_ready, g + 1)
                    mm(pM[0][:, 0:RD], O4[:, :], sel[:, :], start=True, stop=True).then_inc(r_p, 1)

                for c in range(NCH):
                    if c:
                        pe.wait_ge(ab_ready, c)
                    angles(0, c)

                def step(n, s, first, last):
                    if s >= 3 and not last and s in ANGLES_AT:
                        pe.wait_ge(an_ready, n * NI + s - 3 + 1)
                        if ANGLES_AT.index(s):
                            pe.wait_ge(ab_ready, (n + 1) * NCH + ANGLES_AT.index(s))
                        angles(n + 1, ANGLES_AT.index(s))
                    more = s < NI or not last
                    if more:
                        if s in (0, NI):
                            pe.wait_ge(packed[0], (n + s // NI + 1) * 16 * len(TERMS_L))
                            pe.wait_ge(packed[2], (n + s // NI + 1) * 16 * len(TERMS_L))
                        diagonal(n, s)
                    used = 0 <= s - 2 and (s - 2 < NI or not last)
                    for c in range(NCH):
                        if more:
                            scores(n, s, c)
                        if used:
                            turn(n, s - 2, c)
                            if c:
                                mix(n, s - 2, c - 1)
                        if c == 1 and s >= 3:
                            if s in ANGLES_AT and not last:
                                pe.wait_ge(ab_ready, (n + 1) * NCH + ANGLES_AT.index(s) + 1)
                            add_groups(n, s - 3)
                    if used:
                        mix(n, s - 2, NCH - 1)

                heads(pe, step)


TOKENS = 1024
ME = 8
FF = 1024
TOPK = 2


def moe_stage(nc, io, g, Acc):
    xT = g["xT"]
    NTT, FC, HALF = TOKENS // P, FF // P, 512
    with ExitStack() as ctx:
        m = Scope(nc, ctx, "me_")
        w1 = [m.sb(f"w1_{j}", [P, KB, FF]) for j in range(2)]
        w2 = [m.sb(f"w2_{j}", [P, FC, D]) for j in range(2)]
        hT = m.sb("hT", [P, FC, TOKENS])
        bias = m.sb("bias", [P, D])
        idx = m.sb("idx", [P, NTT, TOPK], I32)
        idxf = m.sb("idxf", [P, NTT, TOPK])
        ew = m.sb("ew", [P, NTT, TOPK])
        erow = m.sb("erow", [P, ME])
        hit = m.sb("hit", [P, TOPK, NTT, ME])
        cw = m.sb("cw", [P, NTT, ME])
        pH = [m.pb(f"pH{i}", [P, HALF]) for i in range(4)]
        pY = [m.pb(f"pY{i}", [P, 2, D]) for i in range(2)]
        w_in = [m.sem(f"w_in{j}") for j in range(2)]
        loaded, h_p, h_ready, y_p, acc_ready, dve_step = map(m.sem, (
            "loaded", "h_p", "h_ready", "y_p", "acc_ready", "dve_step"))

        with nc.Block() as block:
            @block.sync
            def _(sp):
                for dst, src in ((bias[:, :], "me_bias"), (idx[:, :, :], "me_idx"), (ew[:, :, :], "me_w"),
                                 (erow[:, :], "me_erow")):
                    sp.dma_start(dst, io[src]).then_inc(loaded, 16)
                sp.wait_ge(loaded, 64)

            @block.gpsimd
            def _(pool):
                for s, k in ((y_p, 2 * NTT // 2), (acc_ready, 2), (h_ready, 4)):
                    pool.sem_inc(s, k)

            @block.vector
            def _(dve):
                own = Steps(dve, dve_step)
                dve.wait_ge(loaded, 64)
                nc.vector.tensor_copy(Acc[:, :, :].rearrange("p n (b d) -> p (n b) d", b=NB), across(bias[:, :], NB * NT))
                own.done(nc.vector.tensor_copy(idxf[:, :, :], idx[:, :, :]))
                for k in range(TOPK):
                    ins = nc.vector.tensor_tensor(hit[:, k, :, :], idxf[:, :, k:k + 1].to_broadcast([P, NTT, ME]),
                                                  across(erow[:, :], NTT), ALU.is_equal)
                own.done(ins)
                for k in range(TOPK):
                    ins = nc.vector.tensor_tensor(hit[:, k, :, :], hit[:, k, :, :],
                                                  ew[:, :, k:k + 1].to_broadcast([P, NTT, ME]), ALU.mult)
                own.done(ins)
                nc.vector.tensor_tensor(cw[:, :, :], hit[:, 0, :, :], hit[:, 1, :, :], ALU.add)

        def experts(eng, expert):
            with eng.Fori(0, ME // 2) as pair:
                for j in range(2):
                    expert(pair, pair * 2 + j, j)

        with nc.Block() as block:
            @block.sync
            def _(sp):
                def expert(pair, e, j):
                    sp.wait_ge(y_p, (e + 1) * (NTT // 2))
                    sp.dma_start(w1[j][:, :, :], io["me_w1"][ds(e, 1), :, :, :].rearrange("e p k f -> (e p) k f")).then_inc(w_in[j], 16)
                    sp.dma_start(w2[j][:, :, :], io["me_w2"][ds(e, 1), :, :, :].rearrange("e p k f -> (e p) k f")).then_inc(w_in[j], 16)

                experts(sp, expert)

            @block.scalar
            def _(act):
                def expert(pair, e, j):
                    for f in range(FC):
                        for half in range(2):
                            i = (2 * f + half) % 4
                            act.wait_ge(h_p, e * 2 * FC + 2 * f + half + 1)
                            nc.scalar.activation(hT[:, f, half * HALF:(half + 1) * HALF], pH[i][:, :],
                                                 ACT.Gelu).then_inc(h_ready, 1)

                experts(act, expert)

            @block.vector
            def _(dve):
                def expert(pair, e, j):
                    for t in range(NTT):
                        if t % 2 == 0:
                            dve.wait_ge(y_p, e * (NTT // 2) + t // 2 + 1 + NTT)
                            dve.wait_ge(acc_ready, e * (NTT // 2) + t // 2 + 1)
                        ins = nc.vector.scalar_tensor_tensor(Acc[:, t, 0:D], pY[t // 2 % 2][:, t % 2, :],
                                                             cw[:, t, ds(e, 1)], Acc[:, t, 0:D], ALU.mult, ALU.add)
                        if t % 2:
                            ins.then_inc(acc_ready, 1)

                experts(dve, expert)

            @block.tensor
            def _(pe):
                mm = nc.tensor.matmul

                def expert(pair, e, j):
                    pe.wait_ge(w_in[j], (pair + 1) * 32)
                    for f in range(FC):
                        for half in range(2):
                            i = (2 * f + half) % 4
                            pe.wait_ge(h_ready, e * 2 * FC + 2 * f + half + 1)
                            for k in range(KB):
                                at = PAD + half * HALF
                                ins = mm(pH[i][:, :], w1[j][:, k, f * P:(f + 1) * P], xT[:, k, 0, at:at + HALF],
                                         start=(k == 0), stop=(k == KB - 1))
                            ins.then_inc(h_p, 1)
                    pe.wait_ge(h_ready, (e + 1) * 2 * FC + 4)
                    for t in range(NTT):
                        if t % 2 == 0:
                            pe.wait_ge(acc_ready, e * (NTT // 2) + t // 2 + 1)
                        for f in range(FC):
                            ins = mm(pY[t // 2 % 2][:, t % 2, :], hT[:, f, t * P:(t + 1) * P], w2[j][:, f, :],
                                     start=(f == 0), stop=(f == FC - 1))
                        if t % 2:
                            ins.then_inc(y_p, 1)

                experts(pe, expert)


def rows_norm_stage(nc, io, g, name, rows, out=None):
    xT, ident, mhalf = g["xT"], g["ident"], g["mhalf"]
    with ExitStack() as ctx:
        m = Scope(nc, ctx, name)
        xs = m.sb("xs", [P, KB, NB, P])
        y = m.sb("y", [P, NB, D])
        st6 = m.sb("st6", [P, NB, 6])
        mv = m.sb("mv", [P, NB, 2])
        vpe = m.sb("vpe", [P, NB])
        rstd = m.sb("rstd", [P, NB])
        yn = m.sb("yn", [P, NB, D])
        pT = m.pb("pT", [P, NB, D])
        pB = m.pb("pB", [P, KB, NB, P])
        staged, t_p, var_ready, rstd_ready, yn_ready, b_p, x_stored, dve_step, sum_ready = map(m.sem, (
            "staged", "t_p", "var_ready", "rstd_ready", "yn_ready", "b_p", "x_stored", "dve_step", "sum_ready"))
        with nc.Block() as block:
            if out is None:
                @block.scalar
                def _(act):
                    with act.Fori(0, NT) as n:
                        act.wait_ge(b_p, n + 1)
                        for b in range(NB):
                            nc.scalar.activation(xT[:, :, b, ds(n * P + PAD, P)], pB[:, :, b, :], ACT.Copy).then_inc(x_stored, 8)
            else:
                @block.sync
                def _(sp):
                    with sp.Fori(0, NT) as n:
                        sp.wait_ge(yn_ready, n + 1)
                        sp.dma_start(out[:, ds(n * P, P), :].rearrange("b p d -> p b d"), yn[:, :, :]).then_inc(x_stored, 16)
                    sp.wait_ge(x_stored, 16 * NT)

            @block.gpsimd
            def _(pool):
                pool.sem_inc(t_p, 1)
                with pool.Fori(0, NT) as n:
                    pool.wait_ge(t_p, n + 1)
                    pool.nop(nofuse=True)
                    for b in range(NB):
                        nc.gpsimd.tensor_copy(xs[:, :, b, :], xT[:, :, b, ds(n * P + PAD, P)]).then_inc(staged, 1)
                    pool.wait_ge(var_ready, n + 1)
                    nc.gpsimd.tensor_tensor(rstd[:, :], vpe[:, :], mhalf[:, 0:NB], ALU.pow).then_inc(rstd_ready, 1)

            @block.vector
            def _(dve):
                def turn(n, first):
                    own = Steps(dve, dve_step, 2, n)
                    dve.wait_ge(t_p, n + 2)
                    if not first:
                        dve.wait_ge(yn_ready, n)
                    for b in range(NB):
                        ins = nc.vector.tensor_tensor(y[:, b, :].unsqueeze(1), pT[:, b, :].unsqueeze(1),
                                                      rows[:, ds(n, 1), b * D:(b + 1) * D], ALU.add)
                    ins.then_inc(sum_ready, 1)
                    dve.wait_ge(sum_ready, n + 1)
                    for b in range(NB):
                        ins = nc.vector.bn_stats(st6[:, b, :], y[:, b, :])
                    own.done(ins)
                    dve.nop(nofuse=True)
                    for b in range(NB):
                        ins = nc.vector.bn_aggr(mv[:, b, :], st6[:, b, :])
                    own.done(ins)
                    nc.vector.tensor_scalar(vpe[:, :], mv[:, :, 1], LN_EPS, None, ALU.add).then_inc(var_ready, 1)
                    dve.wait_ge(rstd_ready, n + 1)
                    if not first:
                        dve.wait_ge(x_stored, n * 16)
                    for b in range(NB):
                        ins = nc.vector.tensor_scalar(yn[:, b, :], y[:, b, :], mv[:, b, 0:1], rstd[:, b:b + 1],
                                                      ALU.subtract, ALU.mult)
                    ins.then_inc(yn_ready, 1)
                    own.close()

                turn(0, True)
                with dve.Fori(1, NT) as n:
                    turn(n, False)

            @block.tensor
            def _(pe):
                def turn(n, first):
                    pe.wait_ge(staged, (n + 1) * NB)
                    if not first:
                        pe.wait_ge(sum_ready, n)
                    for b in range(NB):
                        for k in range(KB):
                            ins = nc.tensor.transpose(pT[:, b, k * P:(k + 1) * P], xs[:, k, b, :], ident[:, :])
                    ins.then_inc(t_p, 1)
                    if out is None:
                        pe.wait_ge(yn_ready, n + 1)
                        for b in range(NB):
                            for k in range(KB):
                                ins = nc.tensor.transpose(pB[:, k, b, :], yn[:, b, k * P:(k + 1) * P], ident[:, :])
                        ins.then_inc(b_p, 1)

                turn(0, True)
                with pe.Fori(1, NT) as n:
                    turn(n, False)


def store_stage(nc, io, g):
    xT = g["xT"]
    with nc.semaphore("st_out") as out, nc.Block() as block:
        @block.sync
        def _(sp):
            for k in range(KB):
                sp.dma_start(io["outT"][:, k, :, :], xT[:, k, :, PAD:]).then_inc(out, 16)
            sp.wait_ge(out, 16 * KB)


STAGES = 4


def program(nc, io):
    with ExitStack() as ctx:
        m = Scope(nc, ctx, "g_")
        g = dict(x1T=m.sb("x1T", [P, KB, NB, PAD + T]), xT=m.sb("xT", [P, KB, NB, PAD + T]), ident=m.sb("ident", [P, P]), ones=m.sb("ones", [P, P]),
                 mhalf=m.sb("mhalf", [P, 16]))
        delta_rule_stage(nc, io, g)
        if STAGES > 1:
            local_stage(nc, io, g)
            add_norm_stage(nc, io, g)
        if STAGES > 2:
            rows = g["x1T"][:, :, :, :].rearrange("p k b t -> p (k b t)")[:, 0:NB * NT * D].rearrange("p (n d) -> p n d", d=NB * D)
            scratch = {"x": nc.dram_tensor("x_kept", (P, KB, NB, T), F32).ap(),
                       "quk": nc.dram_tensor("quk_parts", (3, 3, NB * D, T), BF16).ap(),
                       "wr": nc.dram_tensor("wr_parts", (3, NB * D, D), BF16).ap()}
            with nc.sbuf_tensor("v_rows", [P, NT, NB * D], F32) as Vall:
                project_stage(nc, io, g, scratch, Vall)
                keep_x(nc, io, g, scratch, False)
                relative_stage(nc, io, g, scratch, Vall, rows)
                keep_x(nc, io, g, scratch, True)
            rows_norm_stage(nc, io, g, "rn_", rows)
        if STAGES > 3:
            moe_stage(nc, io, g, rows)
            rows_norm_stage(nc, io, g, "fi_", rows, io["out"])
        else:
            store_stage(nc, io, g)


def kernel(**inputs):
    import numpy as _np
    import concourse.bacc as _bacc
    from concourse import mybir as _mybir
    from concourse.bass_utils import run_bass_kernel_spmd as _run

    nc = _bacc.Bacc("TRN2", target_bir_lowering=False, num_devices=1)
    i = {k: _np.asarray(v) for k, v in inputs.items()}

    def by_block(w):
        return w.reshape(w.shape[0] // P, P, -1).transpose(1, 0, 2)

    laid = {
        "xT": i["L0_attn_x"].reshape(NB, T, KB, P).transpose(3, 2, 0, 1),
        "ident": _np.eye(P, dtype=_np.float32),
        "masks": delta_rule_masks(),
        "dr_wkv": by_block(_np.concatenate([i["L0_attn_" + n].T for n in ("Wk", "Wv", "Wa", "Wb")], 1)),
        "dr_wqg": _np.stack([by_block(i["L0_attn_" + n].T) for n in ("Wq", "Wg")], 2),
        "dr_wo": i["L0_attn_Wo"].T,
        "dr_bkv": _np.concatenate([i["L0_attn_" + n] for n in ("bk", "bv", "ba", "bb")])[None],
        "dr_bqg": _np.stack([i["L0_attn_bq"], i["L0_attn_bg"]], 1),
        "dr_bo": i["L0_attn_bo"][None],
    }
    half = lambda s: _np.roll(s, DH // 2, -1)
    laid["lo_mask"] = window_masks()
    b1 = i["L0_ffn_b1"].reshape(DEPTH, 2, HID)
    b1 = _np.concatenate([b1, _np.zeros((DEPTH, 2, HC * P - HID), b1.dtype)], 2).reshape(DEPTH, 2, HC, P)
    w2 = i["L0_ffn_w2"]
    w2 = _np.concatenate([w2, _np.zeros((DEPTH, HC * P - HID, D), w2.dtype)], 1)
    laid["lo_wts"] = _np.stack([_np.concatenate([a.reshape(P, -1) for a in (
        by_block(i["L0_ffn_wqkv"][l]), by_block(i["L0_ffn_wo"][l]), by_block(i["L0_ffn_w1"][l]), by_block(w2[l]),
        b1[l].transpose(2, 0, 1), i["L0_ffn_b2"][l].reshape(KB, P).T, i["L0_ffn_ln_g"][l].reshape(KB, P).T,
        i["L0_ffn_ln_b"][l].reshape(KB, P).T,
        _np.broadcast_to(_np.concatenate([i["L0_ffn_q_scale"][l], i["L0_ffn_k_scale"][l],
                                          half(i["L0_ffn_q_scale"][l]), half(i["L0_ffn_k_scale"][l])]), (P, 4 * DH)),
        rotary_tables())], 1) for l in range(DEPTH)])
    E, rot = angle_tables()
    for n, w in (("rl_wq", "Wq"), ("rl_wk", "Wk"), ("rl_wv", "Wv")):
        laid[n] = by_block(i["L1_attn_" + w].T)
    laid["rl_wr"] = by_block(i["L1_attn_Wr"].reshape(D, P, 2).transpose(0, 2, 1).reshape(D, D))
    laid["rl_uv"] = _np.stack([i["L1_attn_" + n].reshape(KB, P).T for n in ("u_bias", "v_bias")], 1)
    laid["rl_E"], laid["rl_rot"] = E, rot.reshape(P, -1)
    laid["rl_dmask"] = diagonal_masks()
    laid["rl_sel"] = (_np.arange(P)[:, None] % 32 == _np.arange(RD)[None, :]).astype(_np.float32)
    laid["me_bias"] = _np.broadcast_to(i["L1_ffn_bias"], (P, D))
    laid["me_idx"] = i["L1_ffn_expert_indices"].reshape(TOKENS // P, P, TOPK).transpose(1, 0, 2)
    laid["me_w"] = i["L1_ffn_expert_weights"].reshape(TOKENS // P, P, TOPK).transpose(1, 0, 2)
    laid["me_erow"] = _np.broadcast_to(_np.arange(ME, dtype=_np.float32), (P, ME))
    laid["me_w1"] = i["L1_ffn_w1"].reshape(ME, KB, P, FF).transpose(0, 2, 1, 3)
    laid["me_w2"] = i["L1_ffn_w2"].reshape(ME, FF // P, P, D).transpose(0, 2, 1, 3)
    arrays, io = {}, {}
    for name, a in laid.items():
        a = _np.ascontiguousarray(a)
        arrays["in_" + name] = a
        io[name] = nc.dram_tensor("in_" + name, a.shape, _mybir.dt.from_np(a.dtype), kind="ExternalInput").ap()
    if STAGES < 4:
        io["outT"] = nc.dram_tensor("out_x", (P, KB, NB, T), F32, kind="ExternalOutput").ap()
    else:
        io["out"] = nc.dram_tensor("out_x", (NB, T, D), F32, kind="ExternalOutput").ap()
    program(nc, io)
    r = _run(nc, [arrays], core_ids=[0])
    if STAGES == 4:
        return r.results[0]["out_x"]
    return r.results[0]["out_x"].transpose(2, 3, 1, 0).reshape(NB, T, D)
```

```python
from contextlib import ExitStack

import numpy as np

import concourse.bass as bass
from concourse import mybir

F32 = mybir.dt.float32
BF16 = mybir.dt.bfloat16
I32 = mybir.dt.int32
ACT = mybir.ActivationFunctionType
ALU = mybir.AluOpType
AX_X = mybir.AxisListType.X

P = 128
NB = 2
T = 2048
D = 256
KB = D // P
NT = T // P
PAD = 4
LN_EPS = 1e-5
LEVELS = 7


class Steps:

    def __init__(self, eng, sem, per_turn=0, turn=0):
        self.eng, self.sem, self.per, self.turn, self.k = eng, sem, per_turn, turn, 0

    def done(self, ins):
        self.k += 1
        ins.then_inc(self.sem, 1)
        self.eng.wait_ge(self.sem, self.turn * self.per + self.k)

    def close(self):
        assert self.k == self.per, self.k


def across(ap, n):
    return ap.unsqueeze(1).to_broadcast([ap.shape[0], n, ap.shape[1]])


def ds(at, n):
    return bass.ds(at, n)


class Scope:

    def __init__(self, nc, ctx, prefix):
        self.nc, self.ctx, self.prefix = nc, ctx, prefix

    def sb(self, name, shape, dt=F32):
        return self.ctx.enter_context(self.nc.sbuf_tensor(self.prefix + name, shape, dt))

    def pb(self, name, shape, dt=F32):
        return self.ctx.enter_context(self.nc.psum_tensor(self.prefix + name, shape, dt))

    def sem(self, name):
        return self.ctx.enter_context(self.nc.semaphore(self.prefix + name))


def turns(eng, turn):
    turn(0, 0, tail=False)
    with eng.Fori(0, NT // 2 - 1) as pair:
        turn(2 * pair + 1, 1)
        turn(2 * pair + 2, 0)
    turn(NT - 1, 1)
    turn(NT, 0, head=False)


def delta_rule_masks():
    s, t = np.arange(P)[:, None], np.arange(P)[None, :]
    out = [s <= t, s > t]
    size = 1
    while size < P:
        out.append((t // size % 2 == 1) & (s // size == t // size - 1))
        size *= 2
    return np.stack(out, 1).astype(np.float32)


def delta_rule_stage(nc, io, g):
    xT, ident, ones, mhalf = g["xT"], g["ident"], g["ones"], g["mhalf"]
    PER_DVE, PER_DVE_TAIL = 4, 2
    C = P
    NKV = 2 * C + 2
    with ExitStack() as ctx:
        m = Scope(nc, ctx, "dr_")
        masks = m.sb("masks", [P, 2 + LEVELS, P])
        upto, after = masks[:, 0, :], masks[:, 1, :]
        wkv = m.sb("wkv", [P, KB, NKV])
        wqg = m.sb("wqg", [P, KB, 2, C])
        wo = m.sb("wo", [P, D])
        bkv = m.sb("bkv", [1, NKV])
        bo = m.sb("bo", [1, D])
        bqg = m.sb("bqg", [P, 2])
        xs = [m.sb(f"xs{i}", [P, KB, NB, P]) for i in range(2)]
        junk = m.sb("junk", [P, NB, C])
        ss = m.sb("ss", [P, NB])
        rn = m.sb("rn", [P, NB])
        z = m.sb("z", [P, NB, 2])
        e = m.sb("e", [P, NB, 2])
        den = m.sb("den", [P, NB, 2])
        zneg = m.sb("zneg", [P, NB])
        beta = m.sb("beta", [P, NB, 2])
        ln1 = m.sb("ln1", [P, NB])
        la = m.sb("la", [P, NB])
        laB = m.sb("laB", [P, NB, P])
        gcol = m.sb("gcol", [P, NB])
        eg = [m.sb(f"eg{i}", [P, 3, NB]) for i in range(2)]
        gb = m.sb("gb", [P, NB])
        kn = [m.sb(f"kn{i}", [P, NB, C]) for i in range(2)]
        kb = m.sb("kb", [P, NB, C])
        gbk = m.sb("gbk", [P, NB, C])
        kend = [m.sb(f"kend{i}", [P, NB, C]) for i in range(2)]
        bv = m.sb("bv", [P, NB, C])
        qT = [m.sb(f"qT{i}", [P, NB, P]) for i in range(2)]
        qgT = [m.sb(f"qgT{i}", [P, NB, P]) for i in range(2)]
        gz = m.sb("gz", [P, NB, P])
        gd = m.sb("gd", [P, NB, P])
        gateT = [m.sb(f"gateT{i}", [P, NB, P]) for i in range(2)]
        dneg = m.sb("dneg", [P, NB, P])
        dec = m.sb("dec", [P, NB, P])
        decM = [m.sb(f"decM{i}", [P, NB, P]) for i in range(2)]
        egrow = m.sb("egrow", [P, NB, P])
        kT = m.sb("kT", [P, 2, NB, P])
        AT = m.sb("AT", [P, NB, P])
        XT = m.sb("XT", [P, LEVELS, NB, P])
        TR = m.sb("TR", [P, 2, NB, P])
        Y = m.sb("Y", [P, NB, P])
        W0 = [m.sb(f"W0{i}", [P, 2, NB, P]) for i in range(2)]
        W1T = [m.sb(f"W1T{i}", [P, NB, P]) for i in range(2)]
        U = m.sb("U", [P, 2, NB, P])
        S = m.sb("S", [P, NB, 2, P])
        PT = m.sb("PT", [P, NB, P])
        ogT = m.sb("ogT", [P, NB, P])
        st6 = m.sb("st6", [P, NB, 6])
        mv = m.sb("mv", [P, NB, 2])
        vpe = m.sb("vpe", [P, NB])
        rstd = m.sb("rstd", [P, NB])
        yn = m.sb("yn", [P, NB, D])

        pKV = m.pb("pKV", [P, NB, 2 * C])
        pQG = m.pb("pQG", [P, 2, NB, P])
        pG = m.pb("pG", [P, 512])
        pY = m.pb("pY", [P, 2, NB, P])
        pZ = m.pb("pZ", [P, 2, NB, P])
        pU = m.pb("pU", [P, 2, NB, P])
        pO = m.pb("pO", [P, 2, NB, P])
        pR = m.pb("pR", [P, NB, D])
        grow_p = pG[:, 0:NB * P].rearrange("p (b t) -> p b t", b=NB)
        gcol_p = pG[:, 256:256 + 3 * NB].rearrange("p (k b) -> p k b", k=3)
        z_p = pG[:, 256 + 3 * NB:256 + 5 * NB].rearrange("p (b k) -> p b k", b=NB)
        Y_p, W1T_p = pY[:, 0, :, :], pY[:, 1, :, :]
        O_p, PT_p = pO[:, 0, :, :], pO[:, 1, :, :]
        ynT_pb = pR[:, :, :].rearrange("p a (b t) -> p a b t", b=NB)

        loaded, staged, kv_p, qg_p, ss_ready, ssm_ready, rn_ready = map(m.sem, (
            "loaded", "staged", "kv_p", "qg_p", "ss_ready", "ssm_ready", "rn_ready"))
        q_ready, gz_ready, e_ready, ln_ready, la_ready, g_p, eg_ready = map(m.sem, (
            "q_ready", "gz_ready", "e_ready", "ln_ready", "la_ready", "g_p", "eg_ready"))
        d_ready, dec_ready, decM_ready, qgT_ready, scaled, kT_p, kT_ready = map(m.sem, (
            "d_ready", "dec_ready", "decM_ready", "qgT_ready", "scaled", "kT_p", "kT_ready"))
        kk_p, at_ready, xt_ready, tr_ready, level_y, y_ready, level_z = map(m.sem, (
            "kk_p", "at_ready", "xt_ready", "tr_ready", "level_y", "y_ready", "level_z"))
        w_p, w0_ready, w1_ready, u_p, u_ready, pt_p, pt_ready, s_p, s_ready, o_p, og_ready = map(m.sem, (
            "w_p", "w0_ready", "w1_ready", "u_p", "u_ready", "pt_p", "pt_ready", "s_p", "s_ready", "o_p", "og_ready"))
        y_p, var_ready, rstd_ready, yn_ready, ynT_p, x_stored, inited, dve_step = map(m.sem, (
            "y_p", "var_ready", "rstd_ready", "yn_ready", "ynT_p", "x_stored", "inited", "dve_step"))
        dve_tail_step = m.sem("dve_tail_step")

        with nc.Block() as block:
            @block.sync
            def _(sp):
                for dst, src in ((masks[:, :, :], io["masks"]), (wkv[:, :, :], io["dr_wkv"]),
                                 (wqg[:, :, :, :], io["dr_wqg"]), (wo[:, :], io["dr_wo"]),
                                 (bkv[:, :], io["dr_bkv"]), (bo[:, :], io["dr_bo"]), (bqg[:, :], io["dr_bqg"]),
                                 (ident[:, :], io["ident"])):
                    sp.dma_start(dst, src).then_inc(loaded, 16)
                for k in range(KB):
                    sp.dma_start(xT[:, k, :, PAD:], io["xT"][:, k, :, :]).then_inc(loaded, 16)
                sp.wait_ge(loaded, 16 * (8 + KB))

            @block.gpsimd
            def _(pool):
                pool.memset(xT[:, :, :, 0:PAD], 0.0)
                pool.memset(ones[:, :], 1.0)
                pool.memset(mhalf[:, :], -0.5)
                pool.memset(S[:, :, :, :], 0.0).then_inc(s_ready, 1)
                pool.memset(ss[:, :], 1.0).then_inc(y_p, 1)
                pool.memset(z[:, :, :], 0.0).then_inc(x_stored, 1)

        with nc.Block() as block:
            @block.gpsimd
            def _(pool):
                def turn(n, s, head=True, tail=True):
                    k = n - 1
                    if head:
                        if type(n) is not int or n > 0:
                            pool.wait_ge(y_p, n)
                        for b in range(NB):
                            nc.gpsimd.tensor_copy(xs[s][:, :, b, :], xT[:, :, b, ds(n * P + PAD, P)]).then_inc(staged, 1)
                        pool.wait_ge(ssm_ready, n + 1)
                        nc.gpsimd.tensor_tensor(rn[:, :], ss[:, :], mhalf[:, 0:NB], ALU.pow).then_inc(rn_ready, 1)
                        pool.wait_ge(q_ready, n + 1)
                        pool.wait_ge(eg_ready, n + 1)
                        nc.gpsimd.tensor_tensor(qgT[s][:, :, :], qT[s][:, :, :], egrow[:, :, :],
                                                ALU.mult).then_inc(qgT_ready, 1)
                        pool.wait_ge(dec_ready, n + 1)
                        nc.gpsimd.tensor_tensor(decM[s][:, :, :], dec[:, :, :], across(upto, NB),
                                                ALU.mult).then_inc(decM_ready, 1)
                        pool.wait_ge(at_ready, n + 1)
                        for lv in range(LEVELS):
                            nc.gpsimd.tensor_tensor(XT[:, lv, :, :], AT[:, :, :], across(masks[:, 2 + lv, :], NB),
                                                    ALU.mult).then_inc(xt_ready, 1)
                    if tail:
                        pool.wait_ge(var_ready, k + 1)
                        nc.gpsimd.tensor_tensor(rstd[:, :], vpe[:, :], mhalf[:, 0:NB], ALU.pow).then_inc(rstd_ready, 1)

                turns(pool, turn)

            @block.scalar
            def _(act):
                def turn(n, s, head=True, tail=True):
                    k = n - 1
                    if head:
                        act.wait_ge(kv_p, n + 1)
                        for b in range(NB):
                            nc.scalar.activation(z[:, b, 0:1], z_p[:, b, 0:1], ACT.Abs)
                            nc.scalar.activation(z[:, b, 1:2], z_p[:, b, 1:2], ACT.Copy)
                            ins = nc.scalar.activation(junk[:, b, :], pKV[:, b, 0:C], ACT.Square, accum_out=ss[:, b:b + 1])
                        ins.then_inc(ss_ready, 1)
                        act.wait_ge(ss_ready, n + 1)
                        nc.scalar.activation(e[:, :, :], z[:, :, :], ACT.Exp, scale=-1.0).then_inc(e_ready, 1)
                        act.wait_ge(e_ready, n + 1)
                        nc.scalar.activation(ln1[:, :], e[:, :, 0], ACT.Ln, bias=1.0).then_inc(ln_ready, 1)
                        act.wait_ge(qg_p, n + 1)
                        nc.scalar.activation(qT[s][:, :, :], pQG[:, 0, :, :], ACT.Identity,
                                             bias=bqg[:, 0:1]).then_inc(q_ready, 1)
                        nc.scalar.activation(gz[:, :, :], pQG[:, 1, :, :], ACT.Exp, bias=bqg[:, 1:2],
                                             scale=-1.0).then_inc(gz_ready, 1)
                        act.wait_ge(d_ready, n + 1)
                        nc.scalar.activation(eg[s][:, :, :], gcol_p, ACT.Exp)
                        nc.scalar.activation(egrow[:, :, :], grow_p, ACT.Exp).then_inc(eg_ready, 1)
                        nc.scalar.activation(dec[:, :, :], dneg[:, :, :], ACT.Exp).then_inc(dec_ready, 1)
                        act.wait_ge(kT_p, n + 1)
                        nc.scalar.activation(kT[:, :, :, :], pZ[:, :, :, :], ACT.Copy).then_inc(kT_ready, 1)
                    if tail:
                        act.wait_ge(ynT_p, k + 1)
                        for b in range(NB):
                            ins = nc.scalar.activation(xT[:, :, b, ds(k * P + PAD, P)], ynT_pb[:, :, b, :], ACT.Copy)
                        ins.then_inc(x_stored, 1)
                    if head:
                        act.wait_ge(w_p, n + 1)
                        nc.scalar.activation(W1T[s][:, :, :], W1T_p, ACT.Copy).then_inc(w1_ready, 1)

                turns(act, turn)

            @block.vector
            def _(dve):
                nc.vector.tensor_scalar(bqg[:, 1:2], bqg[:, 1:2], -1.0, None, ALU.mult).then_inc(inited, 1)

                def turn(n, s, head=True, tail=True):
                    k, r = n - 1, 1 - s
                    own, own_tail = Steps(dve, dve_step, PER_DVE, n), Steps(dve, dve_tail_step, PER_DVE_TAIL, k)
                    if tail:
                        dve.wait_ge(w0_ready, k + 1)
                        dve.wait_ge(u_p, k + 1)
                        nc.vector.tensor_tensor(U[:, :, :, :], W0[r][:, :, :, :], pU[:, :, :, :],
                                                ALU.subtract).then_inc(u_ready, 1)
                    if head:
                        dve.wait_ge(ss_ready, n + 1)
                        for b in range(NB):
                            nc.vector.tensor_scalar(zneg[:, b:b + 1], z_p[:, b, 0:1], 0.0, None, ALU.min)
                        nc.vector.tensor_scalar(ss[:, :], ss[:, :], 1e-24, None, ALU.max).then_inc(ssm_ready, 1)
                        dve.wait_ge(ssm_ready, n + 1)
                        dve.wait_ge(ln_ready, n + 1)
                        nc.vector.tensor_tensor(la[:, :], zneg[:, :], ln1[:, :], ALU.subtract)
                        own.done(nc.vector.tensor_scalar(den[:, :, :], e[:, :, :], 1.0, None, ALU.add))
                        nc.vector.reciprocal(beta[:, :, :], den[:, :, :])
                        for b in range(NB):
                            ins = nc.vector.tensor_scalar(laB[:, b, :], ones[:, :], la[:, b:b + 1], None, ALU.mult)
                        ins.then_inc(la_ready, 1)
                    if tail:
                        dve.wait_ge(pt_p, k + 1)
                        dve.wait_ge(decM_ready, k + 1)
                        nc.vector.tensor_tensor(PT[:, :, :], PT_p, decM[r][:, :, :], ALU.mult).then_inc(pt_ready, 1)
                    if head:
                        dve.wait_ge(gz_ready, n + 1)
                        own.done(nc.vector.tensor_scalar(gd[:, :, :], gz[:, :, :], 1.0, None, ALU.add))
                        nc.vector.reciprocal(gateT[s][:, :, :], gd[:, :, :])
                        dve.wait_ge(g_p, n + 1)
                        own.done(nc.vector.tensor_copy(gcol[:, :], gcol_p[:, 0, :]))
                        for b in range(NB):
                            ins = nc.vector.tensor_scalar(dneg[:, b, :], grow_p[:, b, :], gcol[:, b:b + 1], 0.0,
                                                          ALU.subtract, ALU.min)
                        ins.then_inc(d_ready, 1)
                    if tail:
                        dve.wait_ge(o_p, k + 1)
                        nc.vector.tensor_tensor(ogT[:, :, :], O_p, gateT[r][:, :, :], ALU.mult).then_inc(og_ready, 1)
                        dve.wait_ge(s_p, k + 1)
                        for b in range(NB):
                            ins = nc.vector.scalar_tensor_tensor(S[:, b, :, :], S[:, b, :, :], eg[r][:, 2, b:b + 1],
                                                                 pU[:, :, b, :], ALU.mult, ALU.add)
                        ins.then_inc(s_ready, 1)
                    if head:
                        dve.wait_ge(rn_ready, n + 1)
                        dve.wait_ge(eg_ready, n + 1)
                        nc.vector.tensor_tensor(gb[:, :], beta[:, :, 1], eg[s][:, 0, :], ALU.mult)
                        for b in range(NB):
                            nc.vector.tensor_scalar(bv[:, b, :], pKV[:, b, C:2 * C], beta[:, b, 1:2], None, ALU.mult)
                            ins = nc.vector.tensor_scalar(kn[s][:, b, :], pKV[:, b, 0:C], rn[:, b:b + 1], None, ALU.mult)
                        own.done(ins)
                        for b in range(NB):
                            ins = nc.vector.tensor_scalar(kb[:, b, :], kn[s][:, b, :], beta[:, b, 1:2], None, ALU.mult)
                        ins.then_inc(scaled, 1)
                        for b in range(NB):
                            nc.vector.tensor_scalar(gbk[:, b, :], kn[s][:, b, :], gb[:, b:b + 1], None, ALU.mult)
                            nc.vector.tensor_scalar(kend[s][:, b, :], kn[s][:, b, :], eg[s][:, 1, b:b + 1], None, ALU.mult)
                        nc.vector.tensor_copy(TR[:, :, :, :].rearrange("p a b t -> p (a b) t"),
                                              across(ident[:, :], 2 * NB)).then_inc(tr_ready, 1)
                        dve.wait_ge(kk_p, n + 1)
                        dve.wait_ge(dec_ready, n + 1)
                        nc.vector.tensor_tensor(AT[:, :, :], Y_p, dec[:, :, :], ALU.mult).then_inc(at_ready, 1)
                    for lv in range(LEVELS):
                        if head:
                            dve.wait_ge(level_y, n * LEVELS + lv + 1)
                            nc.vector.tensor_copy(Y[:, :, :], Y_p).then_inc(y_ready, 1)
                        if tail and lv == 0:
                            dve.wait_ge(y_p, k + 2)
                            for b in range(NB):
                                ins = nc.vector.bn_stats(st6[:, b, :], pR[:, b, :])
                            own_tail.done(ins)
                            dve.nop(nofuse=True)
                            for b in range(NB):
                                ins = nc.vector.bn_aggr(mv[:, b, :], st6[:, b, :])
                            own_tail.done(ins)
                            nc.vector.tensor_scalar(vpe[:, :], mv[:, :, 1], LN_EPS, None, ALU.add).then_inc(var_ready, 1)
                        if tail and lv == LEVELS - 2:
                            dve.wait_ge(rstd_ready, k + 1)
                            for b in range(NB):
                                ins = nc.vector.tensor_scalar(yn[:, b, :], pR[:, b, :], mv[:, b, 0:1], rstd[:, b:b + 1],
                                                              ALU.subtract, ALU.mult)
                            ins.then_inc(yn_ready, 1)
                        if head:
                            dve.wait_ge(tr_ready, n * (LEVELS + 1) + lv + 1)
                            dve.wait_ge(level_z, n * LEVELS + lv + 1)
                            nc.vector.tensor_tensor(TR[:, :, :, :], TR[:, :, :, :], pZ[:, :, :, :],
                                                    ALU.subtract).then_inc(tr_ready, 1)
                    if head:
                        dve.wait_ge(w_p, n + 1)
                        nc.vector.tensor_copy(W0[s][:, :, :, :], pZ[:, :, :, :]).then_inc(w0_ready, 1)
                        own.close()
                    if tail:
                        own_tail.close()

                turns(dve, turn)

            @block.tensor
            def _(pe):
                mm = nc.tensor.matmul

                def turn(n, s, head=True, tail=True):
                    k, r = n - 1, 1 - s
                    if head:
                        pe.wait_ge(staged, NB * (n + 1))
                        for b in range(NB):
                            for c, out in ((slice(0, 2 * C), pKV[:, b, :]), (slice(2 * C, NKV), z_p[:, b, :])):
                                for j in range(KB):
                                    mm(out, xs[s][:, j, b, :], wkv[:, j, c], start=(j == 0), stop=False)
                                ins = mm(out, ones[0:1, :], bkv[0:1, c], start=False, stop=True)
                        ins.then_inc(kv_p, 1)
                    if tail:
                        pe.wait_ge(w1_ready, k + 1)
                        pe.wait_ge(s_ready, k + 1)
                        for b in range(NB):
                            mm(pU[:, 0, b, :], W1T[r][:, b, :], S[:, b, 1, :], start=True, stop=True)
                            ins = mm(pU[:, 1, b, :], S[:, b, 1, :], W1T[r][:, b, :], start=True, stop=True)
                        ins.then_inc(u_p, 1)
                    if head:
                        pe.wait_ge(inited, 1)
                        for i in range(2):
                            for j in range(KB):
                                ins = mm(pQG[:, i, :, :], wqg[:, j, i, :], xs[s][:, j, :, :], start=(j == 0),
                                         stop=(j == KB - 1))
                        ins.then_inc(qg_p, 1)
                    if tail:
                        pe.wait_ge(u_ready, k + 1)
                        for b in range(NB):
                            ins = mm(PT_p[:, b, :], U[:, 1, b, :], qT[r][:, b, :], start=True, stop=True)
                        ins.then_inc(pt_p, 1)
                    if head:
                        pe.wait_ge(la_ready, n + 1)
                        for i, w in enumerate((upto, after, ones[:, :])):
                            mm(gcol_p[:, i, :], w, la[:, :], start=True, stop=True)
                        for b in range(NB):
                            ins = mm(grow_p[:, b, :], laB[:, b, :], upto, start=True, stop=True)
                        ins.then_inc(g_p, 1)
                    if tail:
                        pe.wait_ge(pt_ready, k + 1)
                        pe.wait_ge(qgT_ready, k + 1)
                        for b in range(NB):
                            mm(O_p[:, b, :], S[:, b, 0, :], qgT[r][:, b, :], start=True, stop=False)
                            ins = mm(O_p[:, b, :], kn[r][:, b, :], PT[:, b, :], start=False, stop=True)
                        ins.then_inc(o_p, 1)
                        for b in range(NB):
                            mm(pU[:, 0, b, :], U[:, 0, b, :], kend[r][:, b, :], start=True, stop=True)
                            ins = mm(pU[:, 1, b, :], kend[r][:, b, :], U[:, 0, b, :], start=True, stop=True)
                        ins.then_inc(s_p, 1)
                    if head:
                        pe.wait_ge(scaled, n + 1)
                        for b in range(NB):
                            nc.tensor.transpose(pZ[:, 0, b, :], kn[s][:, b, :], ident[:, :])
                            ins = nc.tensor.transpose(pZ[:, 1, b, :], kb[:, b, :], ident[:, :])
                        ins.then_inc(kT_p, 1)
                        pe.wait_ge(kT_ready, n + 1)
                        for b in range(NB):
                            ins = mm(Y_p[:, b, :], kT[:, 0, b, :], kT[:, 1, b, :], start=True, stop=True)
                        ins.then_inc(kk_p, 1)
                    if tail:
                        pe.wait_ge(og_ready, k + 1)
                        pe.wait_ge(x_stored, k + 1)
                        for b in range(NB):
                            mm(pR[:, b, :], ogT[:, b, :], wo[:, :], start=True, stop=False)
                            for j in range(KB):
                                mm(pR[:, b, j * P:(j + 1) * P], xs[r][:, j, b, :], ident[:, :], start=False,
                                   stop=False, skip_group_check=True)
                            ins = mm(pR[:, b, :], ones[0:1, :], bo[0:1, :], start=False, stop=True)
                        ins.then_inc(y_p, 1)
                    for lv in range(LEVELS):
                        if head:
                            pe.wait_ge(xt_ready, n * LEVELS + lv + 1)
                            pe.wait_ge(tr_ready, n * (LEVELS + 1) + lv + 1)
                            for b in range(NB):
                                ins = mm(Y_p[:, b, :], XT[:, lv, b, :], TR[:, 0, b, :], start=True, stop=True)
                            ins.then_inc(level_y, 1)
                            pe.wait_ge(y_ready, n * LEVELS + lv + 1)
                            for b in range(NB):
                                mm(pZ[:, 0, b, :], TR[:, 1, b, :], Y[:, b, :], start=True, stop=True)
                                ins = mm(pZ[:, 1, b, :], Y[:, b, :], TR[:, 1, b, :], start=True, stop=True)
                            ins.then_inc(level_z, 1)
                        if tail and lv == LEVELS - 2:
                            pe.wait_ge(yn_ready, k + 1)
                            for b in range(NB):
                                for j in range(KB):
                                    ins = nc.tensor.transpose(ynT_pb[:, j, b, :], yn[:, b, j * P:(j + 1) * P],
                                                              ident[:, :])
                            ins.then_inc(ynT_p, 1)
                    if head:
                        pe.wait_ge(tr_ready, (n + 1) * (LEVELS + 1))
                        for b in range(NB):
                            mm(W1T_p[:, b, :], gbk[:, b, :], TR[:, 1, b, :], start=True, stop=True)
                            mm(pZ[:, 0, b, :], TR[:, 1, b, :], bv[:, b, :], start=True, stop=True)
                            ins = mm(pZ[:, 1, b, :], bv[:, b, :], TR[:, 1, b, :], start=True, stop=True)
                        ins.then_inc(w_p, 1)

                turns(pe, turn)


DEPTH = 2
HEADS = 8
DH = 64
INNER = HEADS * DH
HP = INNER // P
WINDOW = 128
HID = 682
HC = -(-HID // P)
QKV_AT = 0
WO_AT = QKV_AT + KB * 3 * INNER
W1_AT = WO_AT + HP * D
W2_AT = W1_AT + KB * 2 * HID
B1_AT = W2_AT + HC * D
B2_AT = B1_AT + 2 * HC
LG_AT = B2_AT + KB
LB_AT = LG_AT + KB
QS_AT = LB_AT + KB
TAB_AT = QS_AT + 4 * DH
LAYER_COLS = TAB_AT + NT * 4 * DH
MASKED = -3.0e38


def rotary_tables():
    half = np.arange(0, DH, 2, dtype=np.float32)
    inv = (1.0 / 10000.0 ** (half / DH)).astype(np.float32)
    t = np.arange(T, dtype=np.float32)
    freqs = (t[:, None] * inv[None, :]).astype(np.float32)
    base = ((half + 0.4 * DH) / (1.4 * DH)).astype(np.float32)
    power = (t - T // 2) / float(WINDOW // 2)
    scale = base[None, :].astype(np.float64) ** power[:, None]
    cos, sin = np.cos(freqs.astype(np.float64)), np.sin(freqs.astype(np.float64))

    def both(a, sign=1.0):
        return np.concatenate([sign * a, a], -1)

    kinds = [both(cos * scale) * 8.0, both(cos / scale), both(sin * scale, -1.0) * 8.0, both(sin / scale, -1.0)]
    tab = np.stack(kinds, 1).astype(np.float32)
    return tab.reshape(NT, P, 4 * DH).transpose(1, 0, 2).reshape(P, -1)


def window_masks():
    i, j = np.arange(P)[:, None], np.arange(P)[None, :]
    no = np.full((P, P), MASKED)
    this = np.where(j <= i, 0.0, MASKED)
    last = np.where(j >= i, 0.0, MASKED)
    first, later = np.concatenate([no, this], 1), np.concatenate([last, this], 1)
    return np.stack([np.concatenate([a, a], 1) for a in (first, later)], 1).astype(np.float32)


def local_stage(nc, io, g):
    xT, x1T, ident, ones, mhalf = g["xT"], g["x1T"], g["ident"], g["ones"], g["mhalf"]
    with ExitStack() as ctx:
        m = Scope(nc, ctx, "lo_")
        wts = m.sb("wts", [P, LAYER_COLS])

        def part(at, *shape):
            n = int(np.prod(shape))
            names = "abc"[:len(shape)]
            return wts[:, at:at + n].rearrange(f"p ({' '.join(names)}) -> p {' '.join(names)}",
                                               **dict(zip(names, shape)))

        wqkv = part(QKV_AT, KB, 3 * INNER)
        wo = part(WO_AT, HP, D)
        w1 = part(W1_AT, KB, 2, HID)
        w2 = part(W2_AT, HC, D)
        b1 = part(B1_AT, 2, HC)
        b2, lg, lb = wts[:, B2_AT:B2_AT + KB], wts[:, LG_AT:LG_AT + KB], wts[:, LB_AT:LB_AT + KB]
        qs = wts[:, QS_AT:QS_AT + 4 * DH]
        tab = part(TAB_AT, NT, 4 * DH)

        maskf = m.sb("maskf", [P, 2, 4 * P])
        maskt = m.sb("maskt", [P, 2, 4 * P], BF16)
        identb = m.sb("identb", [P, P], BF16)
        HS = 4
        hs = m.sb("hs", [P, KB, NB, HS + P])
        sq = m.sb("sq", [P, 2 * HEADS, DH])
        ss = m.sb("ss", [P, 2 * HEADS])
        ssm = m.sb("ssm", [P, 2 * HEADS])
        rn = m.sb("rn", [P, 2 * HEADS])
        qn = m.sb("qn", [P, 2, HEADS, DH])
        r1 = m.sb("r1", [P, 2, HEADS, DH])
        r2 = m.sb("r2", [P, 2, HEADS, DH])
        qT = m.sb("qT", [P, HP, P])
        kT = m.sb("kT", [P, HP, NB, 2 * P])
        V = m.sb("V", [P, NB, 2, INNER])
        Pm = m.sb("Pm", [P, 2, 2, 2 * P])
        sums = m.sb("sums", [P, HEADS])
        rsum = m.sb("rsum", [P, HEADS])
        nmx = m.sb("nmx", [P, HEADS])
        PT = m.sb("PT", [P, 2, 4, P])
        OT = m.sb("OT", [P, HP, NB, P])
        xm = m.sb("xm", [P, KB, NB, HS + P])
        st6 = m.sb("st6", [P, NB, 6])
        mv = m.sb("mv", [P, NB, 2])
        vpe = m.sb("vpe", [P, NB])
        rstd = m.sb("rstd", [P, NB])
        hn = m.sb("hn", [P, NB, D])
        hnT = m.sb("hnT", [P, KB, NB, P])
        KLAST = HID - (HC - 1) * P
        hu = m.sb("hu", [P, 2, HC, NB * P])
        hid = m.sb("hid", [P, HC, NB * P])

        pQKV = [m.pb(f"pQKV{n}", [P, 512]) for n in range(3)]
        pAB = [m.pb(f"p{n}", [P, 4, P]) for n in "AB"]
        pS = [m.pb(f"pS{n}", [P, 2, 2 * P]) for n in range(2)]
        pO = m.pb("pO", [P, 4, P])
        y_b = pQKV[0][:, :].rearrange("p (f b t) -> p f b t", f=KB, b=NB)
        x_p = pO[:, :, :].rearrange("p (f b) t -> p f b t", f=KB)
        hn_p = pAB[0][:, :, :].rearrange("p (b k) t -> p b (k t)", b=NB)
        hT_b = pAB[1][:, :, :].rearrange("p (k b) t -> p k b t", k=KB)

        (weights, tables, staged, qkv_p, sq_ready, v_ready, ssm_ready, rn_ready, qn_ready, r2_ready, qr_ready,
         qkT_p, qkT_ready) = map(m.sem, (
             "weights", "tables", "staged", "qkv_p", "sq_ready", "v_ready", "ssm_ready", "rn_ready", "qn_ready",
             "r2_ready", "qr_ready", "qkT_p", "qkT_ready"))
        pool_step, shifted, u_ready, att_step, mlp_step = map(m.sem, (
            "pool_step", "shifted", "u_ready", "att_step", "mlp_step"))
        (s_p, mx_ready, e_ready, pn_ready, pT_p, pT_ready, o_p, ot_ready, xm_p, xm_ready, h_p, var_ready, rstd_ready,
         hn_ready, hT_p, hnT_ready, u_p, gl_ready, hid_ready, y_p, x_stored        ) = map(m.sem, (
             "s_p", "mx_ready", "e_ready", "pn_ready", "pT_p", "pT_ready", "o_p", "ot_ready", "xm_p", "xm_ready",
             "h_p", "var_ready", "rstd_ready", "hn_ready", "hT_p", "hnT_ready", "u_p", "gl_ready", "hid_ready",
             "y_p", "x_stored"))

        with nc.Block() as block:
            @block.sync
            def _(sp):
                sp.dma_start(maskf[:, :, :], io["lo_mask"]).then_inc(weights, 16)
                sp.wait_ge(weights, 16)

            @block.gpsimd
            def _(pool):
                pool.memset(hs[:, :, :, :], 0.0)
                pool.memset(xm[:, :, :, :], 0.0)
                pool.memset(kT[:, :, :, :], 0.0)
                pool.memset(V[:, :, :, :], 0.0).then_inc(x_stored, 1)

            @block.vector
            def _(dve):
                dve.wait_ge(weights, 16)
                nc.vector.tensor_copy(maskt[:, :, :], maskf[:, :, :])
                nc.vector.tensor_copy(identb[:, :], ident[:, :])

            @block.scalar
            def _(act):
                for k in range(KB):
                    nc.scalar.activation(x1T[:, k, :, :], xT[:, k, :, :], ACT.Copy)

        def layers(eng, turn):
            with eng.Fori(0, DEPTH) as layer:
                turn(layer, layer * NT, 0, True, False)
                with eng.Fori(1, NT) as w:
                    turn(layer, layer * NT + w, w, True, True)
                turn(layer, layer * NT + NT, NT, False, True)

        with nc.Block() as block:
            @block.sync
            def _(sp):
                with sp.Fori(0, DEPTH) as layer:
                    sp.wait_ge(x_stored, layer * NT + 1)
                    sp.dma_start(wts[:, :], io["lo_wts"][ds(layer, 1), :, :].rearrange("l p n -> (l p) n")).then_inc(weights, 16)

            @block.gpsimd
            def _(pool):
                def rotate(t, w, b):
                    pool.wait_ge(ssm_ready, t * NB + b + 1)
                    nc.gpsimd.tensor_tensor(rn[:, :], ssm[:, :], mhalf[:, :], ALU.pow).then_inc(rn_ready, 1)
                    pool.wait_ge(qn_ready, t * NB + b + 1)
                    pool.nop(nofuse=True)
                    for to, frm in ((0, DH // 2), (DH // 2, 0)):
                        for qk in range(2):
                            sines = tab[:, ds(w, 1), (2 + qk) * DH + to:(2 + qk) * DH + to + DH // 2]
                            nc.gpsimd.tensor_tensor(r2[:, qk, :, to:to + DH // 2], qn[:, qk, :, frm:frm + DH // 2],
                                                    sines.to_broadcast([P, HEADS, DH // 2]),
                                                    ALU.mult).then_inc(r2_ready, 1)

                def turn(layer, t, w, att, mlp):
                    if not mlp:
                        pool.wait_ge(tables, layer + 1)
                        pool.nop(nofuse=True)
                        nc.gpsimd.memset(hs[:, :, :, HS - 1:HS], 0.0).then_inc(pool_step, 1)
                        nc.gpsimd.memset(V[:, :, 0, :], 0.0).then_inc(shifted, 1)
                    elif att:
                        pool.wait_ge(qkv_p, t * NB)
                        pool.nop(nofuse=True)
                        nc.gpsimd.tensor_copy(hs[:, :, :, HS - 1:HS], hs[:, :, :, HS + P - 1:HS + P]).then_inc(pool_step, 1)
                        pool.wait_ge(pool_step, t + 1)
                        pool.nop(nofuse=True)
                    if att:
                        for k in range(KB):
                            nc.gpsimd.tensor_copy(hs[:, k, :, HS:], x1T[:, k, :, ds(w * P + PAD, P)]).then_inc(staged, 1)
                    if att and mlp:
                        pool.wait_ge(o_p, t * NB)
                        pool.nop(nofuse=True)
                        nc.gpsimd.tensor_copy(V[:, :, 0, :], V[:, :, 1, :])
                        nc.gpsimd.tensor_copy(kT[:, :, :, 0:P], kT[:, :, :, P:]).then_inc(shifted, 1)
                    if att:
                        rotate(t, w, 0)
                    if mlp:
                        pool.wait_ge(var_ready, t)
                        nc.gpsimd.tensor_tensor(rstd[:, :], vpe[:, :], mhalf[:, 0:NB], ALU.pow).then_inc(rstd_ready, 1)
                    if att:
                        rotate(t, w, 1)

                layers(pool, turn)

            @block.scalar
            def _(act):
                def squares_and_v(t, b):
                    act.wait_ge(qkv_p, t * NB + b + 1)
                    for i in range(2):
                        ins = nc.scalar.activation(sq[:, i * HEADS:(i + 1) * HEADS, :].rearrange("p h d -> p (h d)"),
                                                   pQKV[i][:, :], ACT.Square)
                    ins.then_inc(sq_ready, 1)
                    act.wait_ge(shifted, t + 1)
                    nc.scalar.activation(V[:, b, 1, :], pQKV[2][:, :], ACT.Copy).then_inc(v_ready, 1)

                def turned(t, b):
                    act.wait_ge(qkT_p, t * NB + b + 1)
                    nc.scalar.activation(qT[:, :, :], pAB[0][:, :, :], ACT.Copy)
                    nc.scalar.activation(kT[:, :, b, P:], pAB[1][:, :, :], ACT.Copy).then_inc(qkT_ready, 1)

                def probabilities(t, b):
                    at = (t * NB + b) * HP

                    def exps(u):
                        act.wait_ge(mx_ready, at + u + 1)
                        for j in range(2):
                            h = 2 * u + j
                            ins = nc.scalar.activation(Pm[:, u % 2, j, :], pS[u % 2][:, j, :], ACT.Exp,
                                                       bias=nmx[:, h:h + 1], accum_out=sums[:, h:h + 1])
                        ins.then_inc(e_ready, 1)

                    def evac(u):
                        act.wait_ge(pT_p, at + u + 1)
                        nc.scalar.activation(PT[:, u % 2, :, :], pAB[u % 2][:, :, :], ACT.Copy).then_inc(pT_ready, 1)

                    exps(0)
                    exps(1)
                    for u in range(HP):
                        evac(u)
                        if u + 2 < HP:
                            exps(u + 2)
                    act.wait_ge(o_p, t * NB + b + 1)
                    nc.scalar.activation(OT[:, :, b, :], pO[:, :, :], ACT.Copy).then_inc(ot_ready, 1)

                def turn(layer, t, w, att, mlp):
                    if att:
                        squares_and_v(t, 0)
                        squares_and_v(t, 1)
                    if mlp:
                        act.wait_ge(hT_p, t)
                        for k in range(KB):
                            ins = nc.scalar.activation(hnT[:, k, :, :], hT_b[:, k, :, :], ACT.Identity,
                                                       bias=lb[:, k:k + 1], scale=lg[:, k:k + 1])
                        ins.then_inc(hnT_ready, 1)
                    if att:
                        turned(t, 0)
                        probabilities(t, 0)
                        turned(t, 1)
                    if mlp:
                        act.wait_ge(u_ready, t * HC)
                        nc.scalar.activation(hu[:, 1, 0:HC - 1, :], hu[:, 1, 0:HC - 1, :], ACT.Gelu)
                        nc.scalar.activation(hu[0:KLAST, 1, HC - 1, :], hu[0:KLAST, 1, HC - 1, :], ACT.Gelu).then_inc(gl_ready, 1)
                    if att:
                        probabilities(t, 1)

                layers(act, turn)

            @block.vector
            def _(dve):
                def turn(layer, t, w, att, mlp):
                    own = Steps(dve, att_step, 12, t)
                    mine = Steps(dve, mlp_step, 3, t - 1)

                    def lengths(b):
                        dve.wait_ge(sq_ready, t * NB + b + 1)
                        own.done(nc.vector.tensor_reduce(ss[:, :], sq[:, :, :], AX_X, ALU.add))
                        nc.vector.tensor_scalar(ssm[:, :], ss[:, :], 1e-24, None, ALU.max).then_inc(ssm_ready, 1)

                    def unit(b):
                        dve.wait_ge(rn_ready, t * NB + b + 1)
                        rnb = rn[:, :].rearrange("p (a h) -> p a h", a=2)
                        for i in range(2):
                            ins = nc.vector.tensor_tensor(qn[:, i, :, :], pQKV[i][:, :].rearrange("p (h d) -> p h d", d=DH),
                                                          rnb[:, i, :].unsqueeze(2).to_broadcast([P, HEADS, DH]), ALU.mult)
                        ins.then_inc(qn_ready, 1)

                    def rotate(b):
                        dve.wait_ge(qn_ready, t * NB + b + 1)
                        if b:
                            dve.wait_ge(qkT_p, t * NB + b)
                        for qk in range(2):
                            cosines = tab[:, ds(w, 1), qk * DH:(qk + 1) * DH]
                            ins = nc.vector.tensor_tensor(r1[:, qk, :, :], qn[:, qk, :, :],
                                                          cosines.to_broadcast([P, HEADS, DH]), ALU.mult)
                        own.done(ins)
                        dve.wait_ge(r2_ready, (t * NB + b + 1) * 4)
                        nc.vector.tensor_tensor(r1[:, :, :, :], r1[:, :, :, :], r2[:, :, :, :], ALU.add).then_inc(qr_ready, 1)

                    def peak(b, u):
                        dve.wait_ge(s_p, (t * NB + b) * HP + u + 1)
                        nc.vector.tensor_reduce(nmx[:, 2 * u:2 * u + 2], pS[u % 2][:, :, :], AX_X, ALU.max,
                                                negate=True).then_inc(mx_ready, 1)

                    def norm(b, u):
                        dve.wait_ge(e_ready, (t * NB + b) * HP + u + 1)
                        own.done(nc.vector.reciprocal(rsum[:, 2 * u:2 * u + 2], sums[:, 2 * u:2 * u + 2]))
                        for j in range(2):
                            h = 2 * u + j
                            ins = nc.vector.tensor_scalar(Pm[:, u % 2, j, :], Pm[:, u % 2, j, :], rsum[:, h:h + 1],
                                                          None, ALU.mult)
                        ins.then_inc(pn_ready, 1)

                    def hidden(c):
                        K = min(P, HID - c * P)
                        dve.wait_ge(u_p, (t - 1) * HC + c + 1)
                        for ag in range(2):
                            ins = nc.vector.tensor_scalar(hu[0:K, ag, c, :], pQKV[c % 3][0:K, ag * NB * P:(ag + 1) * NB * P],
                                                          b1[0:K, ag, c:c + 1], None, ALU.add)
                        ins.then_inc(u_ready, 1)

                    def gated():
                        dve.wait_ge(gl_ready, t)
                        dve.wait_ge(u_ready, t * HC)
                        nc.vector.tensor_tensor(hid[:, 0:HC - 1, :], hu[:, 0, 0:HC - 1, :], hu[:, 1, 0:HC - 1, :], ALU.mult)
                        nc.vector.tensor_tensor(hid[0:KLAST, HC - 1, :], hu[0:KLAST, 0, HC - 1, :], hu[0:KLAST, 1, HC - 1, :],
                                                ALU.mult).then_inc(hid_ready, 1)

                    if not mlp:
                        dve.wait_ge(weights, layer * 16 + 32)
                        nc.vector.memset(xm[:, :, :, HS + P - 1:HS + P], 0.0)
                        nc.vector.tensor_tensor(tab[:, :, :], tab[:, :, :], across(qs, NT), ALU.mult).then_inc(tables, 1)
                        dve.wait_ge(tables, layer + 1)
                    if att:
                        lengths(0)
                    if mlp:
                        mine.done(nc.vector.tensor_copy(xm[:, :, :, HS - 1:HS], xm[:, :, :, HS + P - 1:HS + P]))
                        dve.wait_ge(xm_p, t)
                        for k in range(KB):
                            ins = nc.vector.tensor_tensor(xm[:, k, :, HS:], x_p[:, k, :, :],
                                                          x1T[:, k, :, ds(w * P - P + PAD, P)], ALU.add)
                        ins.then_inc(xm_ready, 1)
                    if att:
                        unit(0)
                    if mlp:
                        dve.wait_ge(h_p, t)
                        for b in range(NB):
                            ins = nc.vector.bn_stats(st6[:, b, :], hn_p[:, b, :])
                        mine.done(ins)
                        dve.nop(nofuse=True)
                        for b in range(NB):
                            ins = nc.vector.bn_aggr(mv[:, b, :], st6[:, b, :])
                        mine.done(ins)
                        nc.vector.tensor_scalar(vpe[:, :], mv[:, :, 1], LN_EPS, None, ALU.add).then_inc(var_ready, 1)
                    if att:
                        rotate(0)
                    if mlp:
                        dve.wait_ge(rstd_ready, t)
                        for b in range(NB):
                            ins = nc.vector.tensor_scalar(hn[:, b, :], hn_p[:, b, :], mv[:, b, 0:1], rstd[:, b:b + 1],
                                                          ALU.subtract, ALU.mult)
                        ins.then_inc(hn_ready, 1)
                        mine.close()
                    if att:
                        lengths(1)
                        unit(1)
                        peak(0, 0)
                        peak(0, 1)
                        rotate(1)
                    for u in range(HP):
                        if mlp and u == 0:
                            hidden(0)
                            hidden(1)
                        if att:
                            norm(0, u)
                            if u + 2 < HP:
                                peak(0, u + 2)
                        if mlp:
                            hidden(u + 2)
                    if att:
                        peak(1, 0)
                        peak(1, 1)
                    if mlp:
                        gated()
                    if att:
                        for u in range(HP):
                            norm(1, u)
                            if u + 2 < HP:
                                peak(1, u + 2)
                        own.close()
                    if mlp:
                        dve.wait_ge(xm_ready, t)
                        dve.wait_ge(y_p, t)
                        for k in range(KB):
                            ins = nc.vector.scalar_tensor_tensor(x1T[:, k, :, ds(w * P - P + PAD, P)], y_b[:, k, :, :],
                                                                 b2[:, k:k + 1], xm[:, k, :, HS:], ALU.add, ALU.add)
                        ins.then_inc(x_stored, 1)

                layers(dve, turn)

            @block.tensor
            def _(pe):
                mm = nc.tensor.matmul

                def turn(layer, t, w, att, mlp):
                    def project(b):
                        for i in range(3):
                            for k in range(KB):
                                ins = mm(pQKV[i][:, :], hs[:, k, b, HS - k:HS - k + P], wqkv[:, k, i * INNER:(i + 1) * INNER],
                                         start=(k == 0), stop=(k == KB - 1))
                        ins.then_inc(qkv_p, 1)

                    def turn_qk(b):
                        pe.wait_ge(qr_ready, t * NB + b + 1)
                        for qk in range(2):
                            for hp in range(HP):
                                ins = nc.tensor.transpose(pAB[qk][:, hp, :],
                                                          r1[:, qk, 2 * hp:2 * hp + 2, :].rearrange("p h d -> p (h d)"),
                                                          ident[:, :])
                        ins.then_inc(qkT_p, 1)

                    def scores(b, u):
                        if u >= 2:
                            pe.wait_ge(e_ready, (t * NB + b) * HP + u - 1)
                        hh = u % 2
                        for j in range(2):
                            hp = u // 2 * 2 + j
                            mm(pS[u % 2][:, j, :], qT[hh * DH:(hh + 1) * DH, hp, :],
                               kT[hh * DH:(hh + 1) * DH, hp, b, :], start=(j == 0), stop=True, skip_group_check=True)
                        mm(pS[u % 2][:, :, :].rearrange("p a n -> p (a n)"), identb[:, :], maskt[:, 1 if mlp else 0, :],
                           start=False, stop=True, skip_group_check=True).then_inc(s_p, 1)

                    def turn_p(b, u):
                        pe.wait_ge(pn_ready, (t * NB + b) * HP + u + 1)
                        for j in range(2):
                            for half in range(2):
                                ins = nc.tensor.transpose(pAB[u % 2][:, 2 * j + half, :],
                                                          Pm[:, u % 2, j, half * P:(half + 1) * P], ident[:, :])
                        ins.then_inc(pT_p, 1)

                    def mix(b, u):
                        pe.wait_ge(pT_ready, (t * NB + b) * HP + u + 1)
                        if b and u == 0:
                            pe.wait_ge(ot_ready, t * NB + 1)
                        hh = u % 2
                        for j in range(2):
                            hp = u // 2 * 2 + j
                            h = 2 * hp + hh
                            for half in range(2):
                                ins = mm(pO[hh * DH:(hh + 1) * DH, hp, :], V[:, b, half, h * DH:(h + 1) * DH],
                                         PT[:, u % 2, 2 * j + half, :], start=(half == 0), stop=(half == 1))
                        if u == HP - 1:
                            ins.then_inc(o_p, 1)

                    def up(c):
                        K = min(P, HID - c * P)
                        if c == 0 and att:
                            pe.wait_ge(qn_ready, (t + 1) * NB)
                            pe.wait_ge(v_ready, (t + 1) * NB)
                        if c >= 3:
                            pe.wait_ge(u_ready, (t - 1) * HC + c - 2)
                        for ag in range(2):
                            for k in range(KB):
                                ins = mm(pQKV[c % 3][0:K, ag * NB * P:(ag + 1) * NB * P], w1[:, k, ag, c * P:c * P + K],
                                         hnT[:, k, :, :], start=(k == 0), stop=(k == KB - 1))
                        ins.then_inc(u_p, 1)

                    def down(f):
                        if f == 0:
                            pe.wait_ge(hid_ready, t)
                        for c in range(HC):
                            K = min(P, HID - c * P)
                            ins = mm(y_b[:, f, :, :], w2[0:K, c, f * P:(f + 1) * P], hid[0:K, c, :],
                                     start=(c == 0), stop=(c == HC - 1))
                        if f == KB - 1:
                            ins.then_inc(y_p, 1)

                    if not mlp:
                        pe.wait_ge(weights, layer * 16 + 32)
                    if att:
                        pe.wait_ge(staged, (t + 1) * KB)
                        if mlp:
                            pe.wait_ge(x_stored, t)
                        project(0)
                    if mlp:
                        pe.wait_ge(ot_ready, t * NB)
                        for f in range(KB):
                            for hp in range(HP):
                                ins = mm(x_p[:, f, :, :], wo[:, hp, f * P:(f + 1) * P], OT[:, hp, :, :],
                                         start=(hp == 0), stop=(hp == HP - 1))
                        ins.then_inc(xm_p, 1)
                    if att:
                        pe.wait_ge(qn_ready, t * NB + 1)
                        pe.wait_ge(v_ready, t * NB + 1)
                        project(1)
                    if mlp:
                        pe.wait_ge(xm_ready, t)
                        for b in range(NB):
                            for k in range(KB):
                                ins = nc.tensor.transpose(hn_p[:, b, k * P:(k + 1) * P], xm[:, k, b, HS - k:HS - k + P], ident[:, :])
                        ins.then_inc(h_p, 1)
                        pe.wait_ge(hn_ready, t)
                        for b in range(NB):
                            for k in range(KB):
                                ins = nc.tensor.transpose(hT_b[:, k, b, :], hn[:, b, k * P:(k + 1) * P], ident[:, :])
                        ins.then_inc(hT_p, 1)
                        pe.wait_ge(hnT_ready, t)
                    if att:
                        turn_qk(0)
                        pe.wait_ge(qkT_ready, t * NB + 1)
                        scores(0, 0)
                        scores(0, 1)
                    for u in range(HP):
                        if mlp and u == 0:
                            up(0)
                            up(1)
                        if att:
                            turn_p(0, u)
                            if u + 2 < HP:
                                scores(0, u + 2)
                            mix(0, u)
                        if mlp:
                            up(u + 2)
                    if att:
                        turn_qk(1)
                        pe.wait_ge(qkT_ready, (t + 1) * NB)
                        scores(1, 0)
                        scores(1, 1)
                    for u in range(HP):
                        if mlp and u % 2 == 0:
                            down(u // 2)
                        if att:
                            turn_p(1, u)
                            if u + 2 < HP:
                                scores(1, u + 2)
                            mix(1, u)

                layers(pe, turn)


RH = 16
RD = D // RH
SCALE = 1.0 / np.sqrt(np.float32(RD))
DIAG = P + 2
TERMS_L = (0, 0, 0, 1, 1, 1, 2, 2)
TERMS_R = (0, 1, 2, 0, 1, 2, 0, 1)
E0 = T - P


def angle_tables():
    f = (1.0 / 10000.0 ** (np.arange(0, D, 2, dtype=np.float32) / D)).astype(np.float32).astype(np.float64)
    off = np.arange(-E0, T)
    e = np.stack([np.sin(off[None, :] * f[:, None]), np.cos(off[None, :] * f[:, None])], 1)
    i = np.arange(P)
    lo, up = (T - 1 - i)[None, :] * f[:, None], (-(T + 1) - i)[None, :] * f[:, None]
    rot = np.stack([np.stack([np.stack([np.cos(x)] * 2, 1), np.stack([np.sin(x)] * 2, 1)], 1) for x in (lo, up)], 1)
    return e.astype(np.float32), rot.astype(np.float32)


def diagonal_masks():
    i, d = np.arange(P)[:, None], np.arange(DIAG)[None, :]
    return np.stack([d <= i, d >= i + 2], 1).astype(np.float32)


def keep_x(nc, io, g, scratch, back):
    with nc.semaphore("x_kept_back" if back else "x_kept") as kept, nc.Block() as block:
        @block.sync
        def _(sp):
            for k in range(KB):
                here, there = g["xT"][:, k, :, PAD:], scratch["x"][:, k, :, :]
                sp.dma_start(*((here, there) if back else (there, here))).then_inc(kept, 16)
            sp.wait_ge(kept, 16 * KB)


def project_stage(nc, io, g, scratch, Vall):
    xT, ident = g["xT"], g["ident"]
    CH = 512
    NCH = T // CH
    with ExitStack() as ctx:
        m = Scope(nc, ctx, "pr_")
        wq, wk, wv = (m.sb(n, [P, KB, D]) for n in ("wq", "wk", "wv"))
        uv = m.sb("uv", [P, 2, KB])
        wr = m.sb("wr", [P, KB, D])
        full = m.sb("full", [P, 3, CH])
        parts = m.sb("parts", [P, 3, 3, CH], BF16)
        rest = m.sb("rest", [P, 3, CH])
        wrp = m.sb("wrp", [P, 3, KB, D], BF16)
        wrr = m.sb("wrr", [P, KB, D])
        xs = m.sb("xs", [P, KB, P])
        pq, pk = m.pb("pq", [P, CH]), m.pb("pk", [P, CH])
        pv = m.pb("pv", [P, D])
        loaded, wr_step, wr_out, qk_p, full_ready, dve_step, parts_ready, stored, staged, v_p, v_ready = map(m.sem, (
            "loaded", "wr_step", "wr_out", "qk_p", "full_ready", "dve_step", "parts_ready", "stored", "staged",
            "v_p", "v_ready"))
        LOADS = 16 * 5

        with nc.Block() as block:
            @block.sync
            def _(sp):
                for dst, src in ((wq, "rl_wq"), (wk, "rl_wk"), (wv, "rl_wv"), (wr, "rl_wr"), (uv, "rl_uv")):
                    sp.dma_start(dst[:, :, :], io[src]).then_inc(loaded, 16)
                sp.wait_ge(wr_step, 5)
                for p in range(3):
                    for k in range(KB):
                        for b in range(NB):
                            last = (p, k, b) == (2, KB - 1, NB - 1)
                            at = b * D + k * P
                            sp.dma_start(scratch["wr"][p, at:at + P, :],
                                         wrp[:, p, k, :]).then_inc(stored if last else wr_out, 16)
                sp.wait_ge(wr_out, 16 * (3 * KB * NB - 1))
                for mb in range(KB):
                    for b in range(NB):
                        with sp.Fori(0, NCH) as c:
                            turn = (mb * NB + b) * NCH + c
                            sp.wait_ge(parts_ready, turn + 2)
                            for a in range(3):
                                at = b * D + mb * P
                                to = scratch["quk"][a, :, at:at + P, ds(c * CH, CH)]
                                sp.dma_start(to.rearrange("p f t -> f p t"), parts[:, a, :, :]).then_inc(stored, 16)
                sp.wait_ge(stored, 16 * (3 * KB * NB * NCH + 1))

            @block.gpsimd
            def _(pool):
                nc.gpsimd.memset(xs[:, :, :], 0.0).then_inc(v_ready, 1)
                nc.gpsimd.memset(full[:, 0, :], 0.0).then_inc(full_ready, 1)
                nc.gpsimd.memset(full[:, 1, :], 0.0).then_inc(parts_ready, 1)
                for b in range(NB):
                    with pool.Fori(0, NT) as n:
                        pool.wait_ge(v_ready, n + b * NT + 1)
                        pool.nop(nofuse=True)
                        nc.gpsimd.tensor_copy(xs[:, :, :], xT[:, :, b, ds(n * P + PAD, P)]).then_inc(staged, 1)

            @block.scalar
            def _(act):
                act.wait_ge(loaded, LOADS)
                for mb in range(KB):
                    for b in range(NB):
                        with act.Fori(0, NCH) as c:
                            turn = (mb * NB + b) * NCH + c
                            act.wait_ge(qk_p, turn + 1)
                            act.wait_ge(parts_ready, turn + 1)
                            for a in range(2):
                                nc.scalar.activation(full[:, a, :], pq[:, :], ACT.Identity, bias=uv[:, a, mb:mb + 1])
                            nc.scalar.activation(full[:, 2, :], pk[:, :], ACT.Copy).then_inc(full_ready, 1)
                for b in range(NB):
                    with act.Fori(0, NT) as n:
                        act.wait_ge(v_p, n + b * NT + 1)
                        nc.scalar.activation(Vall[:, ds(n, 1), b * D:(b + 1) * D], pv[:, :].unsqueeze(1), ACT.Copy).then_inc(v_ready, 1)

            @block.vector
            def _(dve):
                def split(x, r, part, step):
                    for p in range(3):
                        src = x if p == 0 else r
                        ins = nc.vector.tensor_copy(part(p), src)
                        if p < 2:
                            step(ins)
                            step(nc.vector.tensor_tensor(r, src, part(p), ALU.subtract))
                    return ins

                dve.wait_ge(loaded, LOADS)
                own = Steps(dve, wr_step)
                split(wr[:, :, :], wrr[:, :, :], lambda p: wrp[:, p, :, :], own.done).then_inc(wr_step, 1)
                for mb in range(KB):
                    for b in range(NB):
                        with dve.Fori(0, NCH) as c:
                            turn = (mb * NB + b) * NCH + c
                            own = Steps(dve, dve_step, 4, turn)
                            dve.wait_ge(full_ready, turn + 2)
                            dve.wait_ge(stored, turn * 48 + 16)
                            split(full[:, :, :], rest[:, :, :], lambda p: parts[:, :, p, :], own.done).then_inc(parts_ready, 1)
                            own.close()

            @block.tensor
            def _(pe):
                mm = nc.tensor.matmul
                pe.wait_ge(loaded, LOADS)
                for mb in range(KB):
                    for b in range(NB):
                        with pe.Fori(0, NCH) as c:
                            turn = (mb * NB + b) * NCH + c
                            pe.wait_ge(full_ready, turn + 1)
                            for w, p in ((wq, pq), (wk, pk)):
                                for k in range(KB):
                                    ins = mm(p[:, :], w[:, k, mb * P:(mb + 1) * P], xT[:, k, b, ds(c * CH + PAD, CH)],
                                             start=(k == 0), stop=(k == KB - 1))
                            ins.then_inc(qk_p, 1)
                for b in range(NB):
                    with pe.Fori(0, NT) as n:
                        pe.wait_ge(staged, n + b * NT + 1)
                        for k in range(KB):
                            ins = mm(pv[:, :], xs[:, k, :], wv[:, k, :], start=(k == 0), stop=(k == KB - 1))
                        ins.then_inc(v_p, 1)


def relative_stage(nc, io, g, scratch, Vall, At):
    ident = g["ident"]
    NI = NT
    HEADS_ALL = NB * RH
    CH = 512
    NCH = T // CH
    RING = 4
    ROWS = 4
    ANGLES_AT = (6, 10, 14, 18)
    with ExitStack() as ctx:
        m = Scope(nc, ctx, "rl_")
        E = m.sb("E", [P, KB, E0 + T])
        rot = m.sb("rot", [P, 2, 2, KB, P])
        dmask = m.sb("dmask", [P, 2, DIAG])
        sel = m.sb("sel", [P, RD])
        qu, kk = (m.sb(n, [P, 2 * T], BF16) for n in ("qu", "kk"))
        qv = m.sb("qv", [P, T], BF16)
        wrp = m.sb("wrp", [P, KB, P], BF16)
        ab = m.sb("ab", [P, KB, T + 4])
        m1, m2 = (m.sb(n, [P, 2, KB, P]) for n in ("m1", "m2"))
        co = m.sb("co", [P, RING, 4, P])
        row = g["xT"][:, :, :, :].rearrange("p k b t -> p (k b t)")[:, 0:ROWS * T].rearrange("p (r t) -> p r t", t=T)
        t12 = m.sb("t12", [P, 2, DIAG])
        td = m.sb("td", [P, DIAG])
        nmx = m.sb("nmx", [P, NI])
        nms = m.sb("nms", [P, NI])
        sums = m.sb("sums", [P, NI])
        rsum = m.sb("rsum", [P, NI])
        PT = m.sb("PT", [P, 2, 4, P])
        vst = m.sb("vst", [P, NT, 32])
        O4 = m.sb("O4", [P, P])

        pS = [m.pb(f"pS{n}", [P, CH]) for n in range(2)]
        pD = m.pb("pD", [P, 2, 256])
        pT = [m.pb(f"pT{n}", [P, 4, P]) for n in range(2)]
        pO = m.pb("pO", [P, 512])
        pM = [m.pb(f"pM{n}", [P, CH]) for n in range(2)]

        (loaded, vst_ready, ab_p, ab_ready, co_ready, co_step, dg_p, diag_done, s_p, row_ready,
         mx_ready, e_ready, pT_p, pt_ready, o_p, o4_ready, r_p, an_ready, dve_step) = map(m.sem, (
             "loaded", "vst_ready", "ab_p", "ab_ready", "co_ready", "co_step", "dg_p",
             "diag_done", "s_p", "row_ready", "mx_ready", "e_ready", "pT_p", "pt_ready", "o_p", "o4_ready", "r_p",
             "an_ready", "dve_step"))
        packed = [m.sem(f"packed{a}") for a in range(3)]
        rsum_ready = m.sem("rsum_ready")

        with nc.Block() as block:
            @block.sync
            def _(sp):
                for dst, src in ((E[:, :, :], "rl_E"), (dmask[:, :, :], "rl_dmask"), (sel[:, :], "rl_sel"),
                                 (rot[:, :, :, :, :].rearrange("p u c k i -> p (u c k i)"), "rl_rot")):
                    sp.dma_start(dst, io[src]).then_inc(loaded, 16)
                sp.wait_ge(loaded, 16 * 4)

            @block.gpsimd
            def _(pool):
                for s, k in ((o_p, 1), (s_p, RING * NCH), (row_ready, 2), (pt_ready, 2), (pT_p, ROWS * NCH),
                             (diag_done, 1), (o4_ready, 1), (an_ready, 1), (co_ready, 1)):
                    pool.sem_inc(s, k)
                nc.gpsimd.memset(ab[:, :, T:], 0.0)
                nc.gpsimd.memset(vst[:, :, :], 0.0)

        LAST = HEADS_ALL - 1

        def count(n, s, more, per=1):
            return n * (NI * per) + (s * per + more)

        def row_of(s):
            return row[:, s % ROWS, :]

        def heads(eng, step):
            for s in range(3):
                step(0, s, True, False)
            with eng.Fori(0, LAST) as n:
                for s in range(3, NI + 3):
                    step(n, s, False, False)
            for s in range(3, NI + 3):
                step(LAST, s, False, True)

        with nc.Block() as block:
            @block.sync
            def _(sp):
                def gather(n, arrays):
                    for a, dst, terms in arrays:
                        for i, part in enumerate(terms):
                            at = dst if a == 1 else dst[:, ds(n % 2 * T, T)]
                            sp.dma_start(at[i * RD:(i + 1) * RD, :],
                                         scratch["quk"][a, part, ds(n * RD, RD), :]).then_inc(packed[a], 16)

                def gather_q(n):
                    gather(n, ((1, qv, TERMS_R),))
                    for i, part in enumerate(TERMS_L):
                        sp.dma_start(wrp[i * RD:(i + 1) * RD, :, :].rearrange("p k f -> p (k f)"),
                                     scratch["wr"][part, ds(n * RD, RD), :]).then_inc(packed[1], 16)

                def gather_k(n):
                    gather(n, ((0, qu, TERMS_L), (2, kk, TERMS_R)))

                gather_q(0)
                gather_k(0)
                with sp.Fori(0, LAST) as n:
                    sp.wait_ge(ab_p, (n + 1) * NCH)
                    gather_q(n + 1)
                    sp.wait_ge(s_p, count(n, 0, RING * NCH + 1, NCH))
                    gather_k(n + 1)

            @block.gpsimd
            def _(pool):
                def blocks(n, first, last):
                    for I in range(first, last):
                        pool.wait_ge(ab_ready, n * NCH + (min(NCH - 1, (I + 1) * P // CH) + 1))
                        pool.wait_ge(s_p, count(n, I, NCH, NCH))
                        pool.wait_ge(co_ready, count(n, I, 1))
                        pool.nop(nofuse=True)
                        for u in range(2):
                            x = ab[:, :, I * P + u:I * P + u + P]
                            nc.gpsimd.tensor_tensor(m1[:, u, :, :], x, rot[:, u, 0, :, :], ALU.mult)
                            ins = nc.gpsimd.tensor_tensor(m2[:, u, :, :], x, rot[:, u, 1, :, :], ALU.mult)
                        ins.then_inc(co_step, 1)
                        pool.wait_ge(co_step, count(n, I, 1))
                        to = co[:, I % RING, :, :].rearrange("p (u k) i -> p u k i", u=2)
                        nc.gpsimd.tensor_tensor(to[:, :, 0, :], m1[:, :, 0, :], m2[:, :, 1, :], ALU.subtract)
                        nc.gpsimd.tensor_tensor(to[:, :, 1, :], m1[:, :, 1, :], m2[:, :, 0, :], ALU.add).then_inc(co_ready, 1)

                with pool.Fori(0, HEADS_ALL) as n:
                    blocks(n, 0, 3)
                    pool.wait_ge(o_p, n * NI + 1)
                    pool.nop(nofuse=True)
                    nc.gpsimd.tensor_copy(vst[:, :, 0:RD], Vall[:, :, ds(n * RD, RD)]).then_inc(vst_ready, 1)
                    blocks(n, 3, NI)

            @block.scalar
            def _(act):
                def angles(n, c):
                    act.wait_ge(ab_p, n * NCH + (c + 1))
                    for k in range(KB):
                        ins = nc.scalar.activation(ab[:, k, c * CH:(c + 1) * CH], pM[k][:, :], ACT.Copy)
                    ins.then_inc(ab_ready, 1)

                def attention_out(n, J):
                    act.wait_ge(o_p, count(n, J, 2))
                    nc.scalar.activation(O4[:, :], pO[:, 0:P], ACT.Copy).then_inc(o4_ready, 1)

                def evac(n, J, c):
                    act.wait_ge(pT_p, count(n, J, c + 1 + NCH * ROWS, NCH))
                    nc.scalar.activation(PT[:, c % 2, :, :], pT[c % 2][:, :, :], ACT.Copy).then_inc(pt_ready, 1)

                def softmax(n, I):
                    act.wait_ge(mx_ready, count(n, I, 1))
                    r = row_of(I)
                    nc.scalar.activation(r, r, ACT.Exp, bias=nms[:, I % NI:I % NI + 1], scale=float(SCALE),
                                         accum_out=sums[:, I % NI:I % NI + 1]).then_inc(e_ready, 1)

                for c in range(NCH):
                    angles(0, c)

                def step(n, s, first, last):
                    if s >= 3:
                        attention_out(n, s - 3)
                        if not last and s in ANGLES_AT:
                            c = ANGLES_AT.index(s)
                            act.wait_ge(co_ready, count(n, min(NI, (c + 1) * CH // P), 1))
                            angles(n + 1, c)
                    for c in range(NCH):
                        if 0 <= s - 2 and (s - 2 < NI or not last):
                            evac(n, s - 2, c)
                        if c == 1 and 0 <= s - 1 and (s - 1 < NI or not last):
                            softmax(n, s - 1)

                heads(act, step)

            @block.vector
            def _(dve):
                def scores(n, s):
                    I = s % NI
                    dve.wait_ge(dg_p, count(n, s, 1))
                    for u in range(2):
                        ins = nc.vector.tensor_tensor(t12[:, u, :], pD[:, u, 0:DIAG], dmask[:, u, :], ALU.mult)
                    ins.then_inc(dve_step, 1)
                    dve.wait_ge(dve_step, count(n, s, 1, 3))
                    nc.vector.tensor_tensor(td[:, :], t12[:, 0, :], t12[:, 1, :], ALU.add).then_inc(diag_done, 1)
                    dve.wait_ge(diag_done, count(n, s, 2))
                    dve.wait_ge(pT_p, count(n, s, NCH, NCH))
                    for c in range(NCH):
                        dve.wait_ge(s_p, count(n, s, c + 1 + RING * NCH, NCH))
                        nc.vector.tensor_copy(row_of(s)[:, c * CH:(c + 1) * CH], pS[c % 2][:, :]).then_inc(row_ready, 1)
                    dve.wait_ge(row_ready, count(n, s, NCH + 2, NCH))
                    W = min(DIAG, T - I * P)
                    at = row_of(s)[:, I * P:I * P + W]
                    nc.vector.tensor_tensor(at, at, td[:, 0:W], ALU.add).then_inc(dve_step, 1)
                    dve.wait_ge(dve_step, count(n, s, 2, 3))
                    nc.vector.tensor_reduce(nmx[:, I:I + 1], row_of(s), AX_X, ALU.max, negate=True).then_inc(dve_step, 1)
                    dve.wait_ge(dve_step, count(n, s, 3, 3))
                    nc.vector.tensor_scalar(nms[:, I:I + 1], nmx[:, I:I + 1], float(SCALE), None,
                                            ALU.mult).then_inc(mx_ready, 1)

                def attention_out(n, J):
                    dve.wait_ge(e_ready, count(n, J, 1))
                    nc.vector.reciprocal(rsum[:, J:J + 1], sums[:, J:J + 1]).then_inc(rsum_ready, 1)
                    dve.wait_ge(rsum_ready, count(n, J, 1))
                    dve.wait_ge(r_p, count(n, J, 1))
                    nc.vector.tensor_scalar(At[:, J, ds(n * RD, RD)], pM[0][:, 0:RD], rsum[:, J:J + 1], None,
                                            ALU.mult).then_inc(an_ready, 1)

                def step(n, s, first, last):
                    if s < NI or not last:
                        scores(n, s)
                    if s >= 3:
                        attention_out(n, s - 3)

                heads(dve, step)

            @block.tensor
            def _(pe):
                mm = nc.tensor.matmul

                def angles(n, c):
                    if c == 0:
                        pe.wait_ge(packed[1], (n + 1) * 16 * 2 * len(TERMS_L))
                    for k in range(KB):
                        ins = mm(pM[k][:, :], wrp[:, k, :], qv[:, c * CH:(c + 1) * CH], start=True, stop=True)
                    ins.then_inc(ab_p, 1)

                def diagonal(n, s):
                    pe.wait_ge(co_ready, count(n, s, 2))
                    pe.wait_ge(diag_done, count(n, s, 1))
                    for u in range(2):
                        for k in range(KB):
                            ins = mm(pD[:, u, 0:DIAG], co[:, s % RING, 2 * u + k, :], E[:, k, E0:E0 + DIAG],
                                     start=(k == 0), stop=(k == KB - 1))
                    ins.then_inc(dg_p, 1)

                def scores(n, s, c):
                    p, I, head = pS[c % 2], s % NI, n + s // NI
                    pe.wait_ge(row_ready, count(n, s, c + 1, NCH))
                    lo_end = min((c + 1) * CH, I * P)
                    up_at = max(c * CH, I * P + DIAG)
                    spans = []
                    if lo_end > c * CH:
                        spans.append((0, c * CH, lo_end))
                    if up_at < (c + 1) * CH:
                        spans.append((1, up_at, (c + 1) * CH))
                    ins = mm(p[:, :], qu[:, ds(head % 2 * T + I * P, P)], kk[:, ds(head % 2 * T + c * CH, CH)],
                             start=True, stop=True, skip_group_check=True)
                    for u, j0, j1 in spans:
                        for k in range(KB):
                            e0 = j0 - I * P + E0
                            ins = mm(p[:, j0 - c * CH:j1 - c * CH], co[:, I % RING, 2 * u + k, :], E[:, k, e0:e0 + j1 - j0],
                                     start=False, stop=True, skip_group_check=True)
                    ins.then_inc(s_p, 1)

                def turn(n, s, c):
                    if c == 0:
                        pe.wait_ge(e_ready, count(n, s, 1))
                    for j in range(4):
                        at = (4 * c + j) * P
                        ins = nc.tensor.transpose(pT[c % 2][:, j, :], row_of(s)[:, at:at + P], ident[:, :])
                    ins.then_inc(pT_p, 1)

                def mix(n, s, c):
                    pe.wait_ge(pt_ready, count(n, s, c + 3, NCH))
                    if c == 0:
                        pe.wait_ge(o4_ready, count(n, s, 1))
                        if s in (0, NI):
                            pe.wait_ge(vst_ready, n + (s // NI + 1))
                    for j in range(4):
                        ins = mm(pO[32 * j:32 * j + 32, 0:P], vst[:, 4 * c + j, :], PT[:, c % 2, j, :],
                                 start=(c == 0), stop=(c == NCH - 1))
                    if c == NCH - 1:
                        ins.then_inc(o_p, 1)

                def add_groups(n, J):
                    pe.wait_ge(o4_ready, count(n, J, 2))
                    pe.wait_ge(an_ready, count(n, J, 1))
                    mm(pM[0][:, 0:RD], O4[:, :], sel[:, :], start=True, stop=True).then_inc(r_p, 1)

                for c in range(NCH):
                    if c:
                        pe.wait_ge(ab_ready, c)
                    angles(0, c)

                def step(n, s, first, last):
                    if s >= 3 and not last and s in ANGLES_AT:
                        pe.wait_ge(an_ready, count(n, s - 3, 1))
                        if ANGLES_AT.index(s):
                            pe.wait_ge(ab_ready, (n + 1) * NCH + ANGLES_AT.index(s))
                        angles(n + 1, ANGLES_AT.index(s))
                    more = s < NI or not last
                    if more:
                        if s in (0, NI):
                            pe.wait_ge(packed[0], (n + s // NI + 1) * 16 * len(TERMS_L))
                            pe.wait_ge(packed[2], (n + s // NI + 1) * 16 * len(TERMS_L))
                        diagonal(n, s)
                    if s >= 3:
                        mix(n, s - 3, NCH - 1)
                    used = 0 <= s - 2 and (s - 2 < NI or not last)
                    for c in range(NCH):
                        if more:
                            scores(n, s, c)
                        if used:
                            turn(n, s - 2, c)
                            if c:
                                mix(n, s - 2, c - 1)
                        if c == 1 and s >= 3:
                            if s in ANGLES_AT and not last:
                                pe.wait_ge(ab_ready, (n + 1) * NCH + ANGLES_AT.index(s) + 1)
                            add_groups(n, s - 3)

                heads(pe, step)


TOKENS = 1024
ME = 8
FF = 1024
TOPK = 2


def moe_stage(nc, io, g, Acc):
    xT = g["xT"]
    NTT, FC, HALF = TOKENS // P, FF // P, 512
    with ExitStack() as ctx:
        m = Scope(nc, ctx, "me_")
        w1 = [m.sb(f"w1_{j}", [P, KB, FF]) for j in range(2)]
        w2 = [m.sb(f"w2_{j}", [P, FC, D]) for j in range(2)]
        hT = m.sb("hT", [P, FC, TOKENS])
        bias = m.sb("bias", [P, D])
        idx = m.sb("idx", [P, NTT, TOPK], I32)
        idxf = m.sb("idxf", [P, NTT, TOPK])
        ew = m.sb("ew", [P, NTT, TOPK])
        erow = m.sb("erow", [P, ME])
        hit = m.sb("hit", [P, TOPK, NTT, ME])
        cw = m.sb("cw", [P, NTT, ME])
        pH = [m.pb(f"pH{i}", [P, HALF]) for i in range(4)]
        pY = [m.pb(f"pY{i}", [P, 2, D]) for i in range(2)]
        w_in = [m.sem(f"w_in{j}") for j in range(2)]
        loaded, h_p, h_ready, y_p, acc_ready, dve_step = map(m.sem, (
            "loaded", "h_p", "h_ready", "y_p", "acc_ready", "dve_step"))

        with nc.Block() as block:
            @block.sync
            def _(sp):
                for dst, src in ((bias[:, :], "me_bias"), (idx[:, :, :], "me_idx"), (ew[:, :, :], "me_w"),
                                 (erow[:, :], "me_erow")):
                    sp.dma_start(dst, io[src]).then_inc(loaded, 16)
                sp.wait_ge(loaded, 64)

            @block.gpsimd
            def _(pool):
                for s, k in ((y_p, 2 * NTT // 2), (acc_ready, 2), (h_ready, 4)):
                    pool.sem_inc(s, k)

            @block.vector
            def _(dve):
                own = Steps(dve, dve_step)
                dve.wait_ge(loaded, 64)
                nc.vector.tensor_copy(Acc[:, :, :].rearrange("p n (b d) -> p (n b) d", b=NB), across(bias[:, :], NB * NT))
                own.done(nc.vector.tensor_copy(idxf[:, :, :], idx[:, :, :]))
                for k in range(TOPK):
                    ins = nc.vector.tensor_tensor(hit[:, k, :, :], idxf[:, :, k:k + 1].to_broadcast([P, NTT, ME]),
                                                  across(erow[:, :], NTT), ALU.is_equal)
                own.done(ins)
                for k in range(TOPK):
                    ins = nc.vector.tensor_tensor(hit[:, k, :, :], hit[:, k, :, :],
                                                  ew[:, :, k:k + 1].to_broadcast([P, NTT, ME]), ALU.mult)
                own.done(ins)
                nc.vector.tensor_tensor(cw[:, :, :], hit[:, 0, :, :], hit[:, 1, :, :], ALU.add)

        def experts(eng, expert):
            with eng.Fori(0, ME // 2) as pair:
                for j in range(2):
                    expert(pair, pair * 2 + j, j)

        with nc.Block() as block:
            @block.sync
            def _(sp):
                def expert(pair, e, j):
                    sp.wait_ge(y_p, (e + 1) * (NTT // 2))
                    sp.dma_start(w1[j][:, :, :], io["me_w1"][ds(e, 1), :, :, :].rearrange("e p k f -> (e p) k f")).then_inc(w_in[j], 16)
                    sp.dma_start(w2[j][:, :, :], io["me_w2"][ds(e, 1), :, :, :].rearrange("e p k f -> (e p) k f")).then_inc(w_in[j], 16)

                experts(sp, expert)

            @block.scalar
            def _(act):
                def expert(pair, e, j):
                    for f in range(FC):
                        for half in range(2):
                            i = (2 * f + half) % 4
                            act.wait_ge(h_p, e * 2 * FC + 2 * f + half + 1)
                            nc.scalar.activation(hT[:, f, half * HALF:(half + 1) * HALF], pH[i][:, :],
                                                 ACT.Gelu).then_inc(h_ready, 1)

                experts(act, expert)

            @block.vector
            def _(dve):
                def expert(pair, e, j):
                    for t in range(NTT):
                        if t % 2 == 0:
                            dve.wait_ge(y_p, e * (NTT // 2) + t // 2 + 1 + NTT)
                            dve.wait_ge(acc_ready, e * (NTT // 2) + t // 2 + 1)
                        ins = nc.vector.scalar_tensor_tensor(Acc[:, t, 0:D], pY[t // 2 % 2][:, t % 2, :],
                                                             cw[:, t, ds(e, 1)], Acc[:, t, 0:D], ALU.mult, ALU.add)
                        if t % 2:
                            ins.then_inc(acc_ready, 1)

                experts(dve, expert)

            @block.tensor
            def _(pe):
                mm = nc.tensor.matmul

                def expert(pair, e, j):
                    pe.wait_ge(w_in[j], (pair + 1) * 32)
                    for f in range(FC):
                        for half in range(2):
                            i = (2 * f + half) % 4
                            pe.wait_ge(h_ready, e * 2 * FC + 2 * f + half + 1)
                            for k in range(KB):
                                at = PAD + half * HALF
                                ins = mm(pH[i][:, :], w1[j][:, k, f * P:(f + 1) * P], xT[:, k, 0, at:at + HALF],
                                         start=(k == 0), stop=(k == KB - 1))
                            ins.then_inc(h_p, 1)
                    pe.wait_ge(h_ready, (e + 1) * 2 * FC + 4)
                    for t in range(NTT):
                        if t % 2 == 0:
                            pe.wait_ge(acc_ready, e * (NTT // 2) + t // 2 + 1)
                        for f in range(FC):
                            ins = mm(pY[t // 2 % 2][:, t % 2, :], hT[:, f, t * P:(t + 1) * P], w2[j][:, f, :],
                                     start=(f == 0), stop=(f == FC - 1))
                        if t % 2:
                            ins.then_inc(y_p, 1)

                experts(pe, expert)


def norm_stage(nc, io, g, name, rows=None, out=None):
    xT, x1T, ident, mhalf = g["xT"], g["x1T"], g["ident"], g["mhalf"]
    with ExitStack() as ctx:
        m = Scope(nc, ctx, name)

        def two(make, what, shape):
            return [make(f"{what}{i}", shape) for i in range(2)]

        xs = two(m.sb, "xs", [P, KB, NB, P])
        y = two(m.sb, "y", [P, NB, D])
        mv = two(m.sb, "mv", [P, NB, 2])
        vpe = two(m.sb, "vpe", [P, NB])
        rstd = two(m.sb, "rstd", [P, NB])
        yn = two(m.sb, "yn", [P, NB, D])
        st6 = m.sb("st6", [P, NB, 6])
        pT = two(m.pb, "pT", [P, NB, D])
        pB = two(m.pb, "pB", [P, KB, NB, P])
        if rows is None:
            y = pT
        staged, t_p, var_ready, rstd_ready, yn_ready, dve_step = map(m.sem, (
            "staged", "t_p", "var_ready", "rstd_ready", "yn_ready", "dve_step"))
        if out is None:
            b_p = m.sem("b_p")
            x_stored = [m.sem("x_stored")] * 2
        else:
            x_stored = [m.sem(f"x_stored{i}") for i in range(2)]
        t_read = yn_ready if rows is None else m.sem("sum_ready")
        with nc.Block() as block:
            if out is None:
                @block.scalar
                def _(act):
                    def turn(n, s, head=True, tail=True):
                        k, r = n - 1, 1 - s
                        if tail:
                            act.wait_ge(b_p, k + 1)
                            for b in range(NB):
                                nc.scalar.activation(xT[:, :, b, ds(k * P + PAD, P)], pB[r][:, :, b, :],
                                                     ACT.Copy).then_inc(x_stored[r], 16 // NB)

                    turns(act, turn)
            else:
                @block.sync
                def _(sp):
                    def turn(n, s, head=True, tail=True):
                        k, r = n - 1, 1 - s
                        if tail:
                            sp.wait_ge(yn_ready, k + 2)
                            sp.dma_start(out[:, ds(k * P, P), :].rearrange("b p d -> p b d"),
                                         yn[r][:, :, :]).then_inc(x_stored[r], 16)

                    turns(sp, turn)
                    for r in range(2):
                        sp.wait_ge(x_stored[r], 16 * (NT // 2 + 1))

            @block.gpsimd
            def _(pool):
                for sem, k in ((t_p, 1), (yn_ready, 1), (x_stored[0], 16), (x_stored[1], 16)):
                    pool.sem_inc(sem, k)
                if rows is not None:
                    pool.sem_inc(t_read, 1)

                def turn(n, s, head=True, tail=True):
                    k, r = n - 1, 1 - s
                    if head:
                        if type(n) is not int or n > 0:
                            pool.wait_ge(t_p, n)
                        pool.nop(nofuse=True)
                        for b in range(NB):
                            at = ds(n * P + PAD, P)
                            if rows is None:
                                ins = nc.gpsimd.tensor_tensor(xs[s][:, :, b, :], xT[:, :, b, at], x1T[:, :, b, at], ALU.add)
                            else:
                                ins = nc.gpsimd.tensor_copy(xs[s][:, :, b, :], xT[:, :, b, at])
                        ins.then_inc(staged, 1)
                    if tail:
                        pool.wait_ge(var_ready, k + 1)
                        nc.gpsimd.tensor_tensor(rstd[r][:, :], vpe[r][:, :], mhalf[:, 0:NB], ALU.pow).then_inc(rstd_ready, 1)

                turns(pool, turn)

            @block.vector
            def _(dve):
                def turn(n, s, head=True, tail=True):
                    k, r = n - 1, 1 - s
                    own = Steps(dve, dve_step, 2, n)
                    if head:
                        dve.wait_ge(t_p, n + 2)
                        if rows is not None:
                            if type(n) is not int or n > 0:
                                dve.wait_ge(yn_ready, n)
                            for b in range(NB):
                                ins = nc.vector.tensor_tensor(y[s][:, b, :].unsqueeze(1), pT[s][:, b, :].unsqueeze(1),
                                                              rows[:, ds(n, 1), b * D:(b + 1) * D], ALU.add)
                            ins.then_inc(t_read, 1)
                            dve.wait_ge(t_read, n + 2)
                        for b in range(NB):
                            ins = nc.vector.bn_stats(st6[:, b, :], y[s][:, b, :])
                        own.done(ins)
                        dve.nop(nofuse=True)
                        for b in range(NB):
                            ins = nc.vector.bn_aggr(mv[s][:, b, :], st6[:, b, :])
                        own.done(ins)
                        nc.vector.tensor_scalar(vpe[s][:, :], mv[s][:, :, 1], LN_EPS, None, ALU.add).then_inc(var_ready, 1)
                        own.close()
                    if tail:
                        dve.wait_ge(rstd_ready, k + 1)
                        dve.wait_ge(x_stored[r], 16 * (k if out is None else k // 2) + 16)
                        for b in range(NB):
                            ins = nc.vector.tensor_scalar(yn[r][:, b, :], y[r][:, b, :], mv[r][:, b, 0:1],
                                                          rstd[r][:, b:b + 1], ALU.subtract, ALU.mult)
                        ins.then_inc(yn_ready, 1)

                turns(dve, turn)

            @block.tensor
            def _(pe):
                def turn(n, s, head=True, tail=True):
                    k, r = n - 1, 1 - s
                    if head:
                        pe.wait_ge(staged, n + 1)
                        if type(n) is not int or n > 0:
                            pe.wait_ge(t_read, n)
                        for b in range(NB):
                            for j in range(KB):
                                ins = nc.tensor.transpose(pT[s][:, b, j * P:(j + 1) * P], xs[s][:, j, b, :], ident[:, :])
                        ins.then_inc(t_p, 1)
                    if tail and out is None:
                        pe.wait_ge(yn_ready, k + 2)
                        for b in range(NB):
                            for j in range(KB):
                                ins = nc.tensor.transpose(pB[r][:, j, b, :], yn[r][:, b, j * P:(j + 1) * P], ident[:, :])
                        ins.then_inc(b_p, 1)

                turns(pe, turn)


def program(nc, io):
    with ExitStack() as ctx:
        m = Scope(nc, ctx, "g_")
        g = dict(x1T=m.sb("x1T", [P, KB, NB, PAD + T]), xT=m.sb("xT", [P, KB, NB, PAD + T]),
                 ident=m.sb("ident", [P, P]), ones=m.sb("ones", [P, P]), mhalf=m.sb("mhalf", [P, 16]))
        delta_rule_stage(nc, io, g)
        local_stage(nc, io, g)
        norm_stage(nc, io, g, "an_")
        rows = g["x1T"][:, :, :, :].rearrange("p k b t -> p (k b t)")[:, 0:NB * NT * D]
        rows = rows.rearrange("p (n d) -> p n d", d=NB * D)
        scratch = {"x": nc.dram_tensor("x_kept", (P, KB, NB, T), F32).ap(),
                   "quk": nc.dram_tensor("quk_parts", (3, 3, NB * D, T), BF16).ap(),
                   "wr": nc.dram_tensor("wr_parts", (3, NB * D, D), BF16).ap()}
        with nc.sbuf_tensor("v_rows", [P, NT, NB * D], F32) as Vall:
            project_stage(nc, io, g, scratch, Vall)
            keep_x(nc, io, g, scratch, False)
            relative_stage(nc, io, g, scratch, Vall, rows)
            keep_x(nc, io, g, scratch, True)
        norm_stage(nc, io, g, "rn_", rows)
        moe_stage(nc, io, g, rows)
        norm_stage(nc, io, g, "fi_", rows, io["out"])


def kernel(**inputs):
    import numpy as _np
    import concourse.bacc as _bacc
    from concourse import mybir as _mybir
    from concourse.bass_utils import run_bass_kernel_spmd as _run

    nc = _bacc.Bacc("TRN2", target_bir_lowering=False, num_devices=1)
    i = {k: _np.asarray(v) for k, v in inputs.items()}

    def by_block(w):
        return w.reshape(w.shape[0] // P, P, -1).transpose(1, 0, 2)

    laid = {
        "xT": i["L0_attn_x"].reshape(NB, T, KB, P).transpose(3, 2, 0, 1),
        "ident": _np.eye(P, dtype=_np.float32),
        "masks": delta_rule_masks(),
        "dr_wkv": by_block(_np.concatenate([i["L0_attn_" + n].T for n in ("Wk", "Wv", "Wa", "Wb")], 1)),
        "dr_wqg": _np.stack([by_block(i["L0_attn_" + n].T) for n in ("Wq", "Wg")], 2),
        "dr_wo": i["L0_attn_Wo"].T,
        "dr_bkv": _np.concatenate([i["L0_attn_" + n] for n in ("bk", "bv", "ba", "bb")])[None],
        "dr_bqg": _np.stack([i["L0_attn_bq"], i["L0_attn_bg"]], 1),
        "dr_bo": i["L0_attn_bo"][None],
    }

    def half(s):
        return _np.roll(s, DH // 2, -1)

    laid["lo_mask"] = window_masks()
    b1 = i["L0_ffn_b1"].reshape(DEPTH, 2, HID)
    b1 = _np.concatenate([b1, _np.zeros((DEPTH, 2, HC * P - HID), b1.dtype)], 2).reshape(DEPTH, 2, HC, P)
    w2 = i["L0_ffn_w2"]
    w2 = _np.concatenate([w2, _np.zeros((DEPTH, HC * P - HID, D), w2.dtype)], 1)
    laid["lo_wts"] = _np.stack([_np.concatenate([a.reshape(P, -1) for a in (
        by_block(i["L0_ffn_wqkv"][l]), by_block(i["L0_ffn_wo"][l]), by_block(i["L0_ffn_w1"][l]), by_block(w2[l]),
        b1[l].transpose(2, 0, 1), i["L0_ffn_b2"][l].reshape(KB, P).T, i["L0_ffn_ln_g"][l].reshape(KB, P).T,
        i["L0_ffn_ln_b"][l].reshape(KB, P).T,
        _np.broadcast_to(_np.concatenate([i["L0_ffn_q_scale"][l], i["L0_ffn_k_scale"][l],
                                          half(i["L0_ffn_q_scale"][l]), half(i["L0_ffn_k_scale"][l])]), (P, 4 * DH)),
        rotary_tables())], 1) for l in range(DEPTH)])
    E, rot = angle_tables()
    for n, w in (("rl_wq", "Wq"), ("rl_wk", "Wk"), ("rl_wv", "Wv")):
        laid[n] = by_block(i["L1_attn_" + w].T)
    laid["rl_wr"] = by_block(i["L1_attn_Wr"].reshape(D, P, 2).transpose(0, 2, 1).reshape(D, D))
    laid["rl_uv"] = _np.stack([i["L1_attn_" + n].reshape(KB, P).T for n in ("u_bias", "v_bias")], 1)
    laid["rl_E"], laid["rl_rot"] = E, rot.reshape(P, -1)
    laid["rl_dmask"] = diagonal_masks()
    laid["rl_sel"] = (_np.arange(P)[:, None] % 32 == _np.arange(RD)[None, :]).astype(_np.float32)
    laid["me_bias"] = _np.broadcast_to(i["L1_ffn_bias"], (P, D))
    laid["me_idx"] = i["L1_ffn_expert_indices"].reshape(TOKENS // P, P, TOPK).transpose(1, 0, 2)
    laid["me_w"] = i["L1_ffn_expert_weights"].reshape(TOKENS // P, P, TOPK).transpose(1, 0, 2)
    laid["me_erow"] = _np.broadcast_to(_np.arange(ME, dtype=_np.float32), (P, ME))
    laid["me_w1"] = i["L1_ffn_w1"].reshape(ME, KB, P, FF).transpose(0, 2, 1, 3)
    laid["me_w2"] = i["L1_ffn_w2"].reshape(ME, FF // P, P, D).transpose(0, 2, 1, 3)
    arrays, io = {}, {}
    for name, a in laid.items():
        a = _np.ascontiguousarray(a)
        arrays["in_" + name] = a
        io[name] = nc.dram_tensor("in_" + name, a.shape, _mybir.dt.from_np(a.dtype), kind="ExternalInput").ap()
    io["out"] = nc.dram_tensor("out_x", (NB, T, D), F32, kind="ExternalOutput").ap()
    program(nc, io)
    r = _run(nc, [arrays], core_ids=[0])
    return r.results[0]["out_x"]
```
